# Optimizing a Trainium2 kernel written in Bass

```python
import numpy as np
import jax
import jax.numpy as jnp

def _softmax(x, axis=-1):
    return jax.nn.softmax(x, axis=axis)

def _gelu(x):
    return jax.nn.gelu(x, approximate=True)

def _silu(x):
    return jax.nn.silu(x)

def _sigmoid(x):
    return jax.nn.sigmoid(x)

def _layernorm(x, axis=-1, eps=1e-05):
    m = jnp.mean(x, axis=axis, keepdims=True)
    v = jnp.var(x, axis=axis, keepdims=True)
    return (x - m) / jnp.sqrt(v + eps)

def _scatter_add(tgt, idx, src, axis=0):
    return tgt.at[idx].add(src)

def _segment_sum(src, seg, n):
    return jax.ops.segment_sum(src, seg, n)
kernel_name = 'mk_xattn_ffn_d2_seqx_r8_88d656'

def setup_inputs(seed: int=0):
    np.random.seed(seed)
    _w = jnp.asarray

    def _rec_inputs():
        import jax
        import jax.numpy as jnp
        _rk = jax.random.key(seed)
        x = 7.22e-05 + 1 * jax.random.normal(jax.random.fold_in(_rk, 1), (8, 128, 128), jnp.float32)
        _lenS = 128 - jax.random.randint(jax.random.fold_in(_rk, 7), (8,), 0, max(1, 128 // 4) + 1, jnp.int32)
        _lenS2 = 128 - jax.random.randint(jax.random.fold_in(_rk, 8), (8,), 0, max(1, 128 // 4) + 1, jnp.int32)
        _ctx_1024P = jax.random.normal(jax.random.fold_in(_rk, 11), (8, 16, 128), jnp.float32)
        _ctx_1024c = jax.random.dirichlet(jax.random.fold_in(_rk, 511), 0.3 * jnp.ones((16,), jnp.float32), (8, 128))
        _ctx_1024t = jnp.einsum('bsk,bkd->bsd', _ctx_1024c, _ctx_1024P)
        _ctx_1024t = _ctx_1024t * jax.lax.rsqrt(jnp.mean(jnp.square(_ctx_1024t)) + 1e-12) * 0.953939
        ctx_1024 = 0.00171412 + 0.999381 * (_ctx_1024t + 0.3 * jax.random.normal(jax.random.fold_in(_rk, 611), (8, 128, 128), jnp.float32))
        return (x, ctx_1024)
    x, ctx_1024 = _rec_inputs()

    def _L0_xattn_setup():
        import jax, jax.numpy as jnp
        import numpy as np
        B, N, P, DIM, H = (8, 128, 77, 128, 16)
        HD = DIM // H
        LN_EPS = 1e-05
        key = jax.random.key(seed)
        ks = jax.random.split(key, 8)
        s = 0.02
        return {'x': jax.random.normal(ks[0], (B, N, DIM), jnp.float32), 'x_text': jax.random.normal(ks[1], (B, P, DIM), jnp.float32), 'Wq': jax.random.normal(ks[2], (DIM, DIM), jnp.float32) * s, 'Wk': jax.random.normal(ks[3], (DIM, DIM), jnp.float32) * s, 'Wv': jax.random.normal(ks[4], (DIM, DIM), jnp.float32) * s, 'gate': jax.random.normal(ks[5], (1, H, 1, 1), jnp.float32) * 0.5, 'ln_g': jnp.ones((DIM,), jnp.float32), 'ln_b': jnp.zeros((DIM,), jnp.float32), 'Wp': jax.random.normal(ks[6], (DIM, DIM), jnp.float32) * s, 'bp': jnp.zeros((DIM,), jnp.float32)}
    _L0_xattn_all = _L0_xattn_setup()
    _L0_xattn_in = {k: v for k, v in _L0_xattn_all.items() if k in ('Wq', 'Wk', 'Wv', 'gate', 'ln_g', 'ln_b', 'Wp', 'bp')}
    del _L0_xattn_all

    def _L0_ffn_setup():
        import jax, jax.numpy as jnp
        import numpy as np
        K_TOP = 4
        ALPHA = 1.702
        LIMIT = 7.0
        key = jax.random.key(seed)
        ks = jax.random.split(key, 4)
        B, S, H, E, inter = (2, 256, 128, 16, 128)
        return {'hidden_states': jax.random.normal(ks[0], (B, S, H), dtype=jnp.float32), 'router_weight': jax.random.normal(ks[1], (E, H), dtype=jnp.float32) * 0.02, 'router_bias': jnp.zeros((E,), dtype=jnp.float32), 'gate_up_proj': jax.random.normal(ks[2], (E, H, 2 * inter), dtype=jnp.float32) * 0.02, 'gate_up_bias': jnp.zeros((E, 2 * inter), dtype=jnp.float32), 'down_proj': jax.random.normal(ks[3], (E, inter, H), dtype=jnp.float32) * 0.02, 'down_bias': jnp.zeros((E, H), dtype=jnp.float32)}
    _L0_ffn_all = _L0_ffn_setup()
    _L0_ffn_in = {k: v for k, v in _L0_ffn_all.items() if k in ('router_weight', 'router_bias', 'gate_up_proj', 'gate_up_bias', 'down_proj', 'down_bias')}
    del _L0_ffn_all

    def _L1_xattn_setup():
        import jax, jax.numpy as jnp
        import numpy as np
        B, S, D = (2, 256, 128)
        H = 16
        DK = D // H
        key = jax.random.key(seed)
        ks = jax.random.split(key, 7)
        scale = 1.0 / np.sqrt(D)
        return {'Query': jax.random.normal(ks[0], (B, S, D), dtype=jnp.float32), 'Key': jax.random.normal(ks[1], (B, S, D), dtype=jnp.float32), 'Value': jax.random.normal(ks[2], (B, S, D), dtype=jnp.float32), 'Wq': jax.random.normal(ks[3], (D, D), dtype=jnp.float32) * scale, 'Wk': jax.random.normal(ks[4], (D, D), dtype=jnp.float32) * scale, 'Wv': jax.random.normal(ks[5], (D, D), dtype=jnp.float32) * scale, 'Wo': jax.random.normal(ks[6], (D, D), dtype=jnp.float32) * scale}
    _L1_xattn_all = _L1_xattn_setup()
    _L1_xattn_in = {k: v for k, v in _L1_xattn_all.items() if k in ('Wq', 'Wk', 'Wv', 'Wo')}
    del _L1_xattn_all

    def _L1_ffn_setup():
        import jax, jax.numpy as jnp
        import numpy as np
        TOP_K = 2

        def _swiglu_mlp(x, wgu, wd, inter):
            gu = x @ wgu
            a = jax.nn.silu(gu[:, :inter]) * gu[:, inter:]
            return a @ wd
        key = jax.random.key(seed)
        ks = jax.random.split(key, 6)
        H, I, E = (128, 352, 8)
        B, S = (2, 128)
        w = 0.02
        return {'x': jax.random.normal(ks[0], (B, S, H), jnp.float32), 'gate_w': jax.random.normal(ks[1], (H, E), jnp.float32) * w, 'base_wgu': jax.random.normal(ks[2], (H, 2 * I), jnp.float32) * w, 'base_wd': jax.random.normal(ks[3], (I, H), jnp.float32) * w, 'exp_wgu': jax.random.normal(ks[4], (E, H, 2 * I), jnp.float32) * w, 'exp_wd': jax.random.normal(ks[5], (E, I, H), jnp.float32) * w}
    _L1_ffn_all = _L1_ffn_setup()
    _L1_ffn_in = {k: v for k, v in _L1_ffn_all.items() if k in ('gate_w', 'base_wgu', 'base_wd', 'exp_wgu', 'exp_wd')}
    del _L1_ffn_all
    return {'x': x, 'ctx_1024': ctx_1024, 'L0_xattn_Wq': _L0_xattn_in['Wq'], 'L0_xattn_Wk': _L0_xattn_in['Wk'], 'L0_xattn_Wv': _L0_xattn_in['Wv'], 'L0_xattn_gate': _L0_xattn_in['gate'], 'L0_xattn_ln_g': _L0_xattn_in['ln_g'], 'L0_xattn_ln_b': _L0_xattn_in['ln_b'], 'L0_xattn_Wp': _L0_xattn_in['Wp'], 'L0_xattn_bp': _L0_xattn_in['bp'], 'L0_ffn_router_weight': _L0_ffn_in['router_weight'], 'L0_ffn_router_bias': _L0_ffn_in['router_bias'], 'L0_ffn_gate_up_proj': _L0_ffn_in['gate_up_proj'], 'L0_ffn_gate_up_bias': _L0_ffn_in['gate_up_bias'], 'L0_ffn_down_proj': _L0_ffn_in['down_proj'], 'L0_ffn_down_bias': _L0_ffn_in['down_bias'], 'L1_xattn_Wq': _L1_xattn_in['Wq'], 'L1_xattn_Wk': _L1_xattn_in['Wk'], 'L1_xattn_Wv': _L1_xattn_in['Wv'], 'L1_xattn_Wo': _L1_xattn_in['Wo'], 'L1_ffn_gate_w': _L1_ffn_in['gate_w'], 'L1_ffn_base_wgu': _L1_ffn_in['base_wgu'], 'L1_ffn_base_wd': _L1_ffn_in['base_wd'], 'L1_ffn_exp_wgu': _L1_ffn_in['exp_wgu'], 'L1_ffn_exp_wd': _L1_ffn_in['exp_wd']}

def reference(x, ctx_1024, L0_xattn_Wq, L0_xattn_Wk, L0_xattn_Wv, L0_xattn_gate, L0_xattn_ln_g, L0_xattn_ln_b, L0_xattn_Wp, L0_xattn_bp, L0_ffn_router_weight, L0_ffn_router_bias, L0_ffn_gate_up_proj, L0_ffn_gate_up_bias, L0_ffn_down_proj, L0_ffn_down_bias, L1_xattn_Wq, L1_xattn_Wk, L1_xattn_Wv, L1_xattn_Wo, L1_ffn_gate_w, L1_ffn_base_wgu, L1_ffn_base_wd, L1_ffn_exp_wgu, L1_ffn_exp_wd):
    import jax
    import jax.numpy as jnp

    def _L0_xattn_ref(x, x_text, Wq, Wk, Wv, gate, ln_g, ln_b, Wp, bp):
        import jax, jax.numpy as jnp
        import numpy as np
        B, N, P, DIM, H = (8, 128, 77, 128, 16)
        HD = DIM // H
        LN_EPS = 1e-05
        b, n, c = x.shape
        h = gate.shape[1]
        q = x @ Wq.T
        k = jnp.concatenate([x_text @ Wk.T, x @ Wk.T], axis=1)
        v = jnp.concatenate([x_text @ Wv.T, x @ Wv.T], axis=1)
        kv = k.shape[1]
        q = q.reshape(b, n, h, -1).transpose(0, 2, 1, 3)
        k = k.reshape(b, kv, h, -1).transpose(0, 2, 1, 3)
        v = v.reshape(b, kv, h, -1).transpose(0, 2, 1, 3)
        d = q.shape[-1]
        scores = jnp.einsum('bhnd,bhkd->bhnk', q, k) / jnp.sqrt(jnp.float32(d))
        first = jnp.tanh(gate) * jnp.ones_like(scores[..., :1])
        rest = jax.nn.softmax(scores[..., 1:], axis=-1)
        attn = jnp.concatenate([first, rest], axis=-1)
        out = jnp.einsum('bhnk,bhkd->bhnd', attn, v)
        out = out.transpose(0, 2, 1, 3).reshape(b, n, -1)
        out = out.astype(jnp.bfloat16).astype(jnp.float32)
        mu = jnp.mean(out, axis=-1, keepdims=True)
        var = jnp.var(out, axis=-1, keepdims=True)
        out = (out - mu) / jnp.sqrt(var + LN_EPS) * ln_g + ln_b
        return out @ Wp.T + bp

    def _L0_ffn_ref(hidden_states, router_weight, router_bias, gate_up_proj, gate_up_bias, down_proj, down_bias):
        import jax, jax.numpy as jnp
        import numpy as np
        K_TOP = 4
        ALPHA = 1.702
        LIMIT = 7.0
        B, S, H = hidden_states.shape
        E, inter, _ = down_proj.shape
        logits = jnp.einsum('bsh,eh->bse', hidden_states, router_weight) + router_bias
        scores = jax.nn.softmax(logits, axis=-1)
        topk_w, topk_i = jax.lax.top_k(scores, K_TOP)
        gu = jnp.einsum('bsh,ehn->bsen', hidden_states, gate_up_proj) + gate_up_bias
        gate = jnp.minimum(gu[..., :inter], LIMIT)
        up = jnp.clip(gu[..., inter:], -LIMIT, LIMIT)
        glu = gate * jax.nn.sigmoid(gate * ALPHA)
        activated = (up + 1.0) * glu
        down = jnp.einsum('bsek,ekh->bseh', activated, down_proj) + down_bias
        sel = jnp.take_along_axis(down, topk_i[..., None], axis=2)
        out = jnp.sum(sel * topk_w[..., None], axis=2)
        return out

    def _L1_xattn_ref(Query, Key, Value, Wq, Wk, Wv, Wo):
        import jax, jax.numpy as jnp
        import numpy as np
        B, S, D = (2, 256, 128)
        H = 16
        DK = D // H
        b = Query.shape[0]
        q = (Query @ Wq.T).reshape(b, -1, H, DK).transpose(0, 2, 1, 3)
        k = (Key @ Wk.T).reshape(b, -1, H, DK).transpose(0, 2, 1, 3)
        v = (Value @ Wv.T).reshape(b, -1, H, DK).transpose(0, 2, 1, 3)
        scores = jnp.einsum('bhqd,bhkd->bhqk', q, k) / jnp.sqrt(jnp.float32(DK))
        attn = jax.nn.softmax(scores, axis=1)
        ctx = jnp.einsum('bhqk,bhkd->bhqd', attn, v)
        ctx = ctx.transpose(0, 2, 1, 3).reshape(b, -1, H * DK)
        return ctx @ Wo.T

    def _L1_ffn_ref(x, gate_w, base_wgu, base_wd, exp_wgu, exp_wd):
        import jax, jax.numpy as jnp
        import numpy as np
        TOP_K = 2

        def _swiglu_mlp(x, wgu, wd, inter):
            gu = x @ wgu
            a = jax.nn.silu(gu[:, :inter]) * gu[:, inter:]
            return a @ wd
        orig_shape = x.shape
        H = orig_shape[-1]
        I = base_wd.shape[0]
        E = gate_w.shape[1]
        xt = x.reshape(-1, H)
        T = xt.shape[0]
        base_y = _swiglu_mlp(xt, base_wgu, base_wd, I)
        logits = xt @ gate_w
        probs = jax.nn.softmax(logits.astype(jnp.float32), axis=-1)
        topw, topi = jax.lax.top_k(probs, TOP_K)
        topw = topw / jnp.sum(topw, axis=-1, keepdims=True)
        topw = topw.astype(x.dtype)
        cw = jnp.zeros((T, E), x.dtype).at[jnp.arange(T)[:, None], topi].add(topw)
        out = base_y
        for e in range(E):
            ye = _swiglu_mlp(xt, exp_wgu[e], exp_wd[e], I)
            out = out + cw[:, e:e + 1] * ye
        return out.reshape(orig_shape)
    x = x + _L0_xattn_ref(_layernorm(x, axis=-1), ctx_1024, L0_xattn_Wq, L0_xattn_Wk, L0_xattn_Wv, L0_xattn_gate, L0_xattn_ln_g, L0_xattn_ln_b, L0_xattn_Wp, L0_xattn_bp)
    x = x + _L0_ffn_ref(_layernorm(x, axis=-1), L0_ffn_router_weight, L0_ffn_router_bias, L0_ffn_gate_up_proj, L0_ffn_gate_up_bias, L0_ffn_down_proj, L0_ffn_down_bias)
    x = x + _L1_xattn_ref(_layernorm(x, axis=-1), ctx_1024, ctx_1024, L1_xattn_Wq, L1_xattn_Wk, L1_xattn_Wv, L1_xattn_Wo)
    x = x + _L1_ffn_ref(_layernorm(x, axis=-1), L1_ffn_gate_w, L1_ffn_base_wgu, L1_ffn_base_wd, L1_ffn_exp_wgu, L1_ffn_exp_wd)
    return x

_drawn_inputs = setup_inputs


def setup_inputs(seed=0):
    import zlib

    import numpy as np

    out = dict(_drawn_inputs(seed))
    spreads = {'L0_xattn_ln_g': (1.0, 0.543),
     'L0_xattn_ln_b': (0.0, 0.497),
     'L0_xattn_bp': (0.0, 0.1),
     'L0_ffn_router_bias': (0.0, 0.8),
     'L0_ffn_gate_up_bias': (0.0, 0.8),
     'L0_ffn_down_bias': (0.0, 0.722)}
    factors = {'L0_xattn_Wq': 8.0,
     'L0_xattn_Wk': 8.0,
     'L0_ffn_router_weight': 5.57,
     'L0_ffn_gate_up_proj': 8.0,
     'L0_ffn_down_proj': 8.0,
     'L1_ffn_gate_w': 8.0,
     'L1_ffn_base_wgu': 8.0,
     'L1_ffn_base_wd': 8.0,
     'L1_ffn_exp_wgu': 8.0,
     'L1_ffn_exp_wd': 8.0}
    for name, (base, spread) in spreads.items():
        noise = np.random.default_rng([zlib.crc32(name.encode()), seed]).standard_normal(out[name].shape)
        drawn = base * np.exp(spread * noise) if base else spread * noise
        out[name] = jnp.asarray(drawn.astype(out[name].dtype))
    for name, factor in factors.items():
        out[name] = (out[name] * factor).astype(out[name].dtype)
    return out
```

```python
from contextlib import ExitStack

import concourse.bass as bass
import numpy as np
from concourse import mybir

F32 = mybir.dt.float32
F32R = mybir.dt.float32r
BF16 = mybir.dt.bfloat16
ALU = mybir.AluOpType
ACT = mybir.ActivationFunctionType
AX_X = mybir.AxisListType.X

P = 128
B = 8
D = 128
H = 16
HD = D // H
GH = 4
G = H // GH
SLOT = P // GH
HB = 4
HALVES = B // HB
HT = HB * P
T = B * P
KEYS = 2 * P
LN_EPS = 1e-5
SCALE = float(HD) ** -0.5
E0, TOP0 = 16, 4
F0 = 128
ALPHA, LIMIT = 1.702, 7.0
E1, TOP1 = 8, 2
F1 = 352
CH1 = [(0, 128), (128, 128), (256, 96)]
PARTS = 3
OUTW = D + H

SH = 3
STAGES = 4
A0_CHAIN, A1_CHAIN = 24, 10

C_ID, C_NEG, C_QSEL, C_KSEL, C_ONE, C_GATHER = 0, 128, 256, 257, 258, 258 + P
C_END = C_GATHER + G * OUTW
W_NAMES = ["wv0", "wp0", "wv1", "rw0", "gw1"]
W_WIDTH = {"wv0": D, "wp0": D, "wv1": D, "rw0": E0, "gw1": E1}
W_AT, _at = {}, 0
for _n in W_NAMES:
    W_AT[_n] = _at
    _at += W_WIDTH[_n]
W_LN = _at
W_WO = _at + 2
W_END = W_WO + G * D
R_GATE, R_BP, R_RB, R_END = 0, H, H + D, H + D + E0


def two_layers(nc, x, ctx_t, qk_w, small_w, consts, rows, down_bias, gu_bias, part_sel, ident_bf, experts0, experts1, out):
    with ExitStack() as ctx:
        def sb(name, shape, dt=F32):
            return ctx.enter_context(nc.sbuf_tensor(name, shape, dt))

        def sem(name):
            return ctx.enter_context(nc.semaphore(name))

        ps = ctx.enter_context(nc.psum_tensor("ps", [P, 8, 512], F32))
        resid = sb("resid", [P, B, D])
        ctx_sb = sb("ctx_sb", [P, T])
        qk_hi = sb("qk_hi", [P, 4, G * P], F32R)
        qk_lo = sb("qk_lo", [P, 4, G * P], F32R)
        small = sb("small", [P, W_END])
        cst = sb("cst", [P, C_END])
        row = sb("row", [1, R_END])
        negid = sb("negid", [P, P], F32R)
        ones = sb("ones", [P, P], F32R)
        ones_but0 = sb("ones_but0", [P, P], F32R)
        zero_r = sb("zero_r", [P, 512], F32R)
        tanh_gate = sb("tanh_gate", [1, H])
        db0 = sb("db0", [P, D])
        psel = sb("psel", [P, E0, P], BF16)
        idb = sb("idb", [P, P], BF16)
        xn = sb("xn", [P, B, D])
        stats = sb("stats", [P, B, 6])
        mv = sb("mv", [P, B, 3])
        rvar = sb("rvar", [P, B])
        rstd = sb("rstd", [P, B])
        x_f = sb("x_f", [P, T])
        x_hi = sb("x_hi", [P, T], F32R)
        x_lo = sb("x_lo", [P, T], F32R)
        c_f = sb("c_f", [P, HT])
        c_hi = sb("c_hi", [P, HT], F32R)
        c_lo = sb("c_lo", [P, HT], F32R)
        vals = sb("vals", [P, 2, HB, H, SLOT])
        first_v = sb("first_v", [1, HB, H, HD])
        first_b = sb("first_b", [P, HB, D])
        rnd = sb("rnd", [P, 2, 512], F32R)
        q_st = sb("q_st", [P, 2, HT], F32R)
        q_blk = sb("q_blk", [P, G, GH, HT], F32R)
        k_st = sb("k_st", [P, G, HB, KEYS], F32R)
        neg_max = sb("neg_max", [P, SH, GH])
        shift = sb("shift", [P, SH, GH, P], F32R)
        rsum = sb("rsum", [P, HB, H])
        attn = sb("attn", [P, HB, H, HD])
        attn_bf = sb("attn_bf", [P, HB, D], BF16)
        ln_t = attn[:].rearrange("p b h d -> p (b h d)")
        hmax = sb("hmax", [P, 2, P], F32R)
        hrec = sb("hrec", [P, 2, P])
        heads1 = sb("heads1", [P, 2, G, P])
        logit = sb("logit", [P, B, E0])
        top8 = sb("top8", [P, B, 8])
        rmax = sb("rmax", [P, B])
        score = [sb(f"score{k}", [P, B, E0 + 8]) for k in range(2)]
        kept = sb("kept", [P, B, E0 + 8])
        tokw = sb("tokw", [P, B, E0])
        tokr = sb("tokr", [P, 2, B, E0])
        wparts = sb("wparts", [P, B, P], BF16)
        wt_bf = sb("wt_bf", [P, T], BF16)
        exp_f = sb("exp_f", [P, 2, 2 * F1])
        exp_d = sb("exp_d", [P, 2, 3 * D])
        exp_hi = sb("exp_hi", [P, 2, 2 * F1], F32R)
        exp_lo = sb("exp_lo", [P, 2, 2 * F1], F32R)
        biases = sb("biases", [P, 2, E0])
        up_b = sb("up_b", [P, E0])

        room = sb("room", [P, 6, 1024])
        flat = room[:].rearrange("p a n -> p (a n)")
        qk_f = flat[:, 0:2048].rearrange("p (w n) -> p w n", w=4)
        probs = flat[:, 0:2048].rearrange("p (s c n) -> p s c n", s=2, c=2)
        heads_t = flat[:, 2048:4096].rearrange("p (g n) -> p g n", g=G)
        hprobs = flat[:, 0:4096].rearrange("p (s h q) -> p s h q", s=2, h=H)
        hsum = flat[:, 4096:6144].rearrange("p (s h q) -> p s h q", s=2, h=H // 2)
        wbc, gate_a, up_a, glu, glw, act_f = (room[:, n, :].rearrange("p (s n) -> p s n", s=2) for n in range(6))
        wt_f = room[:, 5, :]
        acc_sb = x_f

        ident = cst[:, C_ID:C_ID + P]
        qsel, ksel = cst[:, C_QSEL:C_QSEL + 1], cst[:, C_KSEL:C_KSEL + 1]
        one_row = cst[0:1, C_ONE:C_ONE + P]
        gather = cst[:, C_GATHER:C_END].rearrange("p (g n) -> p g n", g=G)
        w = {n: small[:, W_AT[n]:W_AT[n] + W_WIDTH[n]] for n in W_NAMES}
        ln_g, ln_b = small[:, W_LN:W_LN + 1], small[:, W_LN + 1:W_LN + 2]
        wo1 = small[:, W_WO:W_END].rearrange("p (g n) -> p g n", g=G)

        def sems(prefix, names):
            return {n: sem(prefix + n) for n in names.split()}

        loaded = sem("loaded")
        stored = sem("stored")
        ready = sems("ready_", "zeroed ones tanh split qk_hi")
        a0 = sems("a0_", "var std norm xt ctxc xc lo v vcopy first firstp firstb proj rnd stk blk0 blk1 qk max shift st "
                         "exp pv ot gat attn var2 std2 norm2 t2 aff wp res chain")
        a1 = sems("a1_", "var std norm xt ctxc xc lo v vcopy proj rnd stk blk0 blk1 st max nm exp sum rec wts pv ot wo "
                         "res chain pchain")
        ffn = [sems(f"f{k}_", "var std norm xt xc lo logit lmax e tokw wp wt wtc wdma0 wdma1 ddma0 ddma1 wfree whi wlo gu wb wbc "
                              "ga ua glu glw act down acc tr res chain") for k in range(2)]

        def layer_norm_stats(dve, s, src, n, chain, var):
            even, odd = stats[:, 0:n, 1:3], stats[:, 0:n, 4:6]
            for b in range(n):
                chain.step(dve.bn_stats(stats[:, b, :], src(b)))
            chain.sync()
            chain.step(dve.tensor_tensor(mv[:, 0:n, 0:2], even, odd, ALU.add))
            chain.step(dve.tensor_tensor(mv[:, 0:n, 2], even[:, :, 0], odd[:, :, 0], ALU.subtract))
            chain.sync()
            chain.step(dve.tensor_scalar(mv[:, 0:n, 1], mv[:, 0:n, 1], 1.0 / D, LN_EPS, ALU.mult, ALU.add))
            chain.step(dve.scalar_tensor_tensor(mv[:, 0:n, 2], mv[:, 0:n, 2], 0.25, mv[:, 0:n, 2], ALU.mult,
                                                ALU.mult))
            chain.step(dve.tensor_scalar(mv[:, 0:n, 0], mv[:, 0:n, 0], 0.5, None, ALU.mult))
            chain.sync()
            chain.step(dve.tensor_tensor(rvar[:, 0:n], mv[:, 0:n, 1], mv[:, 0:n, 2], ALU.add))
            chain.sync()
            dve.reciprocal(rvar[:, 0:n], rvar[:, 0:n]).then_inc(s[var], 1)

        class Chain:

            def __init__(self, eng, counter, base=0, per=None):
                self.eng, self.counter, self.base, self.per, self.n = eng, counter, base, per, 0

            def step(self, ins):
                self.n += 1
                ins.then_inc(self.counter, 1)

            def sync(self):
                self.eng.wait_ge(self.counter, self.base + self.n)

            def close(self):
                assert self.n == self.per, (self.n, self.per)

        block = ctx.enter_context(nc.Block())

        def pieces_at(n):
            g, b = divmod(n, HB)
            return [] if g + 1 == G or b > 1 else [3 * (g + 1) + 2] if b else [3 * (g + 1), 3 * (g + 1) + 1]

        def fetch_expert(sp, k, src, slot, what="both"):
            width, d_width = ((2 * F0, D), (2 * F1, 3 * D))[k]
            if what != "down":
                sp.dma_start(exp_f[:, slot, 0:width], src[:, 0:width]).then_inc(ffn[k][f"wdma{slot}"], 16)
            if what != "gate_up":
                sp.dma_start(exp_d[:, slot, 0:d_width],
                             src[:, width:width + d_width]).then_inc(ffn[k][f"ddma{slot}"], 16)

        @block.sync
        def _(sp):
            for dst, src in ((resid[:], x.rearrange("b t d -> t b d")), (cst[:], consts), (qk_f, qk_w),
                             (ctx_sb[:], ctx_t), (small[:], small_w), (row[:], rows), (db0[:], down_bias), (biases[:], gu_bias),
                             (psel[:], part_sel), (idb[:], ident_bf)):
                sp.dma_start(dst, src).then_inc(loaded, 16)
            for e in range(2):
                fetch_expert(sp, 0, experts0[e], e)

            def block_queries(s, stk0, per_group):
                for g in range(G):
                    sp.wait_ge(s["stk"], stk0 + per_group * g + 1)
                    for j in range(GH):
                        rows_j = slice(SLOT * j, SLOT * (j + 1))
                        sp.dma_start(q_blk[rows_j, g, j, :].bitcast(F32),
                                     q_st[rows_j, g % 2, :].bitcast(F32)).then_inc(s[f"blk{g % 2}"], 16)

            def fetch_experts(k, experts, n):
                s = ffn[k]
                with sp.Fori(0, n // 2 - 1) as i:
                    for slot in range(2):
                        src = experts[bass.ds(i * 2 + 2 + slot, 1)].rearrange("e p n -> p (e n)")
                        sp.wait_ge(s["wlo"], i * 2 + slot + 1)
                        fetch_expert(sp, k, src, slot, "gate_up")
                        sp.wait_ge(s["wfree"], i * 2 + slot + 1)
                        fetch_expert(sp, k, src, slot, "down")

            sp.wait_ge(ready["zeroed"], 1)
            with sp.Fori(0, HALVES) as i:
                block_queries(a0, i * (3 * G), 3)
            if STAGES > 1:
                fetch_experts(0, experts0, E0)
            if STAGES > 2:
                with sp.Fori(0, HALVES) as i:
                    block_queries(a1, i * (2 * G), 2)
            if STAGES > 3:
                for e in range(2):
                    sp.wait_ge(ffn[0]["down"], 2)
                    fetch_expert(sp, 1, experts1[e], e)
                fetch_experts(1, experts1, E1)
                sp.wait_ge(ffn[1]["wlo"], E1 - 1)
                fetch_expert(sp, 1, experts1[E1], 0, "gate_up")
                sp.wait_ge(ffn[1]["wfree"], E1 - 1)
                fetch_expert(sp, 1, experts1[E1], 0, "down")
            last = [a0["res"], ffn[0]["res"], a1["res"], ffn[1]["res"]][STAGES - 1]
            per = [1, 1, 4, 1][STAGES - 1]
            for h in range(2):
                sp.wait_ge(last, per * (h + 1))
                sp.dma_start(out.rearrange("b t d -> t b d")[:, HB * h:HB * (h + 1), :],
                             resid[:, HB * h:HB * (h + 1), :]).then_inc(stored, 16)
            sp.wait_ge(stored, 32)

        LOADED = 16 * 10

        @block.gpsimd
        def _(pool):
            pool.memset(zero_r[:].bitcast(F32), 0.0)
            pool.memset(wparts[:], 0.0)
            pool.memset(ones[:].bitcast(F32), 1.0).then_inc(ready["ones"], 1)
            pool.memset(k_st[:].bitcast(F32), 0.0)
            pool.memset(vals[:], 0.0).then_inc(ready["ones"], 1)
            pool.wait_ge(ready["ones"], 2)
            pool.memset(vals[:, :, :, :, HD:HD + 1], 1.0).then_inc(ready["ones"], 1)
            pool.wait_ge(ready["ones"], 3)
            pool.memset(vals[0:1, 0, :, :, HD:HD + 1], 0.0)
            pool.tensor_copy(ones_but0[:, 1:P], ones[:, 1:P].bitcast(F32))
            pool.memset(ones_but0[:, 0:1].bitcast(F32), 0.0)
            for k, (e, top) in enumerate(((E0, TOP0), (E1, TOP1))):
                for n in range(8 - top):
                    pool.memset(score[k][:, :, e + n:e + n + 1], -1.0 - n)
            pool.memset(q_blk[:].bitcast(F32), 0.0).then_inc(ready["zeroed"], 1)
            pool.wait_ge(loaded, LOADED)
            with pool.Fori(0, HALVES) as i:
                for n in range(G * HB):
                    pool.wait_ge(a0["max"], i * 32 + 2 * n + 2)
                    if n >= SH:
                        pool.wait_ge(a0["st"], i * 32 + 2 * (n - SH + 1))
                    pool.tensor_tensor(shift[:, n % SH], ident.unsqueeze(1).to_broadcast([P, GH, P]),
                                       neg_max[:, n % SH, :].unsqueeze(2).to_broadcast([P, GH, P]),
                                       ALU.mult).then_inc(a0["shift"], 1)

            def low_parts(s, e, slot, width):
                pool.wait_ge(s["whi"], e + 1)
                pool.tensor_tensor(exp_lo[:, slot, 0:width], exp_f[:, slot, 0:width],
                                   exp_hi[:, slot, 0:width].bitcast(F32), ALU.subtract).then_inc(s["wlo"], 1)

            def weigh(s, n, e, h, slot, m):
                pool.wait_ge(s["glu"], n + 1)
                pool.wait_ge(s["wbc"], e * 2 + h + 1)
                pool.tensor_tensor(glw[0:m, slot, :], glu[0:m, slot, :], wbc[0:m, h, :],
                                   ALU.mult).then_inc(s["glw"], 1)

            if STAGES > 1:
                s = ffn[0]
                low_parts(s, 0, 0, 2 * F0)

                def expert0(e, slot, last):
                    if not last:
                        low_parts(s, e + 1, 1 - slot, 2 * F0)
                    for h in range(2):
                        weigh(s, e * 2 + h, e, h, h, P)

                with pool.Fori(0, E0 // 2 - 1) as i:
                    for slot in range(2):
                        expert0(i * 2 + slot, slot, False)
                for slot in range(2):
                    expert0(E0 - 2 + slot, slot, slot == 1)
            if STAGES > 2:
                with pool.Fori(0, HALVES) as i:
                    chain = Chain(pool, a1["pchain"], i * (3 * HB), 3 * HB)
                    for b in range(HB):
                        pool.wait_ge(a1["exp"], i * HB + b + 1)
                        if b >= 2:
                            pool.wait_ge(a1["rec"], i * HB + b - 1)
                        chain.step(pool.tensor_tensor(hsum[:, b % 2], hprobs[:, b % 2, 0:8, :],
                                                      hprobs[:, b % 2, 8:16, :], ALU.add))
                        for k in (4, 2, 1):
                            chain.sync()
                            ins = pool.tensor_tensor(hsum[:, b % 2, 0:k, :], hsum[:, b % 2, 0:k, :],
                                                     hsum[:, b % 2, k:2 * k, :], ALU.add)
                            if k > 1:
                                chain.step(ins)
                            else:
                                ins.then_inc(a1["sum"], 1)
                    chain.close()
            if STAGES > 3:
                s = ffn[1]
                low_parts(s, 0, 0, 2 * F1)

                def expert1(e, slot):
                    low_parts(s, e + 1, 1 - slot, 2 * F1)
                    for h in range(2):
                        for c, (_, m) in enumerate(CH1):
                            n = h * 3 + c
                            weigh(s, e * 6 + n, e, h, n % 2, m)

                with pool.Fori(0, E1 // 2) as i:
                    for slot in range(2):
                        expert1(i * 2 + slot, slot)

        @block.scalar
        def _(act):
            def copy(dst, src):
                return act.activation(dst, src, ACT.Copy)

            act.wait_ge(loaded, LOADED)
            act.activation(tanh_gate[:], row[:, R_GATE:R_GATE + H], ACT.Tanh).then_inc(ready["tanh"], 1)
            copy(negid[:], cst[:, C_NEG:C_NEG + P])
            copy(qk_hi[:], qk_f).then_inc(ready["qk_hi"], 1)

            def prelude(s, i, k):
                act.wait_ge(s["var"], i * k + 1)
                act.activation(rstd[:, 0:HB], rvar[:, 0:HB], ACT.Sqrt).then_inc(s["std"], 1)
                copy(c_f[:], ctx_sb[:, bass.ds(i * HT, HT)]).then_inc(s["ctxc"], 1)
                copy(c_hi[:], ctx_sb[:, bass.ds(i * HT, HT)]).then_inc(s["ctxc"], 1)
                act.wait_ge(s["xt"], i + 1)
                copy(x_f[:, 0:HT], ps[:, 0, :]).then_inc(s["xc"], 1)
                copy(x_hi[:, 0:HT], ps[:, 0, :]).then_inc(s["xc"], 1)

            def copy_values(s, base, c):
                act.wait_ge(s["v"], base + c + 1)
                copy(vals[:, c, :, :, 0:HD], ps[:, 1 + c, :].rearrange("p (b h d) -> p b h d", b=HB, h=H)
                     ).then_inc(s["vcopy"], 1)

            def round_piece(s, base, n):
                act.wait_ge(s["proj"], base + n + 1)
                if n >= 2:
                    act.wait_ge(s["stk"], base + n - 1)
                copy(rnd[:, n % 2, :], ps[:, n % 2, :]).then_inc(s["rnd"], 1)

            with act.Fori(0, HALVES) as i:
                s = a0
                prelude(s, i, 1)
                for c in range(2):
                    copy_values(s, i * 2, c)
                act.wait_ge(s["firstp"], i + 1)
                copy(first_b[:], ps[:, 3, :].rearrange("p (b d) -> p b d", b=HB)).then_inc(s["firstb"], 1)
                for n in range(3):
                    round_piece(s, i * 12, n)
                for n in range(G * HB):
                    g, b = divmod(n, HB)
                    for c in range(2):
                        act.wait_ge(s["st"], i * 32 + 2 * n + c + 1)
                        if n >= 2:
                            act.wait_ge(s["pv"], i * 16 + n - 1)
                        act.activation(probs[:, n % 2, c, :], ps[:, 4 + c, :], ACT.Exp,
                                       scale=SCALE).then_inc(s["exp"], 1)
                    for piece in pieces_at(n):
                        round_piece(s, i * 12, piece)
                    if g >= 1 and b == 1:
                        act.wait_ge(s["pv"], i * 16 + 4 * g)
                        copy(heads_t[:, g - 1, :], ps[:, 6 + (g - 1) % 2, :]).then_inc(s["ot"], 1)
                act.wait_ge(s["pv"], i * 16 + 16)
                copy(heads_t[:, G - 1, :], ps[:, 6 + (G - 1) % 2, :]).then_inc(s["ot"], 1)
                act.wait_ge(s["var2"], i + 1)
                act.activation(rstd[:, 0:HB], rvar[:, 0:HB], ACT.Sqrt).then_inc(s["std2"], 1)
                act.wait_ge(s["t2"], i + 1)
                act.activation(ln_t, ps[:, 6, :], ACT.Identity, bias=ln_b, scale=ln_g).then_inc(s["aff"], 1)

            def ffn_prelude(s, k):
                act.wait_ge(s["wdma0"], 16)
                width = 2 * (F0, F1)[k]
                copy(exp_hi[:, 0, 0:width], exp_f[:, 0, 0:width]).then_inc(s["whi"], 1)
                act.wait_ge(s["var"], 1)
                act.activation(rstd[:], rvar[:], ACT.Sqrt).then_inc(s["std"], 1)
                act.wait_ge(s["xt"], 1)
                both = ps[:, 0:2, :].rearrange("p k n -> p (k n)")
                copy(x_f[:], both).then_inc(s["xc"], 1)
                copy(x_hi[:], both).then_inc(s["xc"], 1)
                act.wait_ge(s["lmax"], 1)
                e = (E0, E1)[k]
                act.activation(logit[:, :, 0:e], logit[:, :, 0:e], ACT.Exp).then_inc(s["e"], 1)
                act.wait_ge(s["wt"], 1)
                both = ps[:, 3:5, :].rearrange("p k n -> p (k n)")
                copy(wt_bf[:], both).then_inc(s["wtc"], 1)
                if k == 0:
                    copy(wt_f[:], both).then_inc(s["wtc"], 1)

            def high_parts(s, i, slot, k, units):
                width = 2 * (F0, F1)[k]
                act.wait_ge(s[f"wdma{1 - slot}"], (i + slot + 1) * 16)
                act.wait_ge(s["gu"], (i * 2 + slot) * units * 2 + 1)
                copy(exp_hi[:, 1 - slot, 0:width], exp_f[:, 1 - slot, 0:width]).then_inc(s["whi"], 1)

            def weights_copy(s, e, h):
                act.wait_ge(s["wb"], e * 2 + h + 1)
                copy(wbc[:, h, :], ps[:, 4 + h, :]).then_inc(s["wbc"], 1)

            def acc_copy(s):
                for h in range(2):
                    act.wait_ge(s["down"], h + 1)
                    copy(acc_sb[:, 512 * h:512 * (h + 1)], ps[:, 6 + h, :]).then_inc(s["acc"], 1)

            if STAGES > 1:
                s = ffn[0]
                ffn_prelude(s, 0)

                def expert0(i, slot, last):
                    e = i * 2 + slot
                    if not last:
                        high_parts(s, i, slot, 0, 2)
                    for h in range(2):
                        weights_copy(s, e, h)
                        act.wait_ge(s["ga"], e * 2 + h + 1)
                        act.activation(glu[:, h, :], gate_a[:, h, :],
                                       ACT.Gelu_apprx_sigmoid).then_inc(s["glu"], 1)

                act.preload_act_table(ACT.Gelu_apprx_sigmoid)
                with act.Fori(0, E0 // 2 - 1) as i:
                    for slot in range(2):
                        expert0(i, slot, False)
                for slot in range(2):
                    expert0(E0 // 2 - 1, slot, slot == 1)
                acc_copy(s)
            if STAGES > 2:
                s = a1
                with act.Fori(0, HALVES) as i:
                    prelude(s, i, 1)
                    copy_values(s, i, 0)
                    for n in range(2 * G):
                        round_piece(s, i * (2 * G), n)
                    for b in range(HB):
                        act.wait_ge(s["nm"], i * HB + b + 1)
                        act.activation(hprobs[:, b % 2].rearrange("p h q -> p (h q)"),
                                       ps[:, 4 * (b % 2):4 * (b % 2) + 4, :].rearrange("p k n -> p (k n)"),
                                       ACT.Exp, scale=SCALE).then_inc(s["exp"], 1)
                        if b >= 1:
                            act.wait_ge(s["pv"], i * HB + b)
                            copy(heads1[:, (b - 1) % 2].rearrange("p g q -> p (g q)"),
                                 ps[:, 4 * ((b - 1) % 2), :]).then_inc(s["ot"], 1)
                    act.wait_ge(s["pv"], i * HB + HB)
                    copy(heads1[:, (HB - 1) % 2].rearrange("p g q -> p (g q)"),
                         ps[:, 4 * ((HB - 1) % 2), :]).then_inc(s["ot"], 1)
            if STAGES > 3:
                s = ffn[1]
                ffn_prelude(s, 1)

                def silu(e, h, c, m):
                    n = h * 3 + c
                    act.wait_ge(s["gu"], (e * 6 + n) * 2 + 1)
                    act.activation(glu[0:m, n % 2, :], ps[0:m, n % 2, :], ACT.Silu).then_inc(s["glu"], 1)

                def expert1(i, slot, routed):
                    e = i * 2 + slot
                    if routed:
                        high_parts(s, i, slot, 1, 6)
                    for h in range(2):
                        if routed:
                            weights_copy(s, e, h)
                        for c, (_, m) in enumerate(CH1):
                            silu(e, h, c, m)

                act.preload_act_table(ACT.Silu)
                with act.Fori(0, E1 // 2) as i:
                    for slot in range(2):
                        expert1(i, slot, True)
                expert1(E1 // 2, 0, False)
                acc_copy(s)

        @block.vector
        def _(dve):
            dve.wait_ge(loaded, LOADED)
            dve.wait_ge(ready["qk_hi"], 1)
            dve.tensor_tensor(qk_lo[:], qk_f, qk_hi[:].bitcast(F32), ALU.subtract).then_inc(ready["split"], 1)
            dve.tensor_scalar(up_b[:], biases[:, 1, :], 1.0, None, ALU.add)

            def normalised(s, chain, src, n, std, std_at, done):
                dve.wait_ge(s[std], std_at)
                for b in range(n):
                    dve.tensor_scalar(xn[:, b, :], src(b), mv[:, b, 0:1], rstd[:, b:b + 1], ALU.subtract,
                                      ALU.mult).then_inc(s[done], 1)

            def split_half(s, i):
                dve.wait_ge(s["ctxc"], i * 2 + 2)
                dve.tensor_tensor(c_lo[:], c_f[:], c_hi[:].bitcast(F32), ALU.subtract).then_inc(s["lo"], 1)
                dve.wait_ge(s["xc"], i * 2 + 2)
                dve.tensor_tensor(x_lo[:, 0:HT], x_f[:, 0:HT], x_hi[:, 0:HT].bitcast(F32),
                                  ALU.subtract).then_inc(s["lo"], 1)

            def stack_piece(s, base, per_group, n, blk, skip_first):
                g, kind = divmod(n, per_group)
                dve.wait_ge(s["rnd"], base + n + 1)
                src, hi = ps[:, n % 2, :], rnd[:, n % 2, :].bitcast(F32)
                if kind == 0:
                    if g >= 2:
                        dve.wait_ge(s[f"blk{g % 2}"], blk + 16 * GH * (g // 2))
                    dve.scalar_tensor_tensor(q_st[:, g % 2, :], hi, qsel, src, ALU.mult,
                                             ALU.add).then_inc(s["stk"], 1)
                else:
                    lead = 1 if skip_first and kind == 1 else 0
                    at = (kind - 1) * P
                    dve.scalar_tensor_tensor(
                        k_st[:, g, :, at + lead:at + P],
                        hi.rearrange("p (b k) -> p b k", b=HB)[:, :, lead:], ksel,
                        src.rearrange("p (b k) -> p b k", b=HB)[:, :, lead:], ALU.mult,
                        ALU.add).then_inc(s["stk"], 1)

            with dve.Fori(0, HALVES) as i:
                s = a0
                chain = Chain(dve, s["chain"], i * A0_CHAIN, A0_CHAIN)

                def tile_of_half(b):
                    return resid[:, bass.ds(i * HB + b, 1), :].rearrange("p o d -> p (o d)")

                layer_norm_stats(dve, s, tile_of_half, HB, chain, "var")
                normalised(s, chain, tile_of_half, HB, "std", i + 1, "norm")
                split_half(s, i)
                dve.wait_ge(ready["tanh"], 1)
                dve.wait_ge(s["vcopy"], i * 2 + 1)
                chain.step(dve.tensor_tensor(
                    first_v[:], vals[0:1, 0, :, :, 0:HD],
                    tanh_gate[:].unsqueeze(1).unsqueeze(3).to_broadcast([1, HB, H, HD]), ALU.mult))
                chain.sync()
                dve.memset(vals[0:1, 0, :, :, 0:HD], 0.0).then_inc(s["first"], 1)
                dve.wait_ge(ready["zeroed"], 1)
                for n in range(3):
                    stack_piece(s, i * 12, 3, n, i * 128, True)
                for n in range(G * HB):
                    for u in range(2):
                        dve.wait_ge(s["qk"], i * 32 + 2 * n + u + 1)
                        if n >= SH:
                            dve.wait_ge(s["shift"], i * 16 + n - SH + 1)
                        dve.tensor_reduce(neg_max[:, n % SH, 2 * u:2 * u + 2],
                                          ps[:, 2 + u, :].rearrange("p (j k) -> p j k", j=2)[:, :, 1:],
                                          AX_X, ALU.max, negate=True).then_inc(s["max"], 1)
                    if n >= 2:
                        for piece in pieces_at(n - 2):
                            stack_piece(s, i * 12, 3, piece, i * 128, True)
                dve.wait_ge(s["gat"], i * HB + HB)
                chain.step(dve.reciprocal(rsum[:], ps[:, 2:6, D:OUTW]))
                chain.sync()
                chain.step(dve.tensor_tensor(attn[:], ps[:, 2:6, 0:D].rearrange("p b (h d) -> p b h d", h=H),
                                             rsum[:].unsqueeze(3).to_broadcast([P, HB, H, HD]), ALU.mult))
                chain.sync()
                dve.wait_ge(s["firstb"], i + 1)
                chain.step(dve.tensor_tensor(attn_bf[:], attn[:].rearrange("p b h d -> p b (h d)"), first_b[:],
                                             ALU.add))
                chain.sync()
                layer_norm_stats(dve, s, lambda b: attn_bf[:, b, :], HB, chain, "var2")
                normalised(s, chain, lambda b: attn_bf[:, b, :], HB, "std2", i + 1, "norm2")
                dve.wait_ge(s["wp"], i + 1)
                half = resid[:, bass.ds(i * HB, HB), :]
                dve.tensor_tensor(half, half, ps[:, 7, :].rearrange("p (b d) -> p b d", b=HB),
                                  ALU.add).then_inc(s["res"], 1)
                dve.wait_ge(s["res"], i + 1)
                chain.close()

            def ffn_prelude(s, k):
                e, top = ((E0, TOP0), (E1, TOP1))[k]
                fill = 8 - top
                chain = Chain(dve, s["chain"])
                layer_norm_stats(dve, s, lambda b: resid[:, b, :], B, chain, "var")
                normalised(s, chain, lambda b: resid[:, b, :], B, "std", 1, "norm")
                dve.wait_ge(s["xc"], 2)
                dve.tensor_tensor(x_lo[:], x_f[:], x_hi[:].bitcast(F32), ALU.subtract).then_inc(s["lo"], 1)
                dve.wait_ge(s["logit"], 1)
                lg = ps[:, 2, 0:B * e].rearrange("p (t e) -> p t e", t=B)
                chain.step(dve.tensor_reduce(rmax[:], lg, AX_X, ALU.max))
                chain.sync()
                dve.tensor_tensor(logit[:, :, 0:e], lg, rmax[:].unsqueeze(2).to_broadcast([P, B, e]),
                                  ALU.subtract).then_inc(s["lmax"], 1)
                dve.wait_ge(s["e"], 1)
                chain.step(dve.tensor_reduce(rmax[:], logit[:, :, 0:e], AX_X, ALU.add))
                chain.sync()
                chain.step(dve.reciprocal(rmax[:], rmax[:]))
                chain.sync()
                sc = score[k]
                chain.step(dve.tensor_tensor(sc[:, :, 0:e], logit[:, :, 0:e],
                                             rmax[:].unsqueeze(2).to_broadcast([P, B, e]), ALU.mult))
                chain.sync()
                for t in range(B):
                    chain.step(dve.max(top8[:, t, :], sc[:, t, 0:e]))
                chain.sync()
                chain.step(dve.tensor_copy(top8[:, :, top:8], sc[:, :, e:e + fill]))
                chain.sync()
                for t in range(B):
                    chain.step(dve.match_replace(kept[:, t, 0:e + fill], top8[:, t, :], sc[:, t, 0:e + fill], 0.0))
                chain.sync()
                chain.step(dve.tensor_tensor(tokw[:, :, 0:e], sc[:, :, 0:e], kept[:, :, 0:e], ALU.subtract))
                chain.sync()
                if k == 1:
                    chain.step(dve.tensor_reduce(rmax[:], tokw[:, :, 0:e], AX_X, ALU.add))
                    chain.sync()
                    chain.step(dve.reciprocal(rmax[:], rmax[:]))
                    chain.sync()
                    chain.step(dve.tensor_tensor(tokw[:, :, 0:e], tokw[:, :, 0:e],
                                                 rmax[:].unsqueeze(2).to_broadcast([P, B, e]), ALU.mult))
                    chain.sync()
                left = tokw[:, :, 0:e]
                for part in range(PARTS):
                    cols = wparts[:, :, E0 * part:E0 * part + e]
                    ins = dve.tensor_copy(cols, left)
                    if part == PARTS - 1:
                        ins.then_inc(s["wp"], 1)
                        break
                    chain.step(ins)
                    chain.sync()
                    chain.step(dve.tensor_tensor(tokr[:, part, :, 0:e], left, cols, ALU.subtract))
                    chain.sync()
                    left = tokr[:, part, :, 0:e]

            def ffn_residual(s):
                for h in range(2):
                    dve.wait_ge(s["tr"], h + 1)
                    half = resid[:, HB * h:HB * (h + 1), :]
                    dve.tensor_tensor(half, half, ps[:, h, :].rearrange("p (b d) -> p b d", b=HB),
                                      ALU.add).then_inc(s["res"], 1)
                dve.wait_ge(s["res"], 2)

            if STAGES > 1:
                s = ffn[0]
                ffn_prelude(s, 0)

                def clamp0(e, h):
                    at = bass.ds(e, 1)
                    dve.wait_ge(s["gu"], (e * 2 + h) * 2 + 1)
                    dve.tensor_scalar(gate_a[:, h, :], ps[:, h, :], biases[:, 0, at], LIMIT, ALU.add,
                                      ALU.min).then_inc(s["ga"], 1)
                    dve.wait_ge(s["gu"], (e * 2 + h) * 2 + 2)
                    dve.tensor_scalar(up_a[:, h, :], ps[:, 2 + h, :], up_b[:, at], LIMIT + 1.0, ALU.add,
                                      ALU.min).then_inc(s["ua"], 1)

                def activate0(e, h):
                    dve.wait_ge(s["glw"], e * 2 + h + 1)
                    dve.wait_ge(s["ua"], e * 2 + h + 1)
                    dve.scalar_tensor_tensor(act_f[:, h, :], up_a[:, h, :], 1.0 - LIMIT, glw[:, h, :], ALU.max,
                                             ALU.mult).then_inc(s["act"], 1)

                def expert0(e, last):
                    clamp0(e, 1)
                    activate0(e, 0)
                    if not last:
                        clamp0(e + 1, 0)
                    activate0(e, 1)

                clamp0(0, 0)
                with dve.Fori(0, E0 // 2 - 1) as i:
                    for slot in range(2):
                        expert0(i * 2 + slot, False)
                for slot in range(2):
                    expert0(E0 - 2 + slot, slot == 1)
                ffn_residual(s)
            if STAGES > 2:
                with dve.Fori(0, HALVES) as i:
                    s = a1
                    chain = Chain(dve, s["chain"], i * A1_CHAIN, A1_CHAIN)

                    def tile_of_half(b):
                        return resid[:, bass.ds(i * HB + b, 1), :].rearrange("p o d -> p (o d)")

                    layer_norm_stats(dve, s, tile_of_half, HB, chain, "var")
                    normalised(s, chain, tile_of_half, HB, "std", i + 1, "norm")
                    split_half(s, i)
                    for n in range(2 * G):
                        stack_piece(s, i * (2 * G), 2, n, i * 128, False)
                    by_head = ps[:].rearrange("p k (j q) -> p q (k j)", j=GH)

                    def head_max(b):
                        dve.wait_ge(s["st"], i * HB + b + 1)
                        dve.tensor_reduce(hmax[:, b % 2, :], by_head[:, :, H * (b % 2):H * (b % 2) + H], AX_X,
                                          ALU.max).then_inc(s["max"], 1)

                    head_max(0)
                    head_max(1)
                    for b in range(HB):
                        dve.wait_ge(s["sum"], i * HB + b + 1)
                        dve.reciprocal(hrec[:, b % 2, :], hsum[:, b % 2, 0, :]).then_inc(s["rec"], 1)
                        dve.wait_ge(s["rec"], i * HB + b + 1)
                        dve.tensor_tensor(hprobs[:, b % 2], hprobs[:, b % 2],
                                          hrec[:, b % 2, :].unsqueeze(1).to_broadcast([P, H, P]),
                                          ALU.mult).then_inc(s["wts"], 1)
                        dve.wait_ge(s["wo"], i * HB + b + 1)
                        tile = tile_of_half(b)
                        dve.tensor_tensor(tile, tile, ps[:, 4 * (b % 2) + 1, 0:D], ALU.add).then_inc(s["res"], 1)
                        if b + 2 < HB:
                            head_max(b + 2)
                    dve.wait_ge(s["res"], i * HB + HB)
                    chain.close()
            if STAGES > 3:
                s = ffn[1]
                ffn_prelude(s, 1)

                def activate1(e, h, c, m, routed):
                    n = h * 3 + c
                    left = glw if routed else glu
                    dve.wait_ge(s["gu"], (e * 6 + n) * 2 + 2)
                    dve.wait_ge(s["glw" if routed else "glu"], e * 6 + n + 1)
                    dve.tensor_tensor(act_f[0:m, n % 2, :], left[0:m, n % 2, :], ps[0:m, 2 + n % 2, :],
                                      ALU.mult).then_inc(s["act"], 1)

                def expert1(e, routed):
                    for h in range(2):
                        for c, (_, m) in enumerate(CH1):
                            activate1(e, h, c, m, routed)

                with dve.Fori(0, E1 // 2) as i:
                    for slot in range(2):
                        expert1(i * 2 + slot, True)
                expert1(E1, False)
                ffn_residual(s)

        @block.tensor
        def _(pe):
            def mm(dst, lhs, rhs, start=True, stop=True):
                return pe.matmul(dst, lhs, rhs, start=start, stop=stop, skip_group_check=True)

            def three_pass(dst, lhs_hi, lhs_lo, rhs_hi, rhs_lo):
                mm(dst, lhs_hi, rhs_hi, True, False)
                mm(dst, lhs_hi, rhs_lo, False, False)
                return mm(dst, lhs_lo, rhs_hi, False, True)

            pe.wait_ge(loaded, LOADED)
            pe.wait_ge(ready["split"], 1)
            pe.wait_ge(ready["zeroed"], 1)

            def turn(s, count, base, src, n, bank, done):
                for b in range(n):
                    pe.wait_ge(s[count], base + b + 1)
                    ins = pe.transpose(ps[:, bank + b // 4, (b % 4) * P:(b % 4 + 1) * P], src[:, b, :], ident)
                ins.then_inc(s[done], 1)

            def values(s, wv, c, src):
                for b in range(HB):
                    ins = mm(ps[:, 1 + c, b * P:(b + 1) * P], src[:, b * P:(b + 1) * P], wv)
                ins.then_inc(s["v"], 1)

            def project_piece(s, layer, base, per_group, n):
                g, kind = divmod(n, per_group)
                if n >= 2:
                    pe.wait_ge(s["stk"], base + n - 1)
                which, hi, lo = (0, x_hi[:, 0:HT], x_lo[:, 0:HT]) if kind == 0 else \
                    (1, c_hi[:], c_lo[:]) if kind == 1 else (1, x_hi[:, 0:HT], x_lo[:, 0:HT])
                cols = slice(g * P, (g + 1) * P)
                three_pass(ps[:, n % 2, :], qk_hi[:, 2 * layer + which, cols], qk_lo[:, 2 * layer + which, cols],
                           hi, lo).then_inc(s["proj"], 1)

            with pe.Fori(0, HALVES) as i:
                s = a0
                turn(s, "norm", i * HB, xn, HB, 0, "xt")
                pe.wait_ge(s["ctxc"], i * 2 + 2)
                values(s, w["wv0"], 0, c_f)
                pe.wait_ge(s["xc"], i * 2 + 2)
                values(s, w["wv0"], 1, x_f)
                pe.wait_ge(s["lo"], i * 2 + 2)
                pe.wait_ge(s["vcopy"], i * 2 + 2)
                project_piece(s, 0, i * 12, 3, 0)
                project_piece(s, 0, i * 12, 3, 1)
                pe.wait_ge(s["first"], i + 1)
                mm(ps[:, 3, :], one_row, first_v[:].rearrange("p b h d -> p (b h d)")).then_inc(s["firstp"], 1)
                project_piece(s, 0, i * 12, 3, 2)
                pe.wait_ge(s["firstb"], i + 1)

                def scores_by_query(n):
                    g, b = divmod(n, HB)
                    if b == 0:
                        pe.wait_ge(s["stk"], i * 12 + 3 * g + 3)
                        pe.wait_ge(s[f"blk{g % 2}"], i * 128 + 64 * (g // 2 + 1))
                    for u in range(2):
                        if n >= 1:
                            pe.wait_ge(s["max"], i * 32 + 2 * (n - 1) + u + 1)
                        for j in (2 * u, 2 * u + 1):
                            ins = mm(ps[:, 2 + u, (j % 2) * KEYS:(j % 2 + 1) * KEYS],
                                     q_blk[:, g, j, b * P:(b + 1) * P], k_st[:, g, b, :])
                        ins.then_inc(s["qk"], 1)

                def scores_by_key(n):
                    g, b = divmod(n, HB)
                    for c in range(2):
                        if n >= 1:
                            pe.wait_ge(s["exp"], i * 32 + 2 * (n - 1) + c + 1)
                        mm(ps[:, 4 + c, :].rearrange("p (j q) -> p j q", j=GH), k_st[:, g, b, c * P:(c + 1) * P],
                           q_blk[:, g, :, b * P:(b + 1) * P], True, False)
                        if c == 0:
                            pe.wait_ge(s["shift"], i * 16 + n + 1)
                        mm(ps[:, 4 + c, :].rearrange("p (j q) -> p j q", j=GH), (ones_but0, ones)[c][:],
                           shift[:, n % SH], False, True).then_inc(s["st"], 1)

                def weigh_values(n):
                    g, b = divmod(n, HB)
                    if b == 0 and g >= 2:
                        pe.wait_ge(s["ot"], i * G + g - 1)
                    for c in range(2):
                        pe.wait_ge(s["exp"], i * 32 + 2 * n + c + 1)
                        for j in range(GH):
                            ins = mm(ps[SLOT * j:SLOT * (j + 1), 6 + g % 2, b * P:(b + 1) * P],
                                     vals[:, c, b, GH * g + j, :], probs[:, n % 2, c, j * P:(j + 1) * P],
                                     c == 0, c == 1)
                    ins.then_inc(s["pv"], 1)

                scores_by_query(0)
                scores_by_query(1)
                for n in range(G * HB):
                    g, b = divmod(n, HB)
                    if n + 2 < G * HB:
                        scores_by_query(n + 2)
                    scores_by_key(n)
                    for piece in pieces_at(n):
                        project_piece(s, 0, i * 12, 3, piece)
                    if n >= 1:
                        weigh_values(n - 1)
                weigh_values(G * HB - 1)
                pe.wait_ge(s["ot"], i * G + G)
                pe.wait_ge(s["max"], i * 32 + 32)
                for b in range(HB):
                    for g in range(G):
                        ins = mm(ps[:, 2 + b, 0:OUTW], heads_t[:, g, b * P:(b + 1) * P], gather[:, g, :],
                                 g == 0, g == G - 1)
                    ins.then_inc(s["gat"], 1)
                turn(s, "norm2", i * HB, xn, HB, 6, "t2")
                pe.wait_ge(s["aff"], i + 1)
                for b in range(HB):
                    mm(ps[:, 7, b * P:(b + 1) * P], ln_t[:, b * P:(b + 1) * P], w["wp0"], True, False)
                    ins = mm(ps[:, 7, b * P:(b + 1) * P], one_row, row[:, R_BP:R_BP + D], False, True)
                ins.then_inc(s["wp"], 1)

            def ffn_prelude(s, k):
                e = (E0, E1)[k]
                turn(s, "norm", 0, xn, B, 0, "xt")
                pe.wait_ge(s["xc"], 2)
                for t in range(B):
                    dst = ps[:, 2, t * e:(t + 1) * e]
                    ins = mm(dst, x_f[:, t * P:(t + 1) * P], w[("rw0", "gw1")[k]], True, k == 1)
                    if k == 0:
                        ins = mm(dst, one_row, row[:, R_RB:R_RB + e], False, True)
                ins.then_inc(s["logit"], 1)
                pe.wait_ge(s["wp"], 1)
                for t in range(B):
                    ins = mm(ps[:, 3 + t // 4, (t % 4) * P:(t % 4 + 1) * P], wparts[:, t, :], idb[:])
                ins.then_inc(s["wt"], 1)
                pe.wait_ge(s["wtc"], 2 - k)
                for h in range(2):
                    if k == 0:
                        mm(ps[:, 6 + h, :], db0[:], wt_f[:, h * 512:(h + 1) * 512], True, False)
                    else:
                        mm(ps[:, 6 + h, :], zero_r[:, 0:P], zero_r[:], True, False)
                pe.wait_ge(s["lo"], 1)

            def gate_up(s, hi, lo, slot, gate, up, m, width, h, bank):
                tokens = slice(h * 512, (h + 1) * 512)
                for at, b0 in ((gate, 0), (up, 2)):
                    cols = slice(at, at + m)
                    three_pass(ps[0:m, b0 + bank, :], hi[:, slot, cols], lo[:, slot, cols], x_hi[:, tokens],
                               x_lo[:, tokens]).then_inc(s["gu"], 1)

            def spread_weights(s, e, h):
                mm(ps[:, 4 + h, :], psel[:, bass.ds(e, 1), :].rearrange("p o m -> p (o m)"),
                   wt_bf[:, h * 512:(h + 1) * 512]).then_inc(s["wb"], 1)

            def ffn_end(s):
                for h in range(2):
                    pe.wait_ge(s["acc"], h + 1)
                    for b in range(4):
                        ins = pe.transpose(ps[:, h, b * P:(b + 1) * P],
                                           acc_sb[:, (4 * h + b) * P:(4 * h + b + 1) * P], ident)
                    ins.then_inc(s["tr"], 1)

            if STAGES > 1:
                s = ffn[0]
                ffn_prelude(s, 0)

                def gates0(e, slot, h):
                    if h == 0:
                        pe.wait_ge(s["wlo"], e + 1)
                    gate_up(s, exp_hi, exp_lo, slot, 0, F0, F0, F0, h, h)
                    spread_weights(s, e, h)

                def down0(e, i, slot, h, final):
                    if h == 0:
                        pe.wait_ge(s[f"ddma{slot}"], i * 16 + 16)
                    pe.wait_ge(s["act"], e * 2 + h + 1)
                    ins = mm(ps[:, 6 + h, :], exp_d[:, slot, 0:D], act_f[:, h, :], False, final)
                    if final:
                        ins.then_inc(s["down"], 1)
                    elif h == 1:
                        ins.then_inc(s["wfree"], 1)
                    return ins

                def expert0(i, slot, last):
                    e = i * 2 + slot
                    gates0(e, slot, 1)
                    down0(e, i, slot, 0, last)
                    if not last:
                        gates0(e + 1, 1 - slot, 0)
                    down0(e, i, slot, 1, last)

                gates0(0, 0, 0)
                with pe.Fori(0, E0 // 2 - 1) as i:
                    for slot in range(2):
                        expert0(i, slot, False)
                for slot in range(2):
                    expert0(E0 // 2 - 1, slot, slot == 1)
                ffn_end(s)
            if STAGES > 2:
                with pe.Fori(0, HALVES) as i:
                    s = a1
                    turn(s, "norm", i * HB, xn, HB, 0, "xt")
                    pe.wait_ge(s["ctxc"], i * 2 + 2)
                    values(s, w["wv1"], 0, c_f)
                    pe.wait_ge(s["vcopy"], i + 1)
                    pe.wait_ge(s["lo"], i * 2 + 2)
                    for n in range(2 * G):
                        project_piece(s, 1, i * (2 * G), 2, n)

                    def head_scores(b):
                        if b >= 2:
                            pe.wait_ge(s["res"], i * HB + b - 1)
                        for g in range(G):
                            if b == 0:
                                pe.wait_ge(s[f"blk{g % 2}"], i * 128 + 64 * (g // 2 + 1))
                            ins = mm(ps[:, 4 * (b % 2) + g, :].rearrange("p (j q) -> p j q", j=GH),
                                     k_st[:, g, b, 0:P], q_blk[:, g, :, b * P:(b + 1) * P], True, False)
                        ins.then_inc(s["st"], 1)

                    def less_max(b):
                        pe.wait_ge(s["max"], i * HB + b + 1)
                        for g in range(G):
                            ins = mm(ps[:, 4 * (b % 2) + g, :].rearrange("p (j q) -> p j q", j=GH), negid[:],
                                     hmax[:, b % 2, :].unsqueeze(1).to_broadcast([P, GH, P]), False, True)
                        ins.then_inc(s["nm"], 1)

                    pe.wait_ge(s["stk"], i * (2 * G) + 2 * G)
                    head_scores(0)
                    head_scores(1)
                    less_max(0)
                    less_max(1)
                    for b in range(HB):
                        pe.wait_ge(s["wts"], i * HB + b + 1)
                        for g in range(G):
                            for j in range(GH):
                                ins = mm(ps[SLOT * j:SLOT * (j + 1), 4 * (b % 2), g * P:(g + 1) * P],
                                         vals[:, 0, b, GH * g + j, :], hprobs[:, b % 2, GH * g + j, :])
                        ins.then_inc(s["pv"], 1)
                        pe.wait_ge(s["ot"], i * HB + b + 1)
                        for g in range(G):
                            ins = mm(ps[:, 4 * (b % 2) + 1, 0:D], heads1[:, b % 2, g, :], wo1[:, g, :],
                                     g == 0, g == G - 1)
                        ins.then_inc(s["wo"], 1)
                        if b + 2 < HB:
                            head_scores(b + 2)
                            less_max(b + 2)
            if STAGES > 3:
                s = ffn[1]
                ffn_prelude(s, 1)

                def gates1(e, slot, n):
                    h, c = divmod(n, 3)
                    at, m = CH1[c]
                    if n == 0:
                        pe.wait_ge(s["wlo"], e + 1)
                    gate_up(s, exp_hi, exp_lo, slot, at, F1 + at, m, F1, h, n % 2)

                def down1(e, i, slot, n, final):
                    h, c = divmod(n, 3)
                    if n == 0:
                        pe.wait_ge(s[f"ddma{slot}"], i * 16 + 16)
                    m = CH1[c][1]
                    pe.wait_ge(s["act"], e * 6 + n + 1)
                    ins = mm(ps[:, 6 + h, :], exp_d[0:m, slot, c * D:(c + 1) * D],
                             act_f[0:m, n % 2, :], False, final and c == 2)
                    if final and c == 2:
                        ins.then_inc(s["down"], 1)
                    elif n == 5:
                        ins.then_inc(s["wfree"], 1)

                def expert1(i, slot, last):
                    e = i * 2 + slot
                    for n in range(6):
                        if n < 5:
                            gates1(e, slot, n + 1)
                            if n + 1 == 3 and not last:
                                spread_weights(s, e, 1)
                        elif not last:
                            gates1(e + 1, 1 - slot, 0)
                            if not (isinstance(e, int) and e == E1 - 1):
                                spread_weights(s, e + 1, 0)
                        down1(e, i, slot, n, last)

                gates1(0, 0, 0)
                spread_weights(s, 0, 0)
                with pe.Fori(0, E1 // 2 - 1) as i:
                    for slot in range(2):
                        expert1(i, slot, False)
                for slot in range(2):
                    expert1(E1 // 2 - 1, slot, False)
                expert1(E1 // 2, 0, True)
                ffn_end(s)


def _head_slots(wt, lanes):
    a = np.zeros((D, H, GH, HD), wt.dtype)
    a[:, :, :3, :] = wt.T.reshape(D, H, 1, HD)
    return a.reshape(D, G * P)


def kernel(**inputs):
    import concourse.bacc as bacc
    from concourse.bass_utils import run_bass_kernel_spmd

    a = {n: np.asarray(v) for n, v in inputs.items()}
    f32 = np.float32
    bf16 = mybir.dt.np(BF16)
    consts = np.zeros((P, C_END), f32)
    consts[:, C_ID:C_ID + P] = np.eye(P)
    consts[:, C_NEG:C_NEG + P] = -np.eye(P)
    lane = np.arange(P) % SLOT // HD
    consts[:, C_QSEL] = np.where(lane == 1, -1.0, 0.0)
    consts[:, C_KSEL] = np.where(lane == 2, -1.0, 0.0)
    consts[0, C_ONE:C_ONE + P] = 1.0
    gather = np.zeros((P, G, OUTW), f32)
    for h in range(H):
        g, j = divmod(h, GH)
        for d in range(HD):
            gather[SLOT * j + d, g, h * HD + d] = 1.0
        gather[SLOT * j + HD, g, D + h] = 1.0
    consts[:, C_GATHER:] = gather.reshape(P, G * OUTW)
    part_sel = np.zeros((P, E0, P), bf16)
    for part in range(PARTS):
        for e in range(E0):
            part_sel[E0 * part + e, e, :] = 1.0
    qk = np.stack([_head_slots(a[n], 0) for n in ("L0_xattn_Wq", "L0_xattn_Wk", "L1_xattn_Wq", "L1_xattn_Wk")], 1)
    small = np.zeros((P, W_END), f32)
    for n, v in (("wv0", a["L0_xattn_Wv"].T), ("wp0", a["L0_xattn_Wp"].T), ("wv1", a["L1_xattn_Wv"].T),
                 ("rw0", a["L0_ffn_router_weight"].T), ("gw1", a["L1_ffn_gate_w"])):
        small[:, W_AT[n]:W_AT[n] + W_WIDTH[n]] = v
    small[:, W_LN], small[:, W_LN + 1] = a["L0_xattn_ln_g"], a["L0_xattn_ln_b"]
    wo = np.zeros((GH, SLOT, G, D), f32)
    wo[:, :HD] = a["L1_xattn_Wo"].T.reshape(G, GH, HD, D).transpose(1, 2, 0, 3)
    small[:, W_WO:] = wo.reshape(P, G * D)
    rows = np.concatenate([a["L0_xattn_gate"].reshape(-1), a["L0_xattn_bp"], a["L0_ffn_router_bias"]])[None, :]
    down_bias = np.zeros((P, D), f32)
    for part in range(PARTS):
        down_bias[E0 * part:E0 * (part + 1)] = a["L0_ffn_down_bias"]
    gu_bias = a["L0_ffn_gate_up_bias"].reshape(E0, 2, F0).transpose(2, 1, 0)
    experts0 = np.concatenate([a["L0_ffn_gate_up_proj"], a["L0_ffn_down_proj"]], 2)
    wgu = np.concatenate([a["L1_ffn_exp_wgu"], a["L1_ffn_base_wgu"][None]], 0)
    wd = np.zeros((E1 + 1, 3 * P, D), f32)
    wd[:, :F1] = np.concatenate([a["L1_ffn_exp_wd"], a["L1_ffn_base_wd"][None]], 0)
    experts1 = np.concatenate([wgu, wd.reshape(E1 + 1, 3, P, D).transpose(0, 2, 1, 3).reshape(E1 + 1, P, 3 * D)], 2)
    arrays = {
        "x": a["x"], "ctx_t": a["ctx_1024"].transpose(2, 0, 1).reshape(D, T), "qk_w": qk, "small_w": small,
        "consts": consts, "rows": rows, "down_bias": down_bias, "gu_bias": gu_bias, "part_sel": part_sel,
        "ident_bf": np.eye(P).astype(bf16), "experts0": experts0, "experts1": experts1,
    }
    arrays = {n + "_dram": np.ascontiguousarray(v) for n, v in arrays.items()}
    nc = bacc.Bacc("TRN2", target_bir_lowering=False, num_devices=1)
    args = [nc.dram_tensor(n, v.shape, mybir.dt.from_np(v.dtype), kind="ExternalInput").ap()
            for n, v in arrays.items()]
    out = nc.dram_tensor("out_dram", (B, P, D), F32, kind="ExternalOutput").ap()
    two_layers(nc, *args, out)
    r = run_bass_kernel_spmd(nc, [arrays], core_ids=[0])
    return r.results[0]["out_dram"]
```

```python
from contextlib import ExitStack

import concourse.bass as bass
import numpy as np
from concourse import mybir

F32 = mybir.dt.float32
F32R = mybir.dt.float32r
BF16 = mybir.dt.bfloat16
ALU = mybir.AluOpType
ACT = mybir.ActivationFunctionType
AX_X = mybir.AxisListType.X

P = 128
B = 8
D = 128
H = 16
HD = D // H
GH = 4
G = H // GH
SLOT = P // GH
HB = 4
HALVES = B // HB
HT = HB * P
T = B * P
KEYS = 2 * P
LN_EPS = 1e-5
SCALE = float(HD) ** -0.5
E0, TOP0 = 16, 4
F0 = 128
ALPHA, LIMIT = 1.702, 7.0
E1, TOP1 = 8, 2
F1 = 352
CH1 = [(0, 128), (128, 128), (256, 96)]
PARTS = 3
OUTW = D + H

SH = 3
UQ = P // 2
UNITS = B * P // UQ
POOL_HEADS = 4
STAGES = 4
A0_CHAIN = 24

C_ID, C_NEG, C_QSEL, C_KSEL, C_ONE, C_GATHER = 0, 128, 256, 257, 258, 258 + P
C_END = C_GATHER + G * OUTW
W_NAMES = ["wv0", "wp0", "wv1", "rw0", "gw1"]
W_WIDTH = {"wv0": D, "wp0": D, "wv1": D, "rw0": E0, "gw1": E1}
W_AT, _at = {}, 0
for _n in W_NAMES:
    W_AT[_n] = _at
    _at += W_WIDTH[_n]
W_LN = _at
W_WO = _at + 2
W_END = W_WO + G * D
R_GATE, R_BP, R_RB, R_END = 0, H, H + D, H + D + E0


def two_layers(nc, x, ctx_t, qk_w, small_w, consts, rows, down_bias, gu_bias, part_sel, ident_bf, experts0, experts1, out):
    with ExitStack() as ctx:
        def sb(name, shape, dt=F32):
            return ctx.enter_context(nc.sbuf_tensor(name, shape, dt))

        def sem(name):
            return ctx.enter_context(nc.semaphore(name))

        ps = ctx.enter_context(nc.psum_tensor("ps", [P, 8, 512], F32))
        resid = sb("resid", [P, B, D])
        ctx_sb = sb("ctx_sb", [P, T])
        qk_hi = sb("qk_hi", [P, 4, G * P], F32R)
        qk_lo = sb("qk_lo", [P, 4, G * P], F32R)
        small = sb("small", [P, W_END])
        cst = sb("cst", [P, C_END])
        row = sb("row", [1, R_END])
        negid = sb("negid", [P, P], F32R)
        ones = sb("ones", [P, P], F32R)
        ones_but0 = sb("ones_but0", [P, P], F32R)
        zero_r = sb("zero_r", [P, P], F32R)
        tanh_gate = sb("tanh_gate", [1, H])
        db0 = sb("db0", [P, D])
        psel = sb("psel", [P, E0, P], BF16)
        idb = sb("idb", [P, P], BF16)
        xn = sb("xn", [P, B, D])
        stats = sb("stats", [P, B, 6])
        mv = sb("mv", [P, B, 3])
        rvar = sb("rvar", [P, B])
        rstd = sb("rstd", [P, B])
        x_f = sb("x_f", [P, T])
        x_hi = sb("x_hi", [P, T], F32R)
        x_lo = sb("x_lo", [P, T], F32R)
        c_f = sb("c_f", [P, HT])
        c_hi = sb("c_hi", [P, HT], F32R)
        c_lo = sb("c_lo", [P, HT], F32R)
        vals = sb("vals", [P, 2, HB, H, SLOT])
        first_v = sb("first_v", [1, HB, H, HD])
        first_b = sb("first_b", [P, HB, D])
        rnd = sb("rnd", [P, 2, 512], F32R)
        q_st = sb("q_st", [P, G, HT], F32R)
        q_blk = sb("q_blk", [P, G, GH, HT], F32R)
        k_st = sb("k_st", [P, G, HB, KEYS], F32R)
        neg_max = sb("neg_max", [P, SH, GH])
        shift = sb("shift", [P, SH, GH, P], F32R)
        rsum = sb("rsum", [P, HB, H])
        attn = sb("attn", [P, HB, H, HD])
        attn_bf = sb("attn_bf", [P, HB, D], BF16)
        ln_t = attn[:].rearrange("p b h d -> p (b h d)")
        hmax = sb("hmax", [P, 2, UQ], F32R)
        hrec = sb("hrec", [P, 2, UQ])
        heads1 = sb("heads1", [P, G, P])
        logit = sb("logit", [P, B, E0])
        top8 = sb("top8", [P, B, 8])
        rmax = sb("rmax", [P, B])
        score = [sb(f"score{k}", [P, B, E0 + 8]) for k in range(2)]
        kept = sb("kept", [P, B, E0 + 8])
        tokw = sb("tokw", [P, B, E0])
        tokr = sb("tokr", [P, 2, B, E0])
        wparts = sb("wparts", [P, B, P], BF16)
        wt_bf = sb("wt_bf", [P, T], BF16)
        exp_f = sb("exp_f", [P, 2, 2 * F1])
        exp_d = sb("exp_d", [P, 2, 3 * D])
        exp_hi = sb("exp_hi", [P, 2, 2 * F1], F32R)
        exp_lo = sb("exp_lo", [P, 2, 2 * F1], F32R)
        biases = sb("biases", [P, 2, E0])
        up_b = sb("up_b", [P, E0])

        k1 = k_st[:].rearrange("p g b k -> p g (b k)")
        room = sb("room", [P, 6, 1024])
        flat = room[:].rearrange("p a n -> p (a n)")
        qk_f = flat[:, 0:2048].rearrange("p (w n) -> p w n", w=4)
        probs = flat[:, 0:2048].rearrange("p (s c n) -> p s c n", s=2, c=2)
        heads_t = flat[:, 2048:4096].rearrange("p (g n) -> p g n", g=G)
        hprobs = flat[:, 0:3072].rearrange("p (s h q) -> p s h q", s=3, h=H)
        hsum = flat[:, 3072:4096].rearrange("p (s h q) -> p s h q", s=2, h=H // 2)
        gate_a, up_a = (room[:, n, :].rearrange("p (s n) -> p s n", s=2) for n in (2, 5))
        wbc = room[:, 0:2, :].rearrange("p a (s n) -> p (a s) n", s=2)
        act_f = room[:, 3:5, :].rearrange("p a (s n) -> p (a s) n", s=2)
        wt_f = room[:, 5, :]
        glu1 = room[:, 1:3, :].rearrange("p a (s n) -> p (a s) n", s=2)
        acc_sb = x_f

        ident = cst[:, C_ID:C_ID + P]
        qsel, ksel = cst[:, C_QSEL:C_QSEL + 1], cst[:, C_KSEL:C_KSEL + 1]
        one_row = cst[0:1, C_ONE:C_ONE + P]
        gather = cst[:, C_GATHER:C_END].rearrange("p (g n) -> p g n", g=G)
        w = {n: small[:, W_AT[n]:W_AT[n] + W_WIDTH[n]] for n in W_NAMES}
        ln_g, ln_b = small[:, W_LN:W_LN + 1], small[:, W_LN + 1:W_LN + 2]
        wo1 = small[:, W_WO:W_END].rearrange("p (g n) -> p g n", g=G)

        def sems(prefix, names):
            return {n: sem(prefix + n) for n in names.split()}

        loaded = sem("loaded")
        stored = sem("stored")
        ready = sems("ready_", "zeroed ones tanh split qk_hi")
        a0 = sems("a0_", "var std norm xt ctxc xc lo v vcopy first firstp firstb proj rnd stk blk0 blk1 qk max shift st "
                         "exp pv ot gat attn var2 std2 norm2 t2 aff wp res chain")
        a1 = sems("a1_", "var std norm xt xc xlo ctxc clo v vcopy proj rnd stk blk0 blk1 blk2 blk3 st max nm exp pairs fours sum "
                         "rec wtd wtp pv ot wo res chain")
        ffn = [sems(f"f{k}_", "var std norm xt xc lo logit lmax e tokw wp wt wtc wdma0 wdma1 ddma0 ddma1 wfree whi wlo gu wb wbc "
                              "ga ua glu glw act down acc tr res chain") for k in range(2)]

        def layer_norm_stats(dve, s, src, n, chain, var):
            even, odd = stats[:, 0:n, 1:3], stats[:, 0:n, 4:6]
            for b in range(n):
                chain.step(dve.bn_stats(stats[:, b, :], src(b)))
            chain.sync()
            chain.step(dve.tensor_tensor(mv[:, 0:n, 0:2], even, odd, ALU.add))
            chain.step(dve.tensor_tensor(mv[:, 0:n, 2], even[:, :, 0], odd[:, :, 0], ALU.subtract))
            chain.sync()
            chain.step(dve.tensor_scalar(mv[:, 0:n, 1], mv[:, 0:n, 1], 1.0 / D, LN_EPS, ALU.mult, ALU.add))
            chain.step(dve.scalar_tensor_tensor(mv[:, 0:n, 2], mv[:, 0:n, 2], 0.25, mv[:, 0:n, 2], ALU.mult,
                                                ALU.mult))
            chain.step(dve.tensor_scalar(mv[:, 0:n, 0], mv[:, 0:n, 0], 0.5, None, ALU.mult))
            chain.sync()
            chain.step(dve.tensor_tensor(rvar[:, 0:n], mv[:, 0:n, 1], mv[:, 0:n, 2], ALU.add))
            chain.sync()
            dve.reciprocal(rvar[:, 0:n], rvar[:, 0:n]).then_inc(s[var], 1)

        class Chain:

            def __init__(self, eng, counter, base=0, per=None):
                self.eng, self.counter, self.base, self.per, self.n = eng, counter, base, per, 0

            def step(self, ins):
                self.n += 1
                ins.then_inc(self.counter, 1)

            def sync(self):
                self.eng.wait_ge(self.counter, self.base + self.n)

            def close(self):
                assert self.n == self.per, (self.n, self.per)

        block = ctx.enter_context(nc.Block())

        def pieces_at(n):
            g, b = divmod(n, HB)
            return [] if g + 1 == G or b > 1 else [3 * (g + 1) + 2] if b else [3 * (g + 1), 3 * (g + 1) + 1]

        PIECES1 = [(what, half, g) for what, half in (("k", 1), ("q", 0), ("k", 0), ("q", 1)) for g in range(G)]

        BLOCKS1 = [(0, 1), (1, HB - 1)] + [(b, 1) for b in range(HB, B)]

        def bank1(n):
            return (6, 7, 0, 1)[n % 4] if n < 3 * G else 6 + n % 2

        def fetch_expert(sp, k, src, slot, what="both"):
            width, d_width = ((2 * F0, D), (2 * F1, 3 * D))[k]
            if what != "down":
                sp.dma_start(exp_f[:, slot, 0:width], src[:, 0:width]).then_inc(ffn[k][f"wdma{slot}"], 16)
            if what != "gate_up":
                sp.dma_start(exp_d[:, slot, 0:d_width],
                             src[:, width:width + d_width]).then_inc(ffn[k][f"ddma{slot}"], 16)

        @block.sync
        def _(sp):
            for dst, src in ((resid[:], x.rearrange("b t d -> t b d")), (cst[:], consts), (qk_f, qk_w),
                             (ctx_sb[:], ctx_t), (small[:], small_w), (row[:], rows), (db0[:], down_bias), (biases[:], gu_bias),
                             (psel[:], part_sel), (idb[:], ident_bf)):
                sp.dma_start(dst, src).then_inc(loaded, 16)
            for e in range(2):
                fetch_expert(sp, 0, experts0[e], e)

            def block_queries(s, stk0, per_group):
                for g in range(G):
                    sp.wait_ge(s["stk"], stk0 + per_group * g + 1)
                    for j in range(GH):
                        rows_j = slice(SLOT * j, SLOT * (j + 1))
                        sp.dma_start(q_blk[rows_j, g, j, :].bitcast(F32),
                                     q_st[rows_j, g % 2, :].bitcast(F32)).then_inc(s[f"blk{g % 2}"], 16)

            def fetch_experts(k, experts, n):
                s = ffn[k]

                def gate_up(e, slot, src):
                    sp.wait_ge(s["wlo"], e - 1)
                    fetch_expert(sp, k, src, slot, "gate_up")

                def down(e, slot, src):
                    sp.wait_ge(s["wfree"], e - 1)
                    fetch_expert(sp, k, src, slot, "down")

                def source(at):
                    return experts[bass.ds(at, 1)].rearrange("e p n -> p (e n)")

                for e in (2, 3):
                    gate_up(e, e % 2, experts[e])
                turns = (n - 4) // 2
                with sp.Fori(0, turns) as i:
                    for slot in range(2):
                        down(i * 2 + slot + 2, slot, source(i * 2 + slot + 2))
                        gate_up(i * 2 + slot + 4, slot, source(i * 2 + slot + 4))
                for e in range(2 * turns + 2, n):
                    down(e, e % 2, experts[e])
                    if e + 2 < n:
                        gate_up(e + 2, e % 2, experts[e + 2])

            sp.wait_ge(ready["zeroed"], 1)
            with sp.Fori(0, HALVES) as i:
                block_queries(a0, i * (3 * G), 3)
            if STAGES > 1:
                fetch_experts(0, experts0, E0)
            if STAGES > 2:
                for first, n in BLOCKS1:
                    sp.wait_ge(a1["stk"], (2 if first < HB else 4) * G)
                    if first >= HB:
                        sp.wait_ge(a1["st"], 2 * (first - HB) + 2)
                    b = first % HB
                    cols = slice(b * P, (b + n) * P)
                    for j in range(GH):
                        rows_j = slice(SLOT * j, SLOT * (j + 1))
                        sp.dma_start(q_blk[rows_j, :, j, cols].bitcast(F32),
                                     q_st[rows_j, :, cols].bitcast(F32)).then_inc(a1[f"blk{b}"], 16)
            if STAGES > 3:
                for e in range(2):
                    sp.wait_ge(ffn[0]["down"], 2)
                    fetch_expert(sp, 1, experts1[e], e)
                fetch_experts(1, experts1, E1 + 1)
            last = [a0["res"], ffn[0]["res"], a1["res"], ffn[1]["res"]][STAGES - 1]
            per = [1, 1, 4, 1][STAGES - 1]
            for h in range(2):
                sp.wait_ge(last, per * (h + 1))
                sp.dma_start(out.rearrange("b t d -> t b d")[:, HB * h:HB * (h + 1), :],
                             resid[:, HB * h:HB * (h + 1), :]).then_inc(stored, 16)
            sp.wait_ge(stored, 32)

        LOADED = 16 * 10

        @block.gpsimd
        def _(pool):
            pool.memset(zero_r[:].bitcast(F32), 0.0)
            pool.memset(wparts[:], 0.0)
            pool.memset(ones[:].bitcast(F32), 1.0).then_inc(ready["ones"], 1)
            pool.memset(k_st[:].bitcast(F32), 0.0)
            pool.memset(vals[:], 0.0).then_inc(ready["ones"], 1)
            pool.wait_ge(ready["ones"], 2)
            pool.memset(vals[:, :, :, :, HD:HD + 1], 1.0).then_inc(ready["ones"], 1)
            pool.wait_ge(ready["ones"], 3)
            pool.memset(vals[0:1, 0, :, :, HD:HD + 1], 0.0)
            pool.tensor_copy(ones_but0[:, 1:P], ones[:, 1:P].bitcast(F32))
            pool.memset(ones_but0[:, 0:1].bitcast(F32), 0.0)
            for k, (e, top) in enumerate(((E0, TOP0), (E1, TOP1))):
                for n in range(8 - top):
                    pool.memset(score[k][:, :, e + n:e + n + 1], -1.0 - n)
            pool.memset(q_blk[:].bitcast(F32), 0.0).then_inc(ready["zeroed"], 1)
            pool.wait_ge(loaded, LOADED)
            with pool.Fori(0, HALVES) as i:
                for n in range(G * HB):
                    pool.wait_ge(a0["max"], i * 32 + 2 * n + 2)
                    if n >= SH:
                        pool.wait_ge(a0["st"], i * 32 + 2 * (n - SH + 1))
                    pool.tensor_tensor(shift[:, n % SH], ident.unsqueeze(1).to_broadcast([P, GH, P]),
                                       neg_max[:, n % SH, :].unsqueeze(2).to_broadcast([P, GH, P]),
                                       ALU.mult).then_inc(a0["shift"], 1)

            def low_parts(s, e, slot, width):
                pool.wait_ge(s["whi"], e + 1)
                pool.tensor_tensor(exp_lo[:, slot, 0:width], exp_f[:, slot, 0:width],
                                   exp_hi[:, slot, 0:width].bitcast(F32), ALU.subtract).then_inc(s["wlo"], 1)

            def weigh(s, n, e, h, unit, at):
                pool.wait_ge(s["glu"], n + 1)
                pool.wait_ge(s["wbc"], e * 2 + h + 1)
                pool.tensor_tensor(unit, unit, wbc[0:unit.shape[0], at, :], ALU.mult).then_inc(s["glw"], 1)

            if STAGES > 1:
                s = ffn[0]
                for e in range(2):
                    low_parts(s, e, e, 2 * F0)

                def expert0(e, slot, last):
                    for h in range(2):
                        weigh(s, e * 2 + h, e, h, gate_a[:, h, :], 2 * slot + h)
                    if not last:
                        low_parts(s, e + 2, slot, 2 * F0)

                with pool.Fori(0, E0 // 2 - 1) as i:
                    for slot in range(2):
                        expert0(i * 2 + slot, slot, False)
                for slot in range(2):
                    expert0(E0 - 2 + slot, slot, True)
            if STAGES > 2:
                s = a1

                def four_sums(u):
                    pool.wait_ge(s["exp"], u + 1)
                    if u >= 2:
                        pool.wait_ge(s["sum"], u - 1)
                    pool.tensor_tensor(hsum[:, u % 2], hprobs[:, u % 3, 0:H // 2, :], hprobs[:, u % 3, H // 2:H, :],
                                       ALU.add).then_inc(s["pairs"], 1)
                    pool.wait_ge(s["pairs"], u + 1)
                    pool.tensor_tensor(hsum[:, u % 2, 0:H // 4, :], hsum[:, u % 2, 0:H // 4, :],
                                       hsum[:, u % 2, H // 4:H // 2, :], ALU.add).then_inc(s["fours"], 1)

                four_sums(0)
                for u in range(UNITS):
                    if u + 1 < UNITS:
                        four_sums(u + 1)
                    pool.wait_ge(s["rec"], u + 1)
                    mine = hprobs[:, u % 3, H - POOL_HEADS:H, :]
                    pool.tensor_tensor(mine, mine, hrec[:, u % 2, :].unsqueeze(1).to_broadcast([P, POOL_HEADS, UQ]),
                                       ALU.mult).then_inc(s["wtp"], 1)
            if STAGES > 3:
                s = ffn[1]
                for e in range(2):
                    low_parts(s, e, e, 2 * F1)

                def expert1(e, slot, last):
                    for h in range(2):
                        for c, (_, m) in enumerate(CH1):
                            n = h * 3 + c
                            weigh(s, e * 6 + n, e, h, glu1[0:m, (6 * slot + n) % 4, :], h)
                    if not last:
                        low_parts(s, e + 2, slot, 2 * F1)

                with pool.Fori(0, E1 // 2 - 1) as i:
                    for slot in range(2):
                        expert1(i * 2 + slot, slot, False)
                for slot in range(2):
                    expert1(E1 - 2 + slot, slot, slot == 1)

        @block.scalar
        def _(act):
            def copy(dst, src):
                return act.activation(dst, src, ACT.Copy)

            act.wait_ge(loaded, LOADED)
            act.activation(tanh_gate[:], row[:, R_GATE:R_GATE + H], ACT.Tanh).then_inc(ready["tanh"], 1)
            copy(negid[:], cst[:, C_NEG:C_NEG + P])
            copy(qk_hi[:], qk_f).then_inc(ready["qk_hi"], 1)

            def prelude(s, i, k):
                act.wait_ge(s["var"], i * k + 1)
                act.activation(rstd[:, 0:HB], rvar[:, 0:HB], ACT.Sqrt).then_inc(s["std"], 1)
                copy(c_f[:], ctx_sb[:, bass.ds(i * HT, HT)]).then_inc(s["ctxc"], 1)
                copy(c_hi[:], ctx_sb[:, bass.ds(i * HT, HT)]).then_inc(s["ctxc"], 1)
                act.wait_ge(s["xt"], i + 1)
                copy(x_f[:, 0:HT], ps[:, 0, :]).then_inc(s["xc"], 1)
                copy(x_hi[:, 0:HT], ps[:, 0, :]).then_inc(s["xc"], 1)

            def copy_values(s, base, c):
                act.wait_ge(s["v"], base + c + 1)
                copy(vals[:, c, :, :, 0:HD], ps[:, 1 + c, :].rearrange("p (b h d) -> p b h d", b=HB, h=H)
                     ).then_inc(s["vcopy"], 1)

            def round_piece(s, base, n, bank=None):
                act.wait_ge(s["proj"], base + n + 1)
                if n >= 2:
                    act.wait_ge(s["stk"], base + n - 1)
                copy(rnd[:, n % 2, :], ps[:, n % 2 if bank is None else bank, :]).then_inc(s["rnd"], 1)

            with act.Fori(0, HALVES) as i:
                s = a0
                prelude(s, i, 1)
                for c in range(2):
                    copy_values(s, i * 2, c)
                act.wait_ge(s["firstp"], i + 1)
                copy(first_b[:], ps[:, 3, :].rearrange("p (b d) -> p b d", b=HB)).then_inc(s["firstb"], 1)
                for n in range(3):
                    round_piece(s, i * 12, n)
                for n in range(G * HB):
                    g, b = divmod(n, HB)
                    for c in range(2):
                        act.wait_ge(s["st"], i * 32 + 2 * n + c + 1)
                        if n >= 2:
                            act.wait_ge(s["pv"], i * 16 + n - 1)
                        act.activation(probs[:, n % 2, c, :], ps[:, 4 + c, :], ACT.Exp,
                                       scale=SCALE).then_inc(s["exp"], 1)
                    for piece in pieces_at(n):
                        round_piece(s, i * 12, piece)
                    if g >= 1 and b == 1:
                        act.wait_ge(s["pv"], i * 16 + 4 * g)
                        copy(heads_t[:, g - 1, :], ps[:, 6 + (g - 1) % 2, :]).then_inc(s["ot"], 1)
                act.wait_ge(s["pv"], i * 16 + 16)
                copy(heads_t[:, G - 1, :], ps[:, 6 + (G - 1) % 2, :]).then_inc(s["ot"], 1)
                act.wait_ge(s["var2"], i + 1)
                act.activation(rstd[:, 0:HB], rvar[:, 0:HB], ACT.Sqrt).then_inc(s["std2"], 1)
                act.wait_ge(s["t2"], i + 1)
                act.activation(ln_t, ps[:, 6, :], ACT.Identity, bias=ln_b, scale=ln_g).then_inc(s["aff"], 1)

            def ffn_prelude(s, k):
                width = 2 * (F0, F1)[k]
                for e in range(2):
                    act.wait_ge(s[f"wdma{e}"], 16)
                    copy(exp_hi[:, e, 0:width], exp_f[:, e, 0:width]).then_inc(s["whi"], 1)
                act.wait_ge(s["var"], 1)
                act.activation(rstd[:], rvar[:], ACT.Sqrt).then_inc(s["std"], 1)
                act.wait_ge(s["xt"], 1)
                both = ps[:, 0:2, :].rearrange("p k n -> p (k n)")
                copy(x_f[:], both).then_inc(s["xc"], 1)
                copy(x_hi[:], both).then_inc(s["xc"], 1)
                act.wait_ge(s["lmax"], 1)
                e = (E0, E1)[k]
                act.activation(logit[:, :, 0:e], logit[:, :, 0:e], ACT.Exp).then_inc(s["e"], 1)
                act.wait_ge(s["wt"], 1)
                both = ps[:, 3:5, :].rearrange("p k n -> p (k n)")
                copy(wt_bf[:], both).then_inc(s["wtc"], 1)
                if k == 0:
                    copy(wt_f[:], both).then_inc(s["wtc"], 1)

            def high_parts(s, i, slot, k, units):
                width = 2 * (F0, F1)[k]
                act.wait_ge(s[f"wdma{slot}"], (i + 2) * 16)
                act.wait_ge(s["gu"], (i * 2 + slot + 1) * units * 2)
                copy(exp_hi[:, slot, 0:width], exp_f[:, slot, 0:width]).then_inc(s["whi"], 1)

            def weights_copy(s, e, h, at):
                act.wait_ge(s["wb"], e * 2 + h + 1)
                copy(wbc[:, at, :], ps[:, 4 + h, :]).then_inc(s["wbc"], 1)

            def acc_copy(s):
                for h in range(2):
                    act.wait_ge(s["down"], h + 1)
                    copy(acc_sb[:, 512 * h:512 * (h + 1)], ps[:, 6 + h, :]).then_inc(s["acc"], 1)

            if STAGES > 1:
                s = ffn[0]
                ffn_prelude(s, 0)

                def expert0(i, slot, last):
                    e = i * 2 + slot
                    for h in range(2):
                        weights_copy(s, e, h, 2 * slot + h)
                        act.wait_ge(s["ga"], e * 2 + h + 1)
                        act.activation(gate_a[:, h, :], gate_a[:, h, :],
                                       ACT.Gelu_apprx_sigmoid).then_inc(s["glu"], 1)
                    if not last:
                        high_parts(s, i, slot, 0, 2)

                act.preload_act_table(ACT.Gelu_apprx_sigmoid)
                with act.Fori(0, E0 // 2 - 1) as i:
                    for slot in range(2):
                        expert0(i, slot, False)
                for slot in range(2):
                    expert0(E0 // 2 - 1, slot, True)
                acc_copy(s)
            if STAGES > 2:
                s = a1

                def exponentials(u):
                    act.wait_ge(s["nm"], u + 1)
                    if u >= 3:
                        act.wait_ge(s["pv"], u - 2)
                    act.activation(hprobs[:, u % 3].rearrange("p h q -> p (h q)"),
                                   ps[:, 2 * (u % 3):2 * (u % 3) + 2, :].rearrange("p k n -> p (k n)"),
                                   ACT.Exp, scale=SCALE).then_inc(s["exp"], 1)

                def weighted_values(b):
                    act.wait_ge(s["pv"], 2 * b + 2)
                    if b:
                        act.wait_ge(s["wo"], b)
                    copy(heads1[:].rearrange("p g q -> p (g q)"), ps[:, 7, :]).then_inc(s["ot"], 1)

                for half in range(HALVES):
                    act.wait_ge(s["v"], half + 1)
                    copy(vals[:, half, :, :, 0:HD], ps[:, 4 + half, :].rearrange("p (b h d) -> p b h d", b=HB, h=H)
                         ).then_inc(s["vcopy"], 1)
                act.wait_ge(s["var"], 1)
                act.activation(rstd[:], rvar[:], ACT.Sqrt).then_inc(s["std"], 1)
                for n in range(G):
                    round_piece(s, 0, n, bank1(n))
                act.wait_ge(s["xt"], 1)
                for half in range(HALVES):
                    copy(x_hi[:, half * HT:(half + 1) * HT], ps[:, 2 + half, :]).then_inc(s["xc"], 1)
                act.wait_ge(s["proj"], G)
                copy(c_hi[:], ctx_sb[:, 0:HT]).then_inc(s["ctxc"], 1)
                act.preload_act_table(ACT.Exp)
                for n in range(G, 3 * G + 2):
                    round_piece(s, 0, n, bank1(n))
                exponentials(0)
                for n in range(3 * G + 2, 4 * G):
                    round_piece(s, 0, n, bank1(n))
                for u in range(UNITS):
                    if u + 1 < UNITS:
                        exponentials(u + 1)
                    if u >= 2 and u % 2 == 0:
                        weighted_values(u // 2 - 1)
                weighted_values(B - 1)
            if STAGES > 3:
                s = ffn[1]
                ffn_prelude(s, 1)

                def silu(e, slot, h, c, m):
                    n = h * 3 + c
                    act.wait_ge(s["gu"], (e * 6 + n) * 2 + 1)
                    act.activation(glu1[0:m, (6 * slot + n) % 4, :], ps[0:m, n % 2, :],
                                   ACT.Silu).then_inc(s["glu"], 1)

                def expert1(i, slot, routed, last):
                    e = i * 2 + slot
                    for h in range(2):
                        if routed:
                            weights_copy(s, e, h, h)
                        for c, (_, m) in enumerate(CH1):
                            silu(e, slot, h, c, m)
                    if not last:
                        high_parts(s, i, slot, 1, 6)

                act.preload_act_table(ACT.Silu)
                with act.Fori(0, E1 // 2 - 1) as i:
                    for slot in range(2):
                        expert1(i, slot, True, False)
                for slot in range(2):
                    expert1(E1 // 2 - 1, slot, True, slot == 1)
                expert1(E1 // 2, 0, False, True)
                acc_copy(s)

        @block.vector
        def _(dve):
            dve.wait_ge(loaded, LOADED)
            dve.wait_ge(ready["qk_hi"], 1)
            dve.tensor_tensor(qk_lo[:], qk_f, qk_hi[:].bitcast(F32), ALU.subtract).then_inc(ready["split"], 1)
            dve.tensor_scalar(up_b[:], biases[:, 1, :], 1.0, None, ALU.add)

            def normalised(s, chain, src, n, std, std_at, done):
                dve.wait_ge(s[std], std_at)
                for b in range(n):
                    dve.tensor_scalar(xn[:, b, :], src(b), mv[:, b, 0:1], rstd[:, b:b + 1], ALU.subtract,
                                      ALU.mult).then_inc(s[done], 1)

            def split_half(s, i):
                dve.wait_ge(s["ctxc"], i * 2 + 2)
                dve.tensor_tensor(c_lo[:], c_f[:], c_hi[:].bitcast(F32), ALU.subtract).then_inc(s["lo"], 1)
                dve.wait_ge(s["xc"], i * 2 + 2)
                dve.tensor_tensor(x_lo[:, 0:HT], x_f[:, 0:HT], x_hi[:, 0:HT].bitcast(F32),
                                  ALU.subtract).then_inc(s["lo"], 1)

            def stack_piece(s, base, per_group, n, blk, skip_first):
                g, kind = divmod(n, per_group)
                dve.wait_ge(s["rnd"], base + n + 1)
                src, hi = ps[:, n % 2, :], rnd[:, n % 2, :].bitcast(F32)
                if kind == 0:
                    if g >= 2:
                        dve.wait_ge(s[f"blk{g % 2}"], blk + 16 * GH * (g // 2))
                    dve.scalar_tensor_tensor(q_st[:, g % 2, :], hi, qsel, src, ALU.mult,
                                             ALU.add).then_inc(s["stk"], 1)
                else:
                    lead = 1 if skip_first and kind == 1 else 0
                    at = (kind - 1) * P
                    dve.scalar_tensor_tensor(
                        k_st[:, g, :, at + lead:at + P],
                        hi.rearrange("p (b k) -> p b k", b=HB)[:, :, lead:], ksel,
                        src.rearrange("p (b k) -> p b k", b=HB)[:, :, lead:], ALU.mult,
                        ALU.add).then_inc(s["stk"], 1)

            with dve.Fori(0, HALVES) as i:
                s = a0
                chain = Chain(dve, s["chain"], i * A0_CHAIN, A0_CHAIN)

                def tile_of_half(b):
                    return resid[:, bass.ds(i * HB + b, 1), :].rearrange("p o d -> p (o d)")

                layer_norm_stats(dve, s, tile_of_half, HB, chain, "var")
                normalised(s, chain, tile_of_half, HB, "std", i + 1, "norm")
                split_half(s, i)
                dve.wait_ge(ready["tanh"], 1)
                dve.wait_ge(s["vcopy"], i * 2 + 1)
                chain.step(dve.tensor_tensor(
                    first_v[:], vals[0:1, 0, :, :, 0:HD],
                    tanh_gate[:].unsqueeze(1).unsqueeze(3).to_broadcast([1, HB, H, HD]), ALU.mult))
                chain.sync()
                dve.memset(vals[0:1, 0, :, :, 0:HD], 0.0).then_inc(s["first"], 1)
                dve.wait_ge(ready["zeroed"], 1)
                for n in range(3):
                    stack_piece(s, i * 12, 3, n, i * 128, True)
                for n in range(G * HB):
                    for u in range(2):
                        dve.wait_ge(s["qk"], i * 32 + 2 * n + u + 1)
                        if n >= SH:
                            dve.wait_ge(s["shift"], i * 16 + n - SH + 1)
                        dve.tensor_reduce(neg_max[:, n % SH, 2 * u:2 * u + 2],
                                          ps[:, 2 + u, :].rearrange("p (j k) -> p j k", j=2)[:, :, 1:],
                                          AX_X, ALU.max, negate=True).then_inc(s["max"], 1)
                    if n >= 2:
                        for piece in pieces_at(n - 2):
                            stack_piece(s, i * 12, 3, piece, i * 128, True)
                dve.wait_ge(s["gat"], i * HB + HB)
                chain.step(dve.reciprocal(rsum[:], ps[:, 2:6, D:OUTW]))
                chain.sync()
                chain.step(dve.tensor_tensor(attn[:], ps[:, 2:6, 0:D].rearrange("p b (h d) -> p b h d", h=H),
                                             rsum[:].unsqueeze(3).to_broadcast([P, HB, H, HD]), ALU.mult))
                chain.sync()
                dve.wait_ge(s["firstb"], i + 1)
                chain.step(dve.tensor_tensor(attn_bf[:], attn[:].rearrange("p b h d -> p b (h d)"), first_b[:],
                                             ALU.add))
                chain.sync()
                layer_norm_stats(dve, s, lambda b: attn_bf[:, b, :], HB, chain, "var2")
                normalised(s, chain, lambda b: attn_bf[:, b, :], HB, "std2", i + 1, "norm2")
                dve.wait_ge(s["wp"], i + 1)
                half = resid[:, bass.ds(i * HB, HB), :]
                dve.tensor_tensor(half, half, ps[:, 7, :].rearrange("p (b d) -> p b d", b=HB),
                                  ALU.add).then_inc(s["res"], 1)
                dve.wait_ge(s["res"], i + 1)
                chain.close()

            def ffn_prelude(s, k):
                e, top = ((E0, TOP0), (E1, TOP1))[k]
                fill = 8 - top
                chain = Chain(dve, s["chain"])
                layer_norm_stats(dve, s, lambda b: resid[:, b, :], B, chain, "var")
                normalised(s, chain, lambda b: resid[:, b, :], B, "std", 1, "norm")
                dve.wait_ge(s["xc"], 2)
                dve.tensor_tensor(x_lo[:], x_f[:], x_hi[:].bitcast(F32), ALU.subtract).then_inc(s["lo"], 1)
                dve.wait_ge(s["logit"], 1)
                lg = ps[:, 2, 0:B * e].rearrange("p (t e) -> p t e", t=B)
                chain.step(dve.tensor_reduce(rmax[:], lg, AX_X, ALU.max))
                chain.sync()
                dve.tensor_tensor(logit[:, :, 0:e], lg, rmax[:].unsqueeze(2).to_broadcast([P, B, e]),
                                  ALU.subtract).then_inc(s["lmax"], 1)
                dve.wait_ge(s["e"], 1)
                chain.step(dve.tensor_reduce(rmax[:], logit[:, :, 0:e], AX_X, ALU.add))
                chain.sync()
                chain.step(dve.reciprocal(rmax[:], rmax[:]))
                chain.sync()
                sc = score[k]
                chain.step(dve.tensor_tensor(sc[:, :, 0:e], logit[:, :, 0:e],
                                             rmax[:].unsqueeze(2).to_broadcast([P, B, e]), ALU.mult))
                chain.sync()
                for t in range(B):
                    chain.step(dve.max(top8[:, t, :], sc[:, t, 0:e]))
                chain.sync()
                chain.step(dve.tensor_copy(top8[:, :, top:8], sc[:, :, e:e + fill]))
                chain.sync()
                for t in range(B):
                    chain.step(dve.match_replace(kept[:, t, 0:e + fill], top8[:, t, :], sc[:, t, 0:e + fill], 0.0))
                chain.sync()
                chain.step(dve.tensor_tensor(tokw[:, :, 0:e], sc[:, :, 0:e], kept[:, :, 0:e], ALU.subtract))
                chain.sync()
                if k == 1:
                    chain.step(dve.tensor_reduce(rmax[:], tokw[:, :, 0:e], AX_X, ALU.add))
                    chain.sync()
                    chain.step(dve.reciprocal(rmax[:], rmax[:]))
                    chain.sync()
                    chain.step(dve.tensor_tensor(tokw[:, :, 0:e], tokw[:, :, 0:e],
                                                 rmax[:].unsqueeze(2).to_broadcast([P, B, e]), ALU.mult))
                    chain.sync()
                left = tokw[:, :, 0:e]
                for part in range(PARTS):
                    cols = wparts[:, :, E0 * part:E0 * part + e]
                    ins = dve.tensor_copy(cols, left)
                    if part == PARTS - 1:
                        ins.then_inc(s["wp"], 1)
                        break
                    chain.step(ins)
                    chain.sync()
                    chain.step(dve.tensor_tensor(tokr[:, part, :, 0:e], left, cols, ALU.subtract))
                    chain.sync()
                    left = tokr[:, part, :, 0:e]

            def ffn_residual(s):
                for h in range(2):
                    dve.wait_ge(s["tr"], h + 1)
                    half = resid[:, HB * h:HB * (h + 1), :]
                    dve.tensor_tensor(half, half, ps[:, h, :].rearrange("p (b d) -> p b d", b=HB),
                                      ALU.add).then_inc(s["res"], 1)
                dve.wait_ge(s["res"], 2)

            if STAGES > 1:
                s = ffn[0]
                ffn_prelude(s, 0)

                def clamp0(e, h, first=False):
                    at = bass.ds(e, 1)
                    if not first:
                        dve.wait_ge(s["act"], e * 2 + h - 1)
                    dve.wait_ge(s["gu"], (e * 2 + h) * 2 + 1)
                    dve.tensor_scalar(gate_a[:, h, :], ps[:, h, :], biases[:, 0, at], LIMIT, ALU.add,
                                      ALU.min).then_inc(s["ga"], 1)
                    dve.wait_ge(s["gu"], (e * 2 + h) * 2 + 2)
                    dve.tensor_scalar(up_a[:, h, :], ps[:, 2 + h, :], up_b[:, at], LIMIT + 1.0, ALU.add,
                                      ALU.min).then_inc(s["ua"], 1)

                def activate0(e, slot, h):
                    dve.wait_ge(s["glw"], e * 2 + h + 1)
                    dve.wait_ge(s["ua"], e * 2 + h + 1)
                    dve.scalar_tensor_tensor(act_f[:, 2 * slot + h, :], up_a[:, h, :], 1.0 - LIMIT,
                                             gate_a[:, h, :], ALU.max, ALU.mult).then_inc(s["act"], 1)

                def expert0(e, slot, last):
                    for h in range(2):
                        activate0(e, slot, h)
                        if not last:
                            clamp0(e + 1, h)

                for h in range(2):
                    clamp0(0, h, True)
                with dve.Fori(0, E0 // 2 - 1) as i:
                    for slot in range(2):
                        expert0(i * 2 + slot, slot, False)
                for slot in range(2):
                    expert0(E0 - 2 + slot, slot, slot == 1)
                ffn_residual(s)
            if STAGES > 2:
                s = a1
                chain = Chain(dve, s["chain"])

                def stack1(n):
                    what, half, g = PIECES1[n]
                    dve.wait_ge(s["rnd"], n + 1)
                    if what == "q" and half == 1 and g == 0:
                        for b in range(2):
                            dve.wait_ge(s[f"blk{b}"], 16 * GH)
                    dst, sel = (q_st[:, g, :], qsel) if what == "q" else (k1[:, g, half * HT:(half + 1) * HT], ksel)
                    dve.scalar_tensor_tensor(dst, rnd[:, n % 2, :].bitcast(F32), sel, ps[:, bank1(n), :], ALU.mult,
                                             ALU.add).then_inc(s["stk"], 1)

                def head_max(u):
                    dve.wait_ge(s["st"], u + 1)
                    if u >= 2:
                        dve.wait_ge(s["nm"], u - 1)
                    scores = ps[:, 2 * (u % 3):2 * (u % 3) + 2, :].rearrange("p k (a q) -> p q (k a)", q=UQ)
                    dve.tensor_reduce(hmax[:, u % 2, :], scores, AX_X, ALU.max).then_inc(s["max"], 1)

                def add_batch(b):
                    dve.wait_ge(s["wo"], b + 1)
                    dve.tensor_tensor(resid[:, b, :], resid[:, b, :], ps[:, 6, 0:D], ALU.add).then_inc(s["res"], 1)

                layer_norm_stats(dve, s, lambda b: resid[:, b, :], B, chain, "var")
                for n in range(2):
                    stack1(n)
                normalised(s, chain, lambda b: resid[:, b, :], B, "std", 1, "norm")
                for n in range(2, G):
                    stack1(n)
                for half in range(HALVES):
                    dve.wait_ge(s["xc"], half + 1)
                    cols = slice(half * HT, (half + 1) * HT)
                    dve.tensor_tensor(x_lo[:, cols], ps[:, 2 + half, :], x_hi[:, cols].bitcast(F32),
                                      ALU.subtract).then_inc(s["xlo"], 1)
                stack1(G)
                dve.wait_ge(s["ctxc"], 1)
                dve.tensor_tensor(c_lo[:], ctx_sb[:, 0:HT], c_hi[:].bitcast(F32), ALU.subtract).then_inc(s["clo"], 1)
                for n in range(G + 1, 3 * G):
                    stack1(n)
                head_max(0)
                head_max(1)
                for n in range(3 * G, 4 * G):
                    stack1(n)
                for u in range(UNITS):
                    if u + 2 < UNITS:
                        head_max(u + 2)
                    dve.wait_ge(s["sum"], u + 1)
                    if u >= 2:
                        dve.wait_ge(s["wtp"], u - 1)
                    dve.reciprocal(hrec[:, u % 2, :], ps[:, 2 * (u % 3), 0:UQ]).then_inc(s["rec"], 1)
                    dve.wait_ge(s["rec"], u + 1)
                    mine = hprobs[:, u % 3, 0:H - POOL_HEADS, :]
                    dve.tensor_tensor(mine, mine,
                                      hrec[:, u % 2, :].unsqueeze(1).to_broadcast([P, H - POOL_HEADS, UQ]),
                                      ALU.mult).then_inc(s["wtd"], 1)
                    if u >= 3 and u % 2 == 1:
                        add_batch((u - 3) // 2)
                add_batch(B - 1)
                dve.wait_ge(s["res"], B)
            if STAGES > 3:
                s = ffn[1]
                ffn_prelude(s, 1)

                def activate1(e, slot, h, c, m, routed):
                    n = h * 3 + c
                    at = (6 * slot + n) % 4
                    dve.wait_ge(s["gu"], (e * 6 + n) * 2 + 2)
                    dve.wait_ge(s["glw" if routed else "glu"], e * 6 + n + 1)
                    dve.tensor_tensor(act_f[0:m, at, :], glu1[0:m, at, :], ps[0:m, 2 + n % 2, :],
                                      ALU.mult).then_inc(s["act"], 1)

                def expert1(e, slot, routed):
                    for h in range(2):
                        for c, (_, m) in enumerate(CH1):
                            activate1(e, slot, h, c, m, routed)

                with dve.Fori(0, E1 // 2) as i:
                    for slot in range(2):
                        expert1(i * 2 + slot, slot, True)
                expert1(E1, 0, False)
                ffn_residual(s)

        @block.tensor
        def _(pe):
            def mm(dst, lhs, rhs, start=True, stop=True):
                return pe.matmul(dst, lhs, rhs, start=start, stop=stop, skip_group_check=True)

            def three_pass(dst, lhs_hi, lhs_lo, rhs_hi, rhs_lo):
                mm(dst, lhs_hi, rhs_hi, True, False)
                mm(dst, lhs_hi, rhs_lo, False, False)
                return mm(dst, lhs_lo, rhs_hi, False, True)

            pe.wait_ge(loaded, LOADED)
            pe.wait_ge(ready["split"], 1)
            pe.wait_ge(ready["zeroed"], 1)

            def turn(s, count, base, src, n, bank, done):
                for b in range(n):
                    pe.wait_ge(s[count], base + b + 1)
                    ins = pe.transpose(ps[:, bank + b // 4, (b % 4) * P:(b % 4 + 1) * P], src[:, b, :], ident)
                ins.then_inc(s[done], 1)

            def values(s, wv, c, src):
                for b in range(HB):
                    ins = mm(ps[:, 1 + c, b * P:(b + 1) * P], src[:, b * P:(b + 1) * P], wv)
                ins.then_inc(s["v"], 1)

            def project_piece(s, layer, base, per_group, n):
                g, kind = divmod(n, per_group)
                if n >= 2:
                    pe.wait_ge(s["stk"], base + n - 1)
                which, hi, lo = (0, x_hi[:, 0:HT], x_lo[:, 0:HT]) if kind == 0 else \
                    (1, c_hi[:], c_lo[:]) if kind == 1 else (1, x_hi[:, 0:HT], x_lo[:, 0:HT])
                cols = slice(g * P, (g + 1) * P)
                three_pass(ps[:, n % 2, :], qk_hi[:, 2 * layer + which, cols], qk_lo[:, 2 * layer + which, cols],
                           hi, lo).then_inc(s["proj"], 1)

            with pe.Fori(0, HALVES) as i:
                s = a0
                turn(s, "norm", i * HB, xn, HB, 0, "xt")
                pe.wait_ge(s["ctxc"], i * 2 + 2)
                values(s, w["wv0"], 0, c_f)
                pe.wait_ge(s["xc"], i * 2 + 2)
                values(s, w["wv0"], 1, x_f)
                pe.wait_ge(s["lo"], i * 2 + 2)
                pe.wait_ge(s["vcopy"], i * 2 + 2)
                project_piece(s, 0, i * 12, 3, 0)
                project_piece(s, 0, i * 12, 3, 1)
                pe.wait_ge(s["first"], i + 1)
                mm(ps[:, 3, :], one_row, first_v[:].rearrange("p b h d -> p (b h d)")).then_inc(s["firstp"], 1)
                project_piece(s, 0, i * 12, 3, 2)
                pe.wait_ge(s["firstb"], i + 1)

                def scores_by_query(n):
                    g, b = divmod(n, HB)
                    if b == 0:
                        pe.wait_ge(s["stk"], i * 12 + 3 * g + 3)
                        pe.wait_ge(s[f"blk{g % 2}"], i * 128 + 64 * (g // 2 + 1))
                    for u in range(2):
                        if n >= 1:
                            pe.wait_ge(s["max"], i * 32 + 2 * (n - 1) + u + 1)
                        for j in (2 * u, 2 * u + 1):
                            ins = mm(ps[:, 2 + u, (j % 2) * KEYS:(j % 2 + 1) * KEYS],
                                     q_blk[:, g, j, b * P:(b + 1) * P], k_st[:, g, b, :])
                        ins.then_inc(s["qk"], 1)

                def scores_by_key(n):
                    g, b = divmod(n, HB)
                    for c in range(2):
                        if n >= 1:
                            pe.wait_ge(s["exp"], i * 32 + 2 * (n - 1) + c + 1)
                        mm(ps[:, 4 + c, :].rearrange("p (j q) -> p j q", j=GH), k_st[:, g, b, c * P:(c + 1) * P],
                           q_blk[:, g, :, b * P:(b + 1) * P], True, False)
                        if c == 0:
                            pe.wait_ge(s["shift"], i * 16 + n + 1)
                        mm(ps[:, 4 + c, :].rearrange("p (j q) -> p j q", j=GH), (ones_but0, ones)[c][:],
                           shift[:, n % SH], False, True).then_inc(s["st"], 1)

                def weigh_values(n):
                    g, b = divmod(n, HB)
                    if b == 0 and g >= 2:
                        pe.wait_ge(s["ot"], i * G + g - 1)
                    for c in range(2):
                        pe.wait_ge(s["exp"], i * 32 + 2 * n + c + 1)
                        for j in range(GH):
                            ins = mm(ps[SLOT * j:SLOT * (j + 1), 6 + g % 2, b * P:(b + 1) * P],
                                     vals[:, c, b, GH * g + j, :], probs[:, n % 2, c, j * P:(j + 1) * P],
                                     c == 0, c == 1)
                    ins.then_inc(s["pv"], 1)

                scores_by_query(0)
                scores_by_query(1)
                for n in range(G * HB):
                    g, b = divmod(n, HB)
                    if n + 2 < G * HB:
                        scores_by_query(n + 2)
                    scores_by_key(n)
                    for piece in pieces_at(n):
                        project_piece(s, 0, i * 12, 3, piece)
                    if n >= 1:
                        weigh_values(n - 1)
                weigh_values(G * HB - 1)
                pe.wait_ge(s["ot"], i * G + G)
                pe.wait_ge(s["max"], i * 32 + 32)
                for b in range(HB):
                    for g in range(G):
                        ins = mm(ps[:, 2 + b, 0:OUTW], heads_t[:, g, b * P:(b + 1) * P], gather[:, g, :],
                                 g == 0, g == G - 1)
                    ins.then_inc(s["gat"], 1)
                turn(s, "norm2", i * HB, xn, HB, 6, "t2")
                pe.wait_ge(s["aff"], i + 1)
                for b in range(HB):
                    mm(ps[:, 7, b * P:(b + 1) * P], ln_t[:, b * P:(b + 1) * P], w["wp0"], True, False)
                    ins = mm(ps[:, 7, b * P:(b + 1) * P], one_row, row[:, R_BP:R_BP + D], False, True)
                ins.then_inc(s["wp"], 1)

            def ffn_prelude(s, k):
                e = (E0, E1)[k]
                turn(s, "norm", 0, xn, B, 0, "xt")
                pe.wait_ge(s["xc"], 2)
                for t in range(B):
                    dst = ps[:, 2, t * e:(t + 1) * e]
                    ins = mm(dst, x_f[:, t * P:(t + 1) * P], w[("rw0", "gw1")[k]], True, k == 1)
                    if k == 0:
                        ins = mm(dst, one_row, row[:, R_RB:R_RB + e], False, True)
                ins.then_inc(s["logit"], 1)
                pe.wait_ge(s["wp"], 1)
                for t in range(B):
                    ins = mm(ps[:, 3 + t // 4, (t % 4) * P:(t % 4 + 1) * P], wparts[:, t, :], idb[:])
                ins.then_inc(s["wt"], 1)
                pe.wait_ge(s["wtc"], 2 - k)
                for h in range(2):
                    if k == 0:
                        mm(ps[:, 6 + h, :], db0[:], wt_f[:, h * 512:(h + 1) * 512], True, False)
                    else:
                        mm(ps[:, 6 + h, :], zero_r[:], x_hi[:, 0:512], True, False)
                pe.wait_ge(s["lo"], 1)

            def gate_up(s, slot, gate, up, m, h, bank, gate_read=None, up_read=None):
                hi, lo = exp_hi, exp_lo
                tokens = slice(h * 512, (h + 1) * 512)
                for at, b0, read in ((gate, 0, gate_read), (up, 2, up_read)):
                    if read is not None:
                        pe.wait_ge(*read)
                    cols = slice(at, at + m)
                    three_pass(ps[0:m, b0 + bank, :], hi[:, slot, cols], lo[:, slot, cols], x_hi[:, tokens],
                               x_lo[:, tokens]).then_inc(s["gu"], 1)

            def spread_weights(s, e, h):
                mm(ps[:, 4 + h, :], psel[:, bass.ds(e, 1), :].rearrange("p o m -> p (o m)"),
                   wt_bf[:, h * 512:(h + 1) * 512]).then_inc(s["wb"], 1)

            def ffn_end(s):
                for h in range(2):
                    pe.wait_ge(s["acc"], h + 1)
                    for b in range(4):
                        ins = pe.transpose(ps[:, h, b * P:(b + 1) * P],
                                           acc_sb[:, (4 * h + b) * P:(4 * h + b + 1) * P], ident)
                    ins.then_inc(s["tr"], 1)

            if STAGES > 1:
                s = ffn[0]
                ffn_prelude(s, 0)

                def gates0(e, slot, h, first):
                    if h == 0:
                        pe.wait_ge(s["wlo"], e + 1)
                    read = None if first else (s["ua"], (e - 1) * 2 + h + 1)
                    gate_up(s, slot, 0, F0, F0, h, h, read)

                def down0(e, i, slot, h, final):
                    if h == 0:
                        pe.wait_ge(s[f"ddma{slot}"], i * 16 + 16)
                    pe.wait_ge(s["act"], e * 2 + h + 1)
                    ins = mm(ps[:, 6 + h, :], exp_d[:, slot, 0:D], act_f[:, 2 * slot + h, :], False, final)
                    if final:
                        ins.then_inc(s["down"], 1)
                    elif h == 1:
                        ins.then_inc(s["wfree"], 1)

                def expert0(i, slot, last):
                    e = i * 2 + slot
                    for h in range(2):
                        if not last:
                            gates0(e + 1, 1 - slot, h, False)
                            pe.wait_ge(s["wbc"], e * 2 + h + 1)
                            spread_weights(s, e + 1, h)
                        down0(e, i, slot, h, last)

                for h in range(2):
                    gates0(0, 0, h, True)
                    spread_weights(s, 0, h)
                with pe.Fori(0, E0 // 2 - 1) as i:
                    for slot in range(2):
                        expert0(i, slot, False)
                for slot in range(2):
                    expert0(E0 // 2 - 1, slot, slot == 1)
                ffn_end(s)
            if STAGES > 2:
                s = a1

                def project1(n):
                    what, half, g = PIECES1[n]
                    if n >= 4:
                        pe.wait_ge(s["stk"], n - 3 if n < 3 * G else n - 1)
                    if what == "k":
                        which, hi, lo = 3, c_hi[:], c_lo[:]
                        if half == 0 and g == 0:
                            pe.wait_ge(s["clo"], 1)
                    else:
                        cols = slice(half * HT, (half + 1) * HT)
                        which, hi, lo = 2, x_hi[:, cols], x_lo[:, cols]
                        if g == 0:
                            pe.wait_ge(s["xlo"], half + 1)
                    cols = slice(g * P, (g + 1) * P)
                    three_pass(ps[:, bank1(n), :], qk_hi[:, which, cols], qk_lo[:, which, cols],
                               hi, lo).then_inc(s["proj"], 1)

                def head_scores(u):
                    b, r = divmod(u, 2)
                    if u == 0:
                        pe.wait_ge(s["stk"], 3 * G)
                        pe.wait_ge(s["xlo"], 2)
                    for turn_of, (first, n) in enumerate(BLOCKS1):
                        if r == 0 and b == first:
                            earlier = sum(f % HB == b % HB for f, _ in BLOCKS1[:turn_of])
                            pe.wait_ge(s[f"blk{b % HB}"], 16 * GH * (earlier + 1))
                    if u >= 3:
                        pe.wait_ge(s["rec"], u - 2)
                    at = (b % HB) * P + r * UQ
                    for g in range(G):
                        ins = mm(ps[:, 2 * (u % 3) + g // 2, (g % 2) * GH * UQ:(g % 2 + 1) * GH * UQ
                                    ].rearrange("p (j q) -> p j q", j=GH),
                                 k1[:, g, b * P:(b + 1) * P], q_blk[:, g, :, at:at + UQ], g % 2 == 0, False)
                    ins.then_inc(s["st"], 1)

                def less_max(u):
                    pe.wait_ge(s["max"], u + 1)
                    for k in range(2):
                        ins = mm(ps[:, 2 * (u % 3) + k, :].rearrange("p (a q) -> p a q", q=UQ), negid[:],
                                 hmax[:, u % 2, :].unsqueeze(1).to_broadcast([P, H // 2, UQ]), False, True)
                    ins.then_inc(s["nm"], 1)

                def head_sum(u):
                    pe.wait_ge(s["fours"], u + 1)
                    for h in range(H // 4):
                        ins = mm(ps[:, 2 * (u % 3), 0:UQ], ident, hsum[:, u % 2, h, :], h == 0, h == H // 4 - 1)
                    ins.then_inc(s["sum"], 1)

                def weigh_values1(u):
                    b, r = divmod(u, 2)
                    if u == 0:
                        pe.wait_ge(s["stk"], 4 * G)
                        pe.wait_ge(s["vcopy"], 2)
                    elif r == 0:
                        pe.wait_ge(s["ot"], b)
                    pe.wait_ge(s["wtd"], u + 1)
                    pe.wait_ge(s["wtp"], u + 1)
                    for g in range(G):
                        for j in range(GH):
                            ins = mm(ps[SLOT * j:SLOT * (j + 1), 7, g * P + r * UQ:g * P + (r + 1) * UQ],
                                     vals[:, b // HB, b % HB, GH * g + j, :], hprobs[:, u % 3, GH * g + j, :])
                    ins.then_inc(s["pv"], 1)

                def project_out(b):
                    pe.wait_ge(s["ot"], b + 1)
                    if b:
                        pe.wait_ge(s["res"], b)
                    for g in range(G):
                        ins = mm(ps[:, 6, 0:D], heads1[:, g, :], wo1[:, g, :], g == 0, g == G - 1)
                    ins.then_inc(s["wo"], 1)

                for half in range(HALVES):
                    for b in range(HB):
                        at = (half * HB + b) * P
                        ins = mm(ps[:, 4 + half, b * P:(b + 1) * P], ctx_sb[:, at:at + P], w["wv1"])
                    ins.then_inc(s["v"], 1)
                pe.wait_ge(ffn[0]["res"], 2)
                for n in range(G):
                    project1(n)
                turn(s, "norm", 0, xn, B, 2, "xt")
                for n in range(G, 3 * G):
                    project1(n)
                pe.wait_ge(s["vcopy"], 2)
                head_scores(0)
                head_scores(1)
                for n in (12, 13):
                    project1(n)
                less_max(0)
                for n in (14, 15):
                    project1(n)
                for u in range(UNITS):
                    if u + 1 < UNITS:
                        less_max(u + 1)
                    if u + 2 < UNITS:
                        head_scores(u + 2)
                    head_sum(u)
                    if u >= 1:
                        weigh_values1(u - 1)
                    if u >= 3 and u % 2 == 1:
                        project_out((u - 3) // 2)
                weigh_values1(UNITS - 1)
                project_out(B - 1)
            if STAGES > 3:
                s = ffn[1]
                ffn_prelude(s, 1)

                def gates1(e, slot, n, first=False):
                    h, c = divmod(n, 3)
                    at, m = CH1[c]
                    if n == 0:
                        pe.wait_ge(s["wlo"], e + 1)
                    reads = () if first else ((s["glu"], e * 6 + n - 1), (s["act"], e * 6 + n - 1))
                    gate_up(s, slot, at, F1 + at, m, h, n % 2, *reads)

                def down1(e, i, slot, n, final):
                    h, c = divmod(n, 3)
                    if n == 0:
                        pe.wait_ge(s[f"ddma{slot}"], i * 16 + 16)
                    m = CH1[c][1]
                    pe.wait_ge(s["act"], e * 6 + n + 1)
                    ins = mm(ps[:, 6 + h, :], exp_d[0:m, slot, c * D:(c + 1) * D],
                             act_f[0:m, (6 * slot + n) % 4, :], False, final and c == 2)
                    if final and c == 2:
                        ins.then_inc(s["down"], 1)
                    elif n == 5:
                        ins.then_inc(s["wfree"], 1)

                def expert1(i, slot, kind=""):
                    e = i * 2 + slot
                    for n in range(6):
                        if n < 4:
                            gates1(e, slot, n + 2)
                        elif kind != "base":
                            gates1(e + 1, 1 - slot, n - 4)
                        down1(e, i, slot, n, kind == "base")
                        if n == 0 and kind != "base":
                            spread_weights(s, e, 1)
                        if n == 3 and not kind:
                            spread_weights(s, e + 1, 0)

                gates1(0, 0, 0, True)
                spread_weights(s, 0, 0)
                gates1(0, 0, 1, True)
                with pe.Fori(0, E1 // 2 - 1) as i:
                    for slot in range(2):
                        expert1(i, slot)
                expert1(E1 // 2 - 1, 0)
                expert1(E1 // 2 - 1, 1, "last routed")
                expert1(E1 // 2, 0, "base")
                ffn_end(s)


def _head_slots(wt, lanes):
    a = np.zeros((D, H, GH, HD), wt.dtype)
    a[:, :, :3, :] = wt.T.reshape(D, H, 1, HD)
    return a.reshape(D, G * P)


def kernel(**inputs):
    import concourse.bacc as bacc
    from concourse.bass_utils import run_bass_kernel_spmd

    a = {n: np.asarray(v) for n, v in inputs.items()}
    f32 = np.float32
    bf16 = mybir.dt.np(BF16)
    consts = np.zeros((P, C_END), f32)
    consts[:, C_ID:C_ID + P] = np.eye(P)
    consts[:, C_NEG:C_NEG + P] = -np.eye(P)
    lane = np.arange(P) % SLOT // HD
    consts[:, C_QSEL] = np.where(lane == 1, -1.0, 0.0)
    consts[:, C_KSEL] = np.where(lane == 2, -1.0, 0.0)
    consts[0, C_ONE:C_ONE + P] = 1.0
    gather = np.zeros((P, G, OUTW), f32)
    for h in range(H):
        g, j = divmod(h, GH)
        for d in range(HD):
            gather[SLOT * j + d, g, h * HD + d] = 1.0
        gather[SLOT * j + HD, g, D + h] = 1.0
    consts[:, C_GATHER:] = gather.reshape(P, G * OUTW)
    part_sel = np.zeros((P, E0, P), bf16)
    for part in range(PARTS):
        for e in range(E0):
            part_sel[E0 * part + e, e, :] = 1.0
    qk = np.stack([_head_slots(a[n], 0) for n in ("L0_xattn_Wq", "L0_xattn_Wk", "L1_xattn_Wq", "L1_xattn_Wk")], 1)
    small = np.zeros((P, W_END), f32)
    for n, v in (("wv0", a["L0_xattn_Wv"].T), ("wp0", a["L0_xattn_Wp"].T), ("wv1", a["L1_xattn_Wv"].T),
                 ("rw0", a["L0_ffn_router_weight"].T), ("gw1", a["L1_ffn_gate_w"])):
        small[:, W_AT[n]:W_AT[n] + W_WIDTH[n]] = v
    small[:, W_LN], small[:, W_LN + 1] = a["L0_xattn_ln_g"], a["L0_xattn_ln_b"]
    wo = np.zeros((GH, SLOT, G, D), f32)
    wo[:, :HD] = a["L1_xattn_Wo"].T.reshape(G, GH, HD, D).transpose(1, 2, 0, 3)
    small[:, W_WO:] = wo.reshape(P, G * D)
    rows = np.concatenate([a["L0_xattn_gate"].reshape(-1), a["L0_xattn_bp"], a["L0_ffn_router_bias"]])[None, :]
    down_bias = np.zeros((P, D), f32)
    for part in range(PARTS):
        down_bias[E0 * part:E0 * (part + 1)] = a["L0_ffn_down_bias"]
    gu_bias = a["L0_ffn_gate_up_bias"].reshape(E0, 2, F0).transpose(2, 1, 0)
    experts0 = np.concatenate([a["L0_ffn_gate_up_proj"], a["L0_ffn_down_proj"]], 2)
    wgu = np.concatenate([a["L1_ffn_exp_wgu"], a["L1_ffn_base_wgu"][None]], 0)
    wd = np.zeros((E1 + 1, 3 * P, D), f32)
    wd[:, :F1] = np.concatenate([a["L1_ffn_exp_wd"], a["L1_ffn_base_wd"][None]], 0)
    experts1 = np.concatenate([wgu, wd.reshape(E1 + 1, 3, P, D).transpose(0, 2, 1, 3).reshape(E1 + 1, P, 3 * D)], 2)
    arrays = {
        "x": a["x"], "ctx_t": a["ctx_1024"].transpose(2, 0, 1).reshape(D, T), "qk_w": qk, "small_w": small,
        "consts": consts, "rows": rows, "down_bias": down_bias, "gu_bias": gu_bias, "part_sel": part_sel,
        "ident_bf": np.eye(P).astype(bf16), "experts0": experts0, "experts1": experts1,
    }
    arrays = {n + "_dram": np.ascontiguousarray(v) for n, v in arrays.items()}
    nc = bacc.Bacc("TRN2", target_bir_lowering=False, num_devices=1)
    args = [nc.dram_tensor(n, v.shape, mybir.dt.from_np(v.dtype), kind="ExternalInput").ap()
            for n, v in arrays.items()]
    out = nc.dram_tensor("out_dram", (B, P, D), F32, kind="ExternalOutput").ap()
    two_layers(nc, *args, out)
    r = run_bass_kernel_spmd(nc, [arrays], core_ids=[0])
    return r.results[0]["out_dram"]
```

```python
from contextlib import ExitStack

import concourse.bass as bass
import numpy as np
from concourse import mybir

F32 = mybir.dt.float32
F32R = mybir.dt.float32r
BF16 = mybir.dt.bfloat16
ALU = mybir.AluOpType
ACT = mybir.ActivationFunctionType
AX_X = mybir.AxisListType.X

P = 128
B = 8
D = 128
H = 16
HD = D // H
GH = 4
G = H // GH
SLOT = P // GH
HB = 4
HALVES = B // HB
HT = HB * P
T = B * P
KEYS = 2 * P
LN_EPS = 1e-5
SCALE = float(HD) ** -0.5
E0, TOP0 = 16, 4
F0 = 128
LIMIT = 7.0
E1, TOP1 = 8, 2
F1 = 352
CH1 = [(0, 128), (128, 128), (256, 96)]
PARTS = 3
OUTW = D + H

SH = 3
UQ = P // 2
UNITS = B * P // UQ
POOL_HEADS = 4

C_ID, C_QSEL, C_KSEL, C_ONE = 0, P, P + 1, P + 2
C_NEG = C_ONE + P
C_GATHER = C_NEG + P
C_END = C_GATHER + G * OUTW
W_NAMES = ["wv0", "wp0", "wv1", "rw0", "gw1"]
W_WIDTH = {"wv0": D, "wp0": D, "wv1": D, "rw0": E0, "gw1": E1}
W_AT, _at = {}, 0
for _n in W_NAMES:
    W_AT[_n] = _at
    _at += W_WIDTH[_n]
W_LN = _at
W_WO = _at + 2
W_END = W_WO + G * D
R_GATE, R_BP, R_RB = 0, H, H + HB * D
R_END = R_RB + B * E0


def two_layers(nc, x, ctx_t, qk_w, small_w, consts, rows, down_bias, gu_bias, part_sel, ident_bf, experts0,
               experts1, out):
    with ExitStack() as ctx:
        def sb(name, shape, dt=F32):
            return ctx.enter_context(nc.sbuf_tensor(name, shape, dt))

        def sem(name):
            return ctx.enter_context(nc.semaphore(name))

        ps = ctx.enter_context(nc.psum_tensor("ps", [P, 8, 512], F32))
        resid = sb("resid", [P, B, D])
        ctx_sb = sb("ctx_sb", [P, T])
        qk_hi = sb("qk_hi", [P, 4, G * P], F32R)
        qk_lo = sb("qk_lo", [P, 4, G * P], F32R)
        small = sb("small", [P, W_END])
        cst = sb("cst", [P, C_END])
        row = sb("row", [1, R_END])
        negid = sb("negid", [P, P], F32R)
        ones = sb("ones", [P, P], F32R)
        ones_but0 = sb("ones_but0", [P, P], F32R)
        zero_r = sb("zero_r", [P, P], F32R)
        tanh_gate = sb("tanh_gate", [1, H])
        db0 = sb("db0", [P, D])
        psel = sb("psel", [P, E0, P], BF16)
        idb = sb("idb", [P, P], BF16)
        xn = sb("xn", [P, B, D])
        stats = sb("stats", [P, B, 6])
        mv = sb("mv", [P, B, 3])
        rvar = sb("rvar", [P, B])
        rstd = sb("rstd", [P, B])
        x_f = sb("x_f", [P, T])
        x_hi = sb("x_hi", [P, T], F32R)
        x_lo = sb("x_lo", [P, T], F32R)
        c_hi = sb("c_hi", [P, T], F32R)
        c_lo = sb("c_lo", [P, T], F32R)
        vals = sb("vals", [P, 2, HB, H, SLOT])
        first_b = sb("first_b", [P, HB, D])
        rnd = sb("rnd", [P, 2, HT], F32R)
        q_st = sb("q_st", [P, G, HT], F32R)
        with nc.sbuf_tensor("below_vals_half1", [P, 2, GH, HT], F32R), \
                nc.sbuf_tensor("vals_half1", [P, 2, HB, H, SLOT], F32) as vals_half1:
            pass
        q_blk = sb("q_blk", [P, G, GH, HT], F32R)
        k_st = sb("k_st", [P, G, HB, KEYS], F32R)
        neg_max = sb("neg_max", [P, SH, GH])
        shift = sb("shift", [P, SH, GH, P], F32R)
        rsum = sb("rsum", [P, HB, H])
        attn = sb("attn", [P, HB, H, HD])
        attn_bf = sb("attn_bf", [P, B, D], BF16)
        ln_t = x_f
        hmax = sb("hmax", [P, 2, UQ], F32R)
        hrec = sb("hrec", [P, 2, UQ])
        heads1 = sb("heads1", [P, G, P])
        first_v = heads1[0:1].rearrange("p g n -> p (g n)").rearrange("p (b h d) -> p b h d", b=HB, h=H)
        logit = sb("logit", [P, B, E0])
        top8 = sb("top8", [P, B, 8])
        rmax = sb("rmax", [P, B])
        score = [sb(f"score{k}", [P, B, E0 + 8]) for k in range(2)]
        kept = sb("kept", [P, B, E0 + 8])
        tokw = sb("tokw", [P, B, E0])
        tokr = attn[:].rearrange("p b h d -> p (b h d)")[:, 0:2 * B * E0].rearrange("p (n b e) -> p n b e", n=2, b=B)
        wparts = sb("wparts", [P, B, P], BF16)
        wt_bf = sb("wt_bf", [P, T], BF16)
        exp_f = sb("exp_f", [P, 2, 2 * F1])
        exp_d = sb("exp_d", [P, 2, 3 * D])
        exp_hi = sb("exp_hi", [P, 2, 2 * F1], F32R)
        exp_lo = sb("exp_lo", [P, 2, 2 * F1], F32R)
        biases = sb("biases", [P, 2, E0])
        up_b = sb("up_b", [P, E0])

        vals_of = [vals[:], vals_half1[:]]
        k1 = k_st[:].rearrange("p g b k -> p g (b k)")
        room = sb("room", [P, 6, 1024])
        flat = room[:].rearrange("p a n -> p (a n)")
        qk_f = [flat[:, at:at + 1024].rearrange("p (w n) -> p w n", w=2) for at in (0, 4096)]
        probs = flat[:, 0:2048].rearrange("p (s c n) -> p s c n", s=2, c=2)
        heads_t = [flat[:, at:at + 2048].rearrange("p (g n) -> p g n", g=G) for at in (2048, 4096)]
        hprobs = flat[:, 0:3072].rearrange("p (s h q) -> p s h q", s=3, h=H)
        hsum = flat[:, 3072:4096].rearrange("p (s h q) -> p s h q", s=2, h=H // 2)
        gate_a, up_a = (room[:, n, :].rearrange("p (s n) -> p s n", s=2) for n in (2, 5))
        wbc = room[:, 0:2, :].rearrange("p a (s n) -> p (a s) n", s=2)
        act_f = room[:, 3:5, :].rearrange("p a (s n) -> p (a s) n", s=2)
        wt_f = x_f
        act_hi, act_lo, down_hi, down_lo = (q_blk[:, n] for n in range(4))
        glu1 = room[:, 1:3, :].rearrange("p a (s n) -> p (a s) n", s=2)
        acc_sb = x_f

        ident = cst[:, C_ID:C_ID + P]
        qsel, ksel = cst[:, C_QSEL:C_QSEL + 1], cst[:, C_KSEL:C_KSEL + 1]
        one_row = cst[0:1, C_ONE:C_ONE + P]
        gather = cst[:, C_GATHER:C_END].rearrange("p (g n) -> p g n", g=G)
        w = {n: small[:, W_AT[n]:W_AT[n] + W_WIDTH[n]] for n in W_NAMES}
        ln_g, ln_b = small[:, W_LN:W_LN + 1], small[:, W_LN + 1:W_LN + 2]
        wo1 = small[:, W_WO:W_END].rearrange("p (g n) -> p g n", g=G)

        def sems(prefix, names):
            return {n: sem(prefix + n) for n in names.split()}

        stored = sem("stored")
        came = sems("came_", "x qk cst ctx small late")
        LATE = 16 * 7
        ready = sems("ready_", "own blocks keys vals0 vals1 rest rezeroed tanh split qk_hi negid")
        a0 = sems("a0_", "var std norm xt ctxc xc clo lo v vcopy firstv first firstp firstb proj rnd stk "
                         "blk0 blk1 blk2 "
                         "blk3 qk max shift st exp pv ot gat recip heads var2 std2 norm2 t2 aff wp res chain")
        a1 = sems("a1_", "var std norm xt xc xlo v vcopy proj rnd stk blkv blks blk0 blk1 blk2 blk3 st max nm exp "
                         "pairs fours sum rec wtd wtp pv ot wo res chain")
        ffn = [sems(f"f{k}_", "var std norm xt xc lo logit lmax e wp wt wtc wdma0 wdma1 ddma0 ddma1 whi wlo gu wb wbc "
                              "glu glw act down acc tr res chain" +
                    (" wtf ga ua wfree", " dhi dlo ahi alo wlou")[k]) for k in range(2)]

        def moments(dve, s, chain, var):
            even, odd = stats[:, :, 1:3], stats[:, :, 4:6]
            chain.sync()
            chain.step(dve.tensor_tensor(mv[:, :, 0:2], even, odd, ALU.add))
            chain.step(dve.tensor_tensor(mv[:, :, 2], even[:, :, 0], odd[:, :, 0], ALU.subtract))
            chain.sync()
            chain.step(dve.tensor_scalar(mv[:, :, 1], mv[:, :, 1], 1.0 / D, LN_EPS, ALU.mult, ALU.add))
            chain.step(dve.scalar_tensor_tensor(mv[:, :, 2], mv[:, :, 2], 0.25, mv[:, :, 2], ALU.mult,
                                                ALU.mult))
            chain.step(dve.tensor_scalar(mv[:, :, 0], mv[:, :, 0], 0.5, None, ALU.mult))
            chain.sync()
            chain.step(dve.tensor_tensor(rvar[:], mv[:, :, 1], mv[:, :, 2], ALU.add))
            chain.sync()
            dve.reciprocal(rvar[:], rvar[:]).then_inc(s[var], 1)

        class Chain:

            def __init__(self, eng, counter):
                self.eng, self.counter, self.n = eng, counter, 0

            def step(self, ins):
                self.n += 1
                ins.then_inc(self.counter, 1)

            def sync(self):
                self.eng.wait_ge(self.counter, self.n)

        block = ctx.enter_context(nc.Block())

        SUPER = HALVES * G
        STEPS = SUPER * HB
        aux_at = {-1: [("piece", p) for p in range(4)], 5: [("turn", 0)], 9: [("values", 0)], 13: [("values", 1)],
                  19: [("gather", 0)], 21: [("gather", 1)]}
        for sg in range(1, SUPER):
            for kind, n in enumerate((HB * sg - 6, HB * sg - 5, HB * sg - 4)):
                if sg > 1 or kind:
                    aux_at[max(n, 0)] = aux_at.get(max(n, 0), []) + [("piece", 3 * sg + kind)]
        aux = [item for n in range(-1, STEPS) for item in aux_at.get(n, [])]

        def aux_bank(item):
            return aux.index(item) % 2

        def aux_read(item):
            kind, k = item
            return {"piece": (a0["stk"], k + 1), "turn": (a0["xc"], 4), "values": (a0["vcopy"], k + 3),
                    "gather": (a0["heads"], k + 1)}[kind]

        PIECES1 = [(what, half, g) for what, half in (("q", 0), ("k", 0), ("k", 1), ("q", 1)) for g in range(G)]

        BLOCKS1 = [(1, HB - 1)] + [(b, 1) for b in range(HB, B)]

        def bank1(n):
            return (6, 7, 0, 1)[n % 4] if n < 3 * G else 6 + n % 2

        def fetch_expert(sp, k, src, slot, what="both"):
            width, d_width = ((2 * F0, D), (2 * F1, 3 * D))[k]
            if what != "down":
                sp.dma_start(exp_f[:, slot, 0:width], src[:, 0:width]).then_inc(ffn[k][f"wdma{slot}"], 16)
            if what != "gate_up":
                sp.dma_start(exp_d[:, slot, 0:d_width],
                             src[:, width:width + d_width]).then_inc(ffn[k][f"ddma{slot}"], 16)

        @block.sync
        def _(sp):
            for dst, src, arrived in (
                    (resid[:], x.rearrange("b t d -> t b d"), "x"), (qk_f[0], qk_w[:, 0:2], "qk"),
                    (cst[:, 0:C_NEG], consts[:, 0:C_NEG], "cst"), (ctx_sb[:], ctx_t, "ctx"),
                    (small[:, 0:D], small_w[:, 0:D], "small"), (row[:], rows, "small"),
                    (cst[:, C_NEG:], consts[:, C_NEG:], "late"), (small[:, D:], small_w[:, D:], "late"),
                    (qk_f[1], qk_w[:, 2:4], "late"), (db0[:], down_bias, "late"), (biases[:], gu_bias, "late"),
                    (psel[:], part_sel, "late"), (idb[:], ident_bf, "late")):
                sp.dma_start(dst, src).then_inc(came[arrived], 16)
            for e in range(2):
                fetch_expert(sp, 0, experts0[e], e)

            def fetch_experts(k, experts, n):
                s = ffn[k]

                def gate_up(e, slot, src):
                    sp.wait_ge(s["wlo"], e - 1)
                    if k == 1:
                        sp.wait_ge(s["wlou"], e - 1)
                    fetch_expert(sp, k, src, slot, "gate_up")

                def down(e, slot, src):
                    sp.wait_ge(s[("wfree", "dlo")[k]], e - 1)
                    fetch_expert(sp, k, src, slot, "down")

                def source(at):
                    return experts[bass.ds(at, 1)].rearrange("e p n -> p (e n)")

                for e in (2, 3):
                    gate_up(e, e % 2, experts[e])
                turns = (n - 4) // 2
                with sp.Fori(0, turns) as i:
                    for slot in range(2):
                        down(i * 2 + slot + 2, slot, source(i * 2 + slot + 2))
                        gate_up(i * 2 + slot + 4, slot, source(i * 2 + slot + 4))
                for e in range(2 * turns + 2, n):
                    down(e, e % 2, experts[e])
                    if e + 2 < n:
                        gate_up(e + 2, e % 2, experts[e + 2])

            sp.wait_ge(ready["blocks"], 1)
            for sg in range(SUPER):
                sp.wait_ge(a0["stk"], 3 * sg + 1)
                if sg >= 2:
                    sp.wait_ge(a0["st"], 2 * HB * (sg - 1))
                for j in range(GH):
                    rows_j = slice(SLOT * j, SLOT * (j + 1))
                    sp.dma_start(q_blk[rows_j, sg % 2, j, :].bitcast(F32),
                                 q_st[rows_j, sg % G, :].bitcast(F32)).then_inc(a0[f"blk{sg % G}"], 16)
            fetch_experts(0, experts0, E0)
            sp.wait_ge(ready["rezeroed"], 1)
            for first, n in BLOCKS1:
                sp.wait_ge(a1["stk"], (1 if first < HB else 4) * G)
                if first >= HB:
                    sp.wait_ge(a1["st"], 2 * (first - HB) + 2)
                b = first % HB
                cols = slice(b * P, (b + n) * P)
                for j in range(GH):
                    rows_j = slice(SLOT * j, SLOT * (j + 1))
                    sp.dma_start(q_blk[rows_j, :, j, cols].bitcast(F32),
                                 q_st[rows_j, :, cols].bitcast(F32)).then_inc(a1[f"blk{b}"], 16)
            for e in range(2):
                sp.wait_ge(ffn[0]["down"], 2)
                fetch_expert(sp, 1, experts1[e], e)
            fetch_experts(1, experts1, E1 + 1)
            for h in range(HALVES):
                sp.wait_ge(ffn[1]["res"], h + 1)
                sp.dma_start(out.rearrange("b t d -> t b d")[:, HB * h:HB * (h + 1), :],
                             resid[:, HB * h:HB * (h + 1), :]).then_inc(stored, 16)
            sp.wait_ge(stored, 32)

        @block.gpsimd
        def _(pool):
            own = Chain(pool, ready["own"])
            own.step(pool.memset(ones[:].bitcast(F32), 1.0))
            pool.memset(k_st[:, :, :, 0:1].bitcast(F32), 0.0).then_inc(ready["keys"], 1)
            pool.memset(q_blk[:, 0:2].bitcast(F32), 0.0).then_inc(ready["blocks"], 1)
            for half, v in enumerate(vals_of):
                own.step(pool.memset(v, 0.0))
                own.sync()
                own.step(pool.memset(v[:, :, :, :, HD:HD + 1], 1.0))
                own.sync()
                pool.memset(v[0:1, 0, :, :, HD:HD + 1], 0.0).then_inc(ready[f"vals{half}"], 1)
                if half == 0:
                    pool.tensor_copy(ones_but0[:, 1:P], ones[:, 1:P].bitcast(F32))
                    pool.memset(ones_but0[:, 0:1].bitcast(F32), 0.0).then_inc(ready["keys"], 1)
            pool.memset(zero_r[:].bitcast(F32), 0.0)
            pool.memset(wparts[:], 0.0)
            for k, (e, top) in enumerate(((E0, TOP0), (E1, TOP1))):
                for n in range(8 - top):
                    ins = pool.memset(score[k][:, :, e + n:e + n + 1], -1.0 - n)
            ins.then_inc(ready["rest"], 1)
            pool.wait_ge(came["cst"], 16)
            for n in range(STEPS):
                pool.wait_ge(a0["max"], 2 * n + 2)
                if n >= SH:
                    pool.wait_ge(a0["st"], 2 * (n - SH + 1))
                pool.tensor_tensor(shift[:, n % SH], ident.unsqueeze(1).to_broadcast([P, GH, P]),
                                   neg_max[:, n % SH, :].unsqueeze(2).to_broadcast([P, GH, P]),
                                   ALU.mult).then_inc(a0["shift"], 1)
            pool.wait_ge(a0["pv"], STEPS)
            pool.memset(q_blk[:, 2:4].bitcast(F32), 0.0).then_inc(ready["rezeroed"], 1)

            def low_parts(s, e, slot, width):
                pool.wait_ge(s["whi"], e + 1)
                pool.tensor_tensor(exp_lo[:, slot, 0:width], exp_f[:, slot, 0:width],
                                   exp_hi[:, slot, 0:width].bitcast(F32), ALU.subtract).then_inc(s["wlo"], 1)

            def weigh(s, n, e, h, unit, at):
                pool.wait_ge(s["glu"], n + 1)
                pool.wait_ge(s["wbc"], e * 2 + h + 1)
                pool.tensor_tensor(unit, unit, wbc[0:unit.shape[0], at, :], ALU.mult).then_inc(s["glw"], 1)

            s = ffn[0]
            for e in range(2):
                low_parts(s, e, e, 2 * F0)

            def expert0(e, slot, last):
                for h in range(2):
                    weigh(s, e * 2 + h, e, h, gate_a[:, h, :], 2 * slot + h)
                if not last:
                    low_parts(s, e + 2, slot, 2 * F0)

            with pool.Fori(0, E0 // 2 - 1) as i:
                for slot in range(2):
                    expert0(i * 2 + slot, slot, False)
            for slot in range(2):
                expert0(E0 - 2 + slot, slot, True)
            s = a1

            def four_sums(u):
                pool.wait_ge(s["exp"], u + 1)
                if u >= 2:
                    pool.wait_ge(s["sum"], u - 1)
                pool.tensor_tensor(hsum[:, u % 2], hprobs[:, u % 3, 0:H // 2, :], hprobs[:, u % 3, H // 2:H, :],
                                   ALU.add).then_inc(s["pairs"], 1)
                pool.wait_ge(s["pairs"], u + 1)
                pool.tensor_tensor(hsum[:, u % 2, 0:H // 4, :], hsum[:, u % 2, 0:H // 4, :],
                                   hsum[:, u % 2, H // 4:H // 2, :], ALU.add).then_inc(s["fours"], 1)

            four_sums(0)
            for u in range(UNITS):
                if u + 1 < UNITS:
                    four_sums(u + 1)
                pool.wait_ge(s["rec"], u + 1)
                mine = hprobs[:, u % 3, H - POOL_HEADS:H, :]
                pool.tensor_tensor(mine, mine, hrec[:, u % 2, :].unsqueeze(1).to_broadcast([P, POOL_HEADS, UQ]),
                                   ALU.mult).then_inc(s["wtp"], 1)
            s = ffn[1]
            for e in range(2):
                low_parts(s, e, e, F1)
                pool.tensor_tensor(exp_lo[:, e, F1:], exp_f[:, e, F1:], exp_hi[:, e, F1:].bitcast(F32),
                                   ALU.subtract).then_inc(s["wlou"], 1)

            def expert1(e, slot, last):
                for h in range(2):
                    for c, (_, m) in enumerate(CH1):
                        n = h * 3 + c
                        weigh(s, e * 6 + n, e - 1, h, glu1[0:m, (6 * slot + n) % 4, :], h)
                if not last:
                    low_parts(s, e + 2, slot, F1)

            low_parts(s, 2, 0, F1)
            with pool.Fori(0, E1 // 2 - 1) as i:
                for slot in (1, 0):
                    expert1((i + 1 - slot) * 2 + slot, slot, False)
            for e in (E1 - 1, E1):
                expert1(e, e % 2, True)

        @block.scalar
        def _(act):
            def copy(dst, src):
                return act.activation(dst, src, ACT.Copy)

            act.preload_act_table(ACT.Sqrt)
            act.wait_ge(came["qk"], 16)
            copy(qk_hi[:, 0:2], qk_f[0]).then_inc(ready["qk_hi"], 1)

            def round_piece(s, n, bank):
                act.wait_ge(s["proj"], n + 1)
                if n >= 2:
                    act.wait_ge(s["stk"], n - 1)
                copy(rnd[:, n % 2, :], ps[:, bank, :]).then_inc(s["rnd"], 1)

            s = a0

            def context_high(half):
                cols = slice(half * HT, (half + 1) * HT)
                copy(c_hi[:, cols], ctx_sb[:, cols]).then_inc(s["ctxc"], 1)

            def tokens_copies(half, bank):
                cols = slice(half * HT, (half + 1) * HT)
                act.wait_ge(s["xt"], half + 1)
                copy(x_f[:, cols], ps[:, bank, :]).then_inc(s["xc"], 1)
                copy(x_hi[:, cols], ps[:, bank, :]).then_inc(s["xc"], 1)

            def copy_values(half, c, bank):
                act.wait_ge(s["v"], 2 * half + c + 1)
                copy(vals_of[half][:, c, :, :, 0:HD], ps[:, bank, :].rearrange("p (b h d) -> p b h d", b=HB, h=H)
                     ).then_inc(s["vcopy"], 1)

            act.wait_ge(s["var"], 1)
            act.activation(rstd[:], rvar[:], ACT.Sqrt).then_inc(s["std"], 1)
            act.preload_act_table(ACT.Exp)
            tokens_copies(0, 2)
            act.wait_ge(came["ctx"], 16)
            context_high(0)
            act.wait_ge(came["small"], 32)
            act.activation(tanh_gate[:], row[:, R_GATE:R_GATE + H], ACT.Tanh).then_inc(ready["tanh"], 1)
            round_piece(s, 0, 0)
            round_piece(s, 1, 1)
            act.wait_ge(ready["vals0"], 1)
            copy_values(0, 0, 3)
            round_piece(s, 2, 0)
            copy_values(0, 1, 4)
            round_piece(s, 3, 1)
            act.wait_ge(s["firstp"], 1)
            copy(first_b[:], ps[:, 5, :].rearrange("p (b d) -> p b d", b=HB)).then_inc(s["firstb"], 1)

            for n in range(STEPS):
                sg, b = divmod(n, HB)
                for c in range(2):
                    act.wait_ge(s["st"], 2 * n + c + 1)
                    if n >= 2:
                        act.wait_ge(s["pv"], n - 1)
                    act.activation(probs[:, n % 2, c, :], ps[:, 4 + c, :], ACT.Exp, scale=SCALE).then_inc(s["exp"], 1)
                for kind, k in aux_at.get(n, []):
                    if kind == "piece":
                        round_piece(s, k, aux_bank((kind, k)))
                    elif kind == "turn":
                        tokens_copies(1, aux_bank((kind, k)))
                    elif kind == "values":
                        if k == 0:
                            act.wait_ge(ready["vals1"], 1)
                        copy_values(1, k, aux_bank((kind, k)))
                if n == 3:
                    context_high(1)
                if n == 7:
                    act.wait_ge(came["late"], LATE)
                    copy(qk_hi[:, 2:4], qk_f[1]).then_inc(ready["qk_hi"], 1)
                if n == 14:
                    copy(negid[:], cst[:, C_NEG:C_NEG + P]).then_inc(ready["negid"], 1)
                if sg >= 1 and b == 1:
                    act.wait_ge(s["pv"], HB * sg)
                    copy(heads_t[(sg - 1) // G][:, (sg - 1) % G, :], ps[:, 6 + (sg - 1) % 2, :]).then_inc(s["ot"], 1)
            act.preload_act_table(ACT.Sqrt)
            act.wait_ge(s["pv"], STEPS)
            copy(heads_t[1][:, G - 1, :], ps[:, 6 + (SUPER - 1) % 2, :]).then_inc(s["ot"], 1)
            act.wait_ge(s["var2"], 1)
            act.activation(rstd[:], rvar[:], ACT.Sqrt).then_inc(s["std2"], 1)
            for half in range(HALVES):
                act.wait_ge(s["t2"], half + 1)
                act.activation(ln_t[:, half * HT:(half + 1) * HT], ps[:, 6 + half, :], ACT.Identity, bias=ln_b,
                               scale=ln_g).then_inc(s["aff"], 1)

            def ffn_prelude(s, k):
                width = 2 * (F0, F1)[k]
                for e in range(2):
                    act.wait_ge(s[f"wdma{e}"], 16)
                    copy(exp_hi[:, e, 0:width], exp_f[:, e, 0:width]).then_inc(s["whi"], 1)
                act.wait_ge(s["var"], 1)
                act.activation(rstd[:], rvar[:], ACT.Sqrt).then_inc(s["std"], 1)
                act.preload_act_table(ACT.Exp)
                for dst in (x_f, x_hi):
                    for half in range(HALVES):
                        act.wait_ge(s["xt"], half + 1)
                        copy(dst[:, half * HT:(half + 1) * HT], ps[:, half, :]).then_inc(s["xc"], 1)
                act.wait_ge(s["lmax"], 1)
                e = (E0, E1)[k]
                act.activation(logit[:, :, 0:e], logit[:, :, 0:e], ACT.Exp).then_inc(s["e"], 1)
                act.preload_act_table((ACT.Gelu_apprx_sigmoid, ACT.Silu)[k])

            def turned_weights(s, bank):
                act.wait_ge(s["wt"], 1)
                copy(wt_bf[:], ps[:, bank:bank + 2, :].rearrange("p k n -> p (k n)")).then_inc(s["wtc"], 1)

            def high_parts(s, i, slot, k, units):
                width = 2 * (F0, F1)[k]
                act.wait_ge(s[f"wdma{slot}"], (i + 2) * 16)
                act.wait_ge(s["gu"], (i * 2 + slot + 1) * units * 2)
                copy(exp_hi[:, slot, 0:width], exp_f[:, slot, 0:width]).then_inc(s["whi"], 1)

            def weights_copy(s, e, h, at):
                act.wait_ge(s["wb"], e * 2 + h + 1)
                copy(wbc[:, at, :], ps[:, 4 + h, :]).then_inc(s["wbc"], 1)

            def acc_copy(s):
                for h in range(2):
                    act.wait_ge(s["down"], h + 1)
                    copy(acc_sb[:, 512 * h:512 * (h + 1)], ps[:, 6 + h, :]).then_inc(s["acc"], 1)

            s = ffn[0]
            ffn_prelude(s, 0)
            turned_weights(s, 6)

            def expert0(i, slot, last):
                e = i * 2 + slot
                for h in range(2):
                    weights_copy(s, e, h, 2 * slot + h)
                    act.wait_ge(s["ga"], e * 2 + h + 1)
                    act.activation(gate_a[:, h, :], gate_a[:, h, :],
                                   ACT.Gelu_apprx_sigmoid).then_inc(s["glu"], 1)
                if not last:
                    high_parts(s, i, slot, 0, 2)

            with act.Fori(0, E0 // 2 - 1) as i:
                for slot in range(2):
                    expert0(i, slot, False)
            for slot in range(2):
                expert0(E0 // 2 - 1, slot, True)
            act.preload_act_table(ACT.Sqrt)
            acc_copy(s)
            s = a1

            def exponentials(u):
                act.wait_ge(s["nm"], u + 1)
                if u >= 3:
                    act.wait_ge(s["pv"], u - 2)
                act.activation(hprobs[:, u % 3].rearrange("p h q -> p (h q)"),
                               ps[:, 2 * (u % 3):2 * (u % 3) + 2, :].rearrange("p k n -> p (k n)"),
                               ACT.Exp, scale=SCALE).then_inc(s["exp"], 1)

            def weighted_values(b):
                act.wait_ge(s["pv"], 2 * b + 2)
                if b:
                    act.wait_ge(s["wo"], b)
                copy(heads1[:].rearrange("p g q -> p (g q)"), ps[:, 7, :]).then_inc(s["ot"], 1)

            for half in range(HALVES):
                act.wait_ge(s["v"], half + 1)
                copy(vals[:, half, :, :, 0:HD], ps[:, 4 + half, :].rearrange("p (b h d) -> p b h d", b=HB, h=H)
                     ).then_inc(s["vcopy"], 1)
            act.wait_ge(s["var"], 1)
            act.activation(rstd[:], rvar[:], ACT.Sqrt).then_inc(s["std"], 1)
            def tokens_high(half):
                act.wait_ge(s["xt"], half + 1)
                copy(x_hi[:, half * HT:(half + 1) * HT], ps[:, 2 + half, :]).then_inc(s["xc"], 1)

            tokens_high(0)
            for n in range(3 * G + 2):
                if n == 2 * G:
                    act.preload_act_table(ACT.Exp)
                round_piece(s, n, bank1(n))
                if n == G:
                    act.wait_ge(s["stk"], G)
                    act.wait_ge(ready["rezeroed"], 1)
                    for j in (2, 3):
                        rows_j = slice(SLOT * j, SLOT * (j + 1))
                        copy(q_blk[rows_j, :, j, 0:P], q_st[rows_j, :, 0:P].bitcast(F32)).then_inc(s["blks"], 1)
                    tokens_high(1)
            exponentials(0)
            for n in range(3 * G + 2, 4 * G):
                round_piece(s, n, bank1(n))
            exponentials(1)
            for u in range(UNITS):
                if u >= 2 and u % 2 == 0:
                    weighted_values(u // 2 - 1)
                if u + 2 < UNITS:
                    exponentials(u + 2)
            act.preload_act_table(ACT.Sqrt)
            weighted_values(B - 1)
            s = ffn[1]
            ffn_prelude(s, 1)

            def silu(e, slot, n):
                m = CH1[n % 3][1]
                act.wait_ge(s["gu"], (e * 6 + n) * 2 + 1)
                act.activation(glu1[0:m, (6 * slot + n) % 4, :], ps[0:m, n % 2, :],
                               ACT.Silu).then_inc(s["glu"], 1)

            def act_high(e, slot, n):
                m = CH1[n % 3][1]
                at = (6 * slot + n) % 4
                act.wait_ge(s["act"], e * 6 + n + 1)
                copy(act_hi[0:m, at, :], act_f[0:m, at, :]).then_inc(s["ahi"], 1)

            def down_high(i, slot):
                act.wait_ge(s[f"ddma{1 - slot}"], (i + slot + 1) * 16)
                copy(down_hi[:, 1 - slot, 0:3 * D], exp_d[:, 1 - slot, :]).then_inc(s["dhi"], 1)

            def expert1(i, slot, kind=""):
                e = i * 2 + slot
                for n in range(6):
                    act_high(e, slot, n)
                    if n == 1 and kind != "unweighted":
                        weights_copy(s, e - 1, 1, 1)
                    if n < 4:
                        silu(e, slot, n + 2)
                    if n == 3 and kind == "unweighted":
                        turned_weights(s, 4)
                    if n == 3 and kind != "last":
                        down_high(i, slot)
                        if kind != "next to last":
                            high_parts(s, i, slot, 1, 6)
                    if n == 4 and kind != "last":
                        weights_copy(s, e, 0, 0)
                    if n >= 4 and kind != "last":
                        silu(e + 1, 1 - slot, n - 4)

            act.wait_ge(s["ddma0"], 16)
            copy(down_hi[:, 0, 0:3 * D], exp_d[:, 0, :]).then_inc(s["dhi"], 1)
            for n in range(2):
                silu(0, 0, n)
            expert1(0, 0, "unweighted")
            with act.Fori(0, E1 // 2 - 1) as i:
                for slot in (1, 0):
                    expert1(i + 1 - slot, slot)
            expert1(E1 // 2 - 1, 1, "next to last")
            expert1(E1 // 2, 0, "last")
            acc_copy(s)

        @block.vector
        def _(dve):
            def normalised(s, src, tiles, std, done):
                dve.wait_ge(s[std], 1)
                for b in tiles:
                    dve.tensor_scalar(xn[:, b, :], src(b), mv[:, b, 0:1], rstd[:, b:b + 1], ALU.subtract,
                                      ALU.mult).then_inc(s[done], 1)

            s = a0
            chain = Chain(dve, s["chain"])

            def stack_piece(p, bank):
                sg, kind = divmod(p, 3)
                dve.wait_ge(s["rnd"], p + 1)
                src, hi = ps[:, bank, :], rnd[:, p % 2, :].bitcast(F32)
                if kind == 0:
                    if sg >= G:
                        dve.wait_ge(s[f"blk{sg % G}"], 16 * GH * (sg // G))
                    ins = dve.scalar_tensor_tensor(q_st[:, sg % G, :], hi, qsel, src, ALU.mult, ALU.add)
                else:
                    lead = 1 if kind == 1 else 0
                    at = (kind - 1) * P
                    ins = dve.scalar_tensor_tensor(
                        k_st[:, sg % G, :, at + lead:at + P],
                        hi.rearrange("p (b k) -> p b k", b=HB)[:, :, lead:], ksel,
                        src.rearrange("p (b k) -> p b k", b=HB)[:, :, lead:], ALU.mult, ALU.add)
                ins.then_inc(s["stk"], 1)

            def context_low(half):
                cols = slice(half * HT, (half + 1) * HT)
                dve.wait_ge(s["ctxc"], half + 1)
                dve.tensor_tensor(c_lo[:, cols], ctx_sb[:, cols], c_hi[:, cols].bitcast(F32),
                                  ALU.subtract).then_inc(s["clo"], 1)

            def tokens_low(half):
                cols = slice(half * HT, (half + 1) * HT)
                dve.wait_ge(s["xc"], 2 * half + 2)
                dve.tensor_tensor(x_lo[:, cols], x_f[:, cols], x_hi[:, cols].bitcast(F32),
                                  ALU.subtract).then_inc(s["lo"], 1)

            def first_values(half):
                v = vals_of[half][0:1, 0, :, :, 0:HD]
                dve.wait_ge(s["vcopy"], 2 * half + 1)
                if half:
                    dve.wait_ge(s["firstp"], half)
                dve.tensor_tensor(first_v, v, tanh_gate[:].unsqueeze(1).unsqueeze(3).to_broadcast(
                    [1, HB, H, HD]), ALU.mult).then_inc(s["firstv"], 1)
                dve.wait_ge(s["firstv"], half + 1)
                dve.memset(v, 0.0).then_inc(s["first"], 1)

            def gathered(src, batches, sums, n):
                dve.reciprocal(rsum[:, batches], sums).then_inc(s["recip"], 1)
                dve.wait_ge(s["recip"], n)
                ins = dve.tensor_tensor(attn[:, batches], src.rearrange("p b (h d) -> p b h d", h=H),
                                        rsum[:, batches].unsqueeze(3).to_broadcast(
                                            [P, batches.stop - batches.start, H, HD]), ALU.mult)
                ins.then_inc(s["heads"], 1)
                dve.wait_ge(s["heads"], n)

            dve.wait_ge(came["x"], 16)
            for b in range(B):
                chain.step(dve.bn_stats(stats[:, b, :], resid[:, b, :]))
            moments(dve, s, chain, "var")
            dve.wait_ge(ready["qk_hi"], 1)
            dve.tensor_tensor(qk_lo[:, 0:2], qk_f[0], qk_hi[:, 0:2].bitcast(F32),
                              ALU.subtract).then_inc(ready["split"], 1)
            normalised(s, lambda b: resid[:, b, :], range(HB), "std", "norm")
            tokens_low(0)
            context_low(0)
            dve.wait_ge(came["cst"], 16)
            dve.wait_ge(ready["keys"], 1)
            stack_piece(0, 0)
            stack_piece(1, 1)
            dve.wait_ge(ready["tanh"], 1)
            first_values(0)
            stack_piece(2, 0)
            stack_piece(3, 1)

            for n in range(STEPS):
                for u in range(2):
                    dve.wait_ge(s["qk"], 2 * n + u + 1)
                    if n >= SH:
                        dve.wait_ge(s["shift"], n - SH + 1)
                    dve.tensor_reduce(neg_max[:, n % SH, 2 * u:2 * u + 2],
                                      ps[:, 2 + u, :].rearrange("p (j k) -> p j k", j=2)[:, :, 1:],
                                      AX_X, ALU.max, negate=True).then_inc(s["max"], 1)
                if n == 2:
                    normalised(s, lambda b: resid[:, b, :], range(HB, B), "std", "norm")
                for kind, k in aux_at.get(n - 2, []) if n >= 2 else []:
                    bank = aux_bank((kind, k))
                    if kind == "piece":
                        stack_piece(k, bank)
                    elif kind == "turn":
                        tokens_low(1)
                    elif kind == "values" and k == 0:
                        first_values(1)
                    elif kind == "gather":
                        dve.wait_ge(s["gat"], k + 1)
                        two = ps[:, bank, 0:2 * OUTW].rearrange("p (b n) -> p b n", b=2)
                        gathered(two[:, :, 0:D], slice(2 * k, 2 * k + 2), two[:, :, D:OUTW], k + 1)
                        if k == 0:
                            dve.wait_ge(s["firstb"], 1)
                        chain.step(dve.tensor_tensor(attn_bf[:, 2 * k:2 * k + 2],
                                                     attn[:, 2 * k:2 * k + 2].rearrange("p b h d -> p b (h d)"),
                                                     first_b[:, 2 * k:2 * k + 2], ALU.add))
                        chain.sync()
                        for b in (2 * k, 2 * k + 1):
                            chain.step(dve.bn_stats(stats[:, b, :], attn_bf[:, b, :]))
                if n == 5:
                    context_low(1)
                if n == 9:
                    dve.wait_ge(ready["qk_hi"], 2)
                    dve.tensor_tensor(qk_lo[:, 2:4], qk_f[1], qk_hi[:, 2:4].bitcast(F32),
                                      ALU.subtract).then_inc(ready["split"], 1)
                    dve.tensor_scalar(up_b[:], biases[:, 1, :], 1.0, None, ALU.add)
            for k in range(2):
                two = slice(2 * k, 2 * k + 2)
                dve.wait_ge(s["gat"], 2 + 2 * k + 2)
                gathered(ps[:, 2 + 2 * k:4 + 2 * k, 0:D], two, ps[:, 2 + 2 * k:4 + 2 * k, D:OUTW], 3 + k)
                if k == 0:
                    dve.wait_ge(s["firstp"], 2)
                chain.step(dve.tensor_tensor(
                    attn_bf[:, HB + 2 * k:HB + 2 * k + 2], attn[:, two].rearrange("p b h d -> p b (h d)"),
                    ps[:, 0, 2 * k * D:2 * (k + 1) * D].rearrange("p (b d) -> p b d", b=2), ALU.add))
                chain.sync()
                for b in (HB + 2 * k, HB + 2 * k + 1):
                    chain.step(dve.bn_stats(stats[:, b, :], attn_bf[:, b, :]))
            moments(dve, s, chain, "var2")
            normalised(s, lambda b: attn_bf[:, b, :], range(B), "std2", "norm2")
            def add_half(s, done, half, bank, chain):
                dve.wait_ge(s[done], half + 1)
                tiles = resid[:, half * HB:(half + 1) * HB, :]
                dve.tensor_tensor(tiles, tiles, ps[:, bank, :].rearrange("p (b d) -> p b d", b=HB),
                                  ALU.add).then_inc(s["res"], 1)
                dve.wait_ge(s["res"], half + 1)
                for b in range(half * HB, (half + 1) * HB):
                    chain.step(dve.bn_stats(stats[:, b, :], resid[:, b, :]))

            chain = Chain(dve, ffn[0]["chain"])
            for half in range(HALVES):
                add_half(a0, "wp", half, 2 + half, chain)

            def ffn_prelude(s, k, chain, between=()):
                e, top = ((E0, TOP0), (E1, TOP1))[k]
                fill = 8 - top
                moments(dve, s, chain, "var")
                normalised(s, lambda b: resid[:, b, :], range(B), "std", "norm")
                if k == 0:
                    dve.wait_ge(ready["rest"], 1)
                for half in range(HALVES):
                    cols = slice(half * HT, (half + 1) * HT)
                    dve.wait_ge(s["xc"], half + 3)
                    dve.tensor_tensor(x_lo[:, cols], x_f[:, cols], x_hi[:, cols].bitcast(F32),
                                      ALU.subtract).then_inc(s["lo"], 1)
                dve.wait_ge(s["logit"], 1)
                lg = ps[:, 4, 0:B * e].rearrange("p (t e) -> p t e", t=B)
                chain.step(dve.tensor_reduce(rmax[:], lg, AX_X, ALU.max))
                chain.sync()
                dve.tensor_tensor(logit[:, :, 0:e], lg, rmax[:].unsqueeze(2).to_broadcast([P, B, e]),
                                  ALU.subtract).then_inc(s["lmax"], 1)
                dve.wait_ge(s["e"], 1)
                chain.step(dve.tensor_reduce(rmax[:], logit[:, :, 0:e], AX_X, ALU.add))
                chain.sync()
                chain.step(dve.reciprocal(rmax[:], rmax[:]))
                chain.sync()
                sc = score[k]
                chain.step(dve.tensor_tensor(sc[:, :, 0:e], logit[:, :, 0:e],
                                             rmax[:].unsqueeze(2).to_broadcast([P, B, e]), ALU.mult))
                chain.sync()
                for t in range(B):
                    chain.step(dve.max(top8[:, t, :], sc[:, t, 0:e]))
                chain.sync()
                chain.step(dve.tensor_copy(top8[:, :, top:8], sc[:, :, e:e + fill]))
                chain.sync()
                for t in range(B):
                    chain.step(dve.match_replace(kept[:, t, 0:e + fill], top8[:, t, :], sc[:, t, 0:e + fill], 0.0))
                chain.sync()
                for step in between[0:1]:
                    step()
                chain.step(dve.tensor_tensor(tokw[:, :, 0:e], sc[:, :, 0:e], kept[:, :, 0:e], ALU.subtract))
                chain.sync()
                if k == 1:
                    chain.step(dve.tensor_reduce(rmax[:], tokw[:, :, 0:e], AX_X, ALU.add))
                    chain.sync()
                    chain.step(dve.reciprocal(rmax[:], rmax[:]))
                    chain.sync()
                    chain.step(dve.tensor_tensor(tokw[:, :, 0:e], tokw[:, :, 0:e],
                                                 rmax[:].unsqueeze(2).to_broadcast([P, B, e]), ALU.mult))
                    chain.sync()
                for step in between[1:]:
                    step()
                left = tokw[:, :, 0:e]
                for part in range(PARTS):
                    cols = wparts[:, :, E0 * part:E0 * part + e]
                    ins = dve.tensor_copy(cols, left)
                    if part == PARTS - 1:
                        ins.then_inc(s["wp"], 1)
                        break
                    chain.step(ins)
                    chain.sync()
                    chain.step(dve.tensor_tensor(tokr[:, part, :, 0:e], left, cols, ALU.subtract))
                    chain.sync()
                    left = tokr[:, part, :, 0:e]

            s = ffn[0]
            ffn_prelude(s, 0, chain)

            def clamp0(e, h, first=False):
                at = bass.ds(e, 1)
                if not first:
                    dve.wait_ge(s["act"], e * 2 + h - 1)
                dve.wait_ge(s["gu"], (e * 2 + h) * 2 + 1)
                dve.tensor_scalar(gate_a[:, h, :], ps[:, h, :], biases[:, 0, at], LIMIT, ALU.add,
                                  ALU.min).then_inc(s["ga"], 1)
                dve.wait_ge(s["gu"], (e * 2 + h) * 2 + 2)
                dve.tensor_scalar(up_a[:, h, :], ps[:, 2 + h, :], up_b[:, at], LIMIT + 1.0, ALU.add,
                                  ALU.min).then_inc(s["ua"], 1)

            def activate0(e, slot, h):
                dve.wait_ge(s["glw"], e * 2 + h + 1)
                dve.wait_ge(s["ua"], e * 2 + h + 1)
                dve.scalar_tensor_tensor(act_f[:, 2 * slot + h, :], up_a[:, h, :], 1.0 - LIMIT,
                                         gate_a[:, h, :], ALU.max, ALU.mult).then_inc(s["act"], 1)

            def expert0(e, slot, last):
                for h in range(2):
                    activate0(e, slot, h)
                    if not last:
                        clamp0(e + 1, h)

            for h in range(2):
                clamp0(0, h, True)
            dve.wait_ge(s["wtc"], 1)
            dve.tensor_copy(wt_f[:], ps[:, 6:8, :].rearrange("p k n -> p (k n)")).then_inc(s["wtf"], 1)
            with dve.Fori(0, E0 // 2 - 1) as i:
                for slot in range(2):
                    expert0(i * 2 + slot, slot, False)
            for slot in range(2):
                expert0(E0 - 2 + slot, slot, slot == 1)
            chain = Chain(dve, a1["chain"])
            for half in range(HALVES):
                add_half(s, "tr", half, half, chain)
            s = a1

            def stack1(n):
                what, half, g = PIECES1[n]
                dve.wait_ge(s["rnd"], n + 1)
                if what == "q" and half == 1 and g == 0:
                    dve.wait_ge(s["blks"], 2)
                    dve.wait_ge(s["blk1"], 16 * GH)
                dst, sel = (q_st[:, g, :], qsel) if what == "q" else (k1[:, g, half * HT:(half + 1) * HT], ksel)
                dve.scalar_tensor_tensor(dst, rnd[:, n % 2, :].bitcast(F32), sel, ps[:, bank1(n), :], ALU.mult,
                                         ALU.add).then_inc(s["stk"], 1)

            def head_max(u):
                dve.wait_ge(s["st"], u + 1)
                if u >= 2:
                    dve.wait_ge(s["nm"], u - 1)
                scores = ps[:, 2 * (u % 3):2 * (u % 3) + 2, :].rearrange("p k (a q) -> p q (k a)", q=UQ)
                dve.tensor_reduce(hmax[:, u % 2, :], scores, AX_X, ALU.max).then_inc(s["max"], 1)

            def add_batch(b):
                dve.wait_ge(s["wo"], b + 1)
                dve.tensor_tensor(resid[:, b, :], resid[:, b, :], ps[:, 6, 0:D], ALU.add).then_inc(s["res"], 1)
                dve.wait_ge(s["res"], b + 1)
                chain.step(dve.bn_stats(stats[:, b, :], resid[:, b, :]))

            moments(dve, s, chain, "var")
            normalised(s, lambda b: resid[:, b, :], range(B), "std", "norm")
            chain = Chain(dve, ffn[1]["chain"])

            def tokens_low1(half):
                dve.wait_ge(s["xc"], half + 1)
                cols = slice(half * HT, (half + 1) * HT)
                dve.tensor_tensor(x_lo[:, cols], ps[:, 2 + half, :], x_hi[:, cols].bitcast(F32),
                                  ALU.subtract).then_inc(s["xlo"], 1)

            tokens_low1(0)
            for n in range(3 * G):
                stack1(n)
                if n == G - 1:
                    dve.wait_ge(ready["rezeroed"], 1)
                    dve.wait_ge(s["stk"], G)
                    for j in (0, 1):
                        rows_j = slice(SLOT * j, SLOT * (j + 1))
                        dve.tensor_copy(q_blk[rows_j, :, j, 0:P],
                                        q_st[rows_j, :, 0:P].bitcast(F32)).then_inc(s["blkv"], 1)
                if n == G:
                    tokens_low1(1)
            head_max(0)
            head_max(1)
            for n in range(3 * G, 4 * G):
                stack1(n)
            for u in range(UNITS):
                if u + 2 < UNITS:
                    head_max(u + 2)
                dve.wait_ge(s["sum"], u + 1)
                if u >= 2:
                    dve.wait_ge(s["wtp"], u - 1)
                dve.reciprocal(hrec[:, u % 2, :], ps[:, 2 * (u % 3), 0:UQ]).then_inc(s["rec"], 1)
                dve.wait_ge(s["rec"], u + 1)
                mine = hprobs[:, u % 3, 0:H - POOL_HEADS, :]
                dve.tensor_tensor(mine, mine,
                                  hrec[:, u % 2, :].unsqueeze(1).to_broadcast([P, H - POOL_HEADS, UQ]),
                                  ALU.mult).then_inc(s["wtd"], 1)
                if u >= 3 and u % 2 == 1:
                    add_batch((u - 3) // 2)
            add_batch(B - 1)
            s = ffn[1]
            def activate1(e, slot, n, routed):
                m, at = CH1[n % 3][1], (6 * slot + n) % 4
                dve.wait_ge(s["gu"], (e * 6 + n) * 2 + 2)
                if routed:
                    dve.wait_ge(s["glw"], (e - 1) * 6 + n + 1)
                else:
                    dve.wait_ge(s["glu"], e * 6 + n + 1)
                dve.tensor_tensor(act_f[0:m, at, :], glu1[0:m, at, :], ps[0:m, 2 + n % 2, :],
                                  ALU.mult).then_inc(s["act"], 1)

            def act_low(e, slot, n):
                m, at = CH1[n % 3][1], (6 * slot + n) % 4
                dve.wait_ge(s["ahi"], e * 6 + n + 1)
                dve.tensor_tensor(act_lo[0:m, at, :], act_f[0:m, at, :], act_hi[0:m, at, :].bitcast(F32),
                                  ALU.subtract).then_inc(s["alo"], 1)

            def up_low(e, slot):
                dve.wait_ge(s["whi"], e + 1)
                dve.tensor_tensor(exp_lo[:, slot, F1:], exp_f[:, slot, F1:], exp_hi[:, slot, F1:].bitcast(F32),
                                  ALU.subtract).then_inc(s["wlou"], 1)

            def down_low(e, slot):
                dve.wait_ge(s["dhi"], e + 1)
                dve.tensor_tensor(down_lo[:, slot, 0:3 * D], exp_d[:, slot, :],
                                  down_hi[:, slot, 0:3 * D].bitcast(F32), ALU.subtract).then_inc(s["dlo"], 1)

            def expert1(e, slot, kind="", first=0):
                for n in range(first, 6):
                    if n < 5:
                        activate1(e, slot, n + 1, kind != "unweighted")
                    elif kind != "last":
                        activate1(e + 1, 1 - slot, 0, True)
                    act_low(e, slot, n)
                    if n == 4 and kind != "last":
                        down_low(e + 1, 1 - slot)
                    if n == 5 and kind in ("", "unweighted"):
                        up_low(e + 2, slot)

            def first_low():
                down_low(0, 0)
                act_low(0, 0, 0)

            ffn_prelude(s, 1, chain, (lambda: activate1(0, 0, 0, False), lambda: activate1(0, 0, 1, False), first_low))
            expert1(0, 0, "unweighted", 1)
            with dve.Fori(0, E1 // 2 - 1) as i:
                for slot in (1, 0):
                    expert1((i + 1 - slot) * 2 + slot, slot)
            expert1(E1 - 1, 1, "next to last")
            expert1(E1, 0, "last")
            for half in range(HALVES):
                dve.wait_ge(s["tr"], half + 1)
                tiles = resid[:, half * HB:(half + 1) * HB, :]
                dve.tensor_tensor(tiles, tiles, ps[:, half, :].rearrange("p (b d) -> p b d", b=HB),
                                  ALU.add).then_inc(s["res"], 1)

        @block.tensor
        def _(pe):
            def mm(dst, lhs, rhs, start=True, stop=True):
                return pe.matmul(dst, lhs, rhs, start=start, stop=stop, skip_group_check=True)

            def three_pass(dst, lhs_hi, lhs_lo, rhs_hi, rhs_lo):
                mm(dst, lhs_hi, rhs_hi, True, False)
                mm(dst, lhs_hi, rhs_lo, False, False)
                return mm(dst, lhs_lo, rhs_hi, False, True)

            def turn(s, count, src, n, bank, done, first=0):
                for b in range(first, first + n):
                    pe.wait_ge(s[count], b + 1)
                    ins = pe.transpose(ps[:, bank + (b - first) // 4, (b % 4) * P:(b % 4 + 1) * P], src[:, b, :], ident)
                ins.then_inc(s[done], 1)

            s = a0

            def values(half, c, bank):
                src = (ctx_sb, x_f)[c]
                for b in range(HB):
                    at = (half * HB + b) * P
                    ins = mm(ps[:, bank, b * P:(b + 1) * P], src[:, at:at + P], w["wv0"])
                ins.then_inc(s["v"], 1)

            def project_piece(p, bank):
                sg, kind = divmod(p, 3)
                half, g = divmod(sg, G)
                tokens = slice(half * HT, (half + 1) * HT)
                if g == 0 and kind == 0:
                    pe.wait_ge(s["lo"], half + 1)
                if g == 0 and kind == 1:
                    pe.wait_ge(s["clo"], half + 1)
                which, hi, lo = ((0, x_hi, x_lo), (1, c_hi, c_lo), (1, x_hi, x_lo))[kind]
                cols = slice(g * P, (g + 1) * P)
                three_pass(ps[:, bank, :], qk_hi[:, which, cols], qk_lo[:, which, cols], hi[:, tokens],
                           lo[:, tokens]).then_inc(s["proj"], 1)

            def key0_values(half, bank):
                pe.wait_ge(s["firstv"], half + 1)
                mm(ps[:, bank, :], one_row, first_v.rearrange("p b h d -> p (b h d)")).then_inc(s["firstp"], 1)

            def scores_by_query(n):
                sg, b = divmod(n, HB)
                if b == 0:
                    pe.wait_ge(s["stk"], 3 * sg + 3)
                    pe.wait_ge(s[f"blk{sg % G}"], 16 * GH * (sg // G + 1))
                for u in range(2):
                    if n >= 1:
                        pe.wait_ge(s["max"], 2 * (n - 1) + u + 1)
                    for j in (2 * u, 2 * u + 1):
                        ins = mm(ps[:, 2 + u, (j % 2) * KEYS:(j % 2 + 1) * KEYS],
                                 q_blk[:, sg % 2, j, b * P:(b + 1) * P], k_st[:, sg % G, b, :])
                    ins.then_inc(s["qk"], 1)

            def scores_by_key(n):
                sg, b = divmod(n, HB)
                for c in range(2):
                    if n >= 1:
                        pe.wait_ge(s["exp"], 2 * (n - 1) + c + 1)
                    mm(ps[:, 4 + c, :].rearrange("p (j q) -> p j q", j=GH), k_st[:, sg % G, b, c * P:(c + 1) * P],
                       q_blk[:, sg % 2, :, b * P:(b + 1) * P], True, False)
                    if c == 0:
                        pe.wait_ge(s["shift"], n + 1)
                    mm(ps[:, 4 + c, :].rearrange("p (j q) -> p j q", j=GH), (ones_but0, ones)[c][:],
                       shift[:, n % SH], False, True).then_inc(s["st"], 1)

            def weigh_values(n):
                sg, b = divmod(n, HB)
                if b == 0 and sg >= 2:
                    pe.wait_ge(s["ot"], sg - 1)
                if n == G * HB:
                    pe.wait_ge(s["vcopy"], 4)
                    pe.wait_ge(s["first"], 2)
                for c in range(2):
                    pe.wait_ge(s["exp"], 2 * n + c + 1)
                    for j in range(GH):
                        ins = mm(ps[SLOT * j:SLOT * (j + 1), 6 + sg % 2, b * P:(b + 1) * P],
                                 vals_of[sg // G][:, c, b, GH * (sg % G) + j, :], probs[:, n % 2, c, j * P:(j + 1) * P],
                                 c == 0, c == 1)
                ins.then_inc(s["pv"], 1)

            def gather_heads(half, b, dst):
                for g in range(G):
                    ins = mm(dst, heads_t[half][:, g, b * P:(b + 1) * P], gather[:, g, :], g == 0, g == G - 1)
                return ins

            pe.wait_ge(came["cst"], 16)
            turn(s, "norm", xn, HB, 2, "xt")
            pe.wait_ge(ready["split"], 1)
            project_piece(0, 0)
            project_piece(1, 1)
            pe.wait_ge(came["small"], 32)
            values(0, 0, 3)
            pe.wait_ge(*aux_read(("piece", 0)))
            project_piece(2, 0)
            values(0, 1, 4)
            pe.wait_ge(*aux_read(("piece", 1)))
            project_piece(3, 1)
            key0_values(0, 5)
            pe.wait_ge(ready["keys"], 2)
            pe.wait_ge(s["xc"], 2)
            pe.wait_ge(s["vcopy"], 1)
            scores_by_query(0)
            scores_by_query(1)
            pe.wait_ge(s["vcopy"], 2)
            pe.wait_ge(s["firstb"], 1)
            pe.wait_ge(s["first"], 1)
            for n in range(STEPS):
                if n + 2 < STEPS:
                    scores_by_query(n + 2)
                scores_by_key(n)
                for item in aux_at.get(n, []):
                    kind, k = item
                    bank = aux_bank(item)
                    pe.wait_ge(*aux_read(aux[aux.index(item) - 2]))
                    if kind == "piece":
                        project_piece(k, bank)
                    elif kind == "turn":
                        turn(s, "norm", xn, HB, bank, "xt", HB)
                    elif kind == "values":
                        values(1, k, bank)
                    else:
                        pe.wait_ge(s["ot"], G)
                        for b in (2 * k, 2 * k + 1):
                            ins = gather_heads(0, b, ps[:, bank, (b % 2) * OUTW:(b % 2 + 1) * OUTW])
                        ins.then_inc(s["gat"], 1)
                if n >= 1:
                    weigh_values(n - 1)
            weigh_values(STEPS - 1)
            pe.wait_ge(s["stk"], 3 * SUPER)
            key0_values(1, 0)
            pe.wait_ge(s["max"], 2 * STEPS)
            pe.wait_ge(s["ot"], SUPER)
            for b in range(HB):
                gather_heads(1, b, ps[:, 2 + b, 0:OUTW]).then_inc(s["gat"], 1)
            pe.wait_ge(s["heads"], 4)
            for half in range(HALVES):
                mm(ps[:, 2 + half, :], one_row, row[:, R_BP:R_BP + HB * D], True, False)
            for half in range(HALVES):
                turn(s, "norm2", xn, HB, 6 + half, "t2", half * HB)
            for half in range(HALVES):
                pe.wait_ge(s["aff"], half + 1)
                for b in range(HB):
                    at = (half * HB + b) * P
                    ins = mm(ps[:, 2 + half, b * P:(b + 1) * P], ln_t[:, at:at + P], w["wp0"], False, True)
                ins.then_inc(s["wp"], 1)

            def route(s, k):
                e = (E0, E1)[k]
                for half in range(HALVES):
                    turn(s, "norm", xn, HB, half, "xt", half * HB)
                if k == 0:
                    mm(ps[:, 4, 0:B * e], one_row, row[:, R_RB:R_END], True, False)
                for t in range(B):
                    pe.wait_ge(s["xc"], t // HB + 1)
                    ins = mm(ps[:, 4, t * e:(t + 1) * e], x_f[:, t * P:(t + 1) * P], w[("rw0", "gw1")[k]], k == 1)
                ins.then_inc(s["logit"], 1)
                pe.wait_ge(s["xc"], 4)
                pe.wait_ge(s["lo"], 2)

            def turn_weights(s, bank):
                pe.wait_ge(s["wp"], 1)
                for t in range(B):
                    ins = mm(ps[:, bank + t // 4, (t % 4) * P:(t % 4 + 1) * P], wparts[:, t, :], idb[:])
                ins.then_inc(s["wt"], 1)

            def first_products(s, k):
                if k == 0:
                    pe.wait_ge(s["wtf"], 1)
                for h in range(2):
                    if k == 0:
                        mm(ps[:, 6 + h, :], db0[:], wt_f[:, h * 512:(h + 1) * 512], True, False)
                    else:
                        mm(ps[:, 6 + h, :], zero_r[:], x_hi[:, 0:512], True, False)

            def gate_up(s, slot, gate, up, m, h, bank, gate_read=None, up_read=None):
                hi, lo = exp_hi, exp_lo
                tokens = slice(h * 512, (h + 1) * 512)
                for at, b0, read in ((gate, 0, gate_read), (up, 2, up_read)):
                    if read is not None:
                        pe.wait_ge(*read)
                    cols = slice(at, at + m)
                    three_pass(ps[0:m, b0 + bank, :], hi[:, slot, cols], lo[:, slot, cols], x_hi[:, tokens],
                               x_lo[:, tokens]).then_inc(s["gu"], 1)

            def spread_weights(s, e, h):
                mm(ps[:, 4 + h, :], psel[:, bass.ds(e, 1), :].rearrange("p o m -> p (o m)"),
                   wt_bf[:, h * 512:(h + 1) * 512]).then_inc(s["wb"], 1)

            def ffn_end(s):
                for h in range(2):
                    pe.wait_ge(s["acc"], h + 1)
                    for b in range(4):
                        ins = pe.transpose(ps[:, h, b * P:(b + 1) * P],
                                           acc_sb[:, (4 * h + b) * P:(4 * h + b + 1) * P], ident)
                    ins.then_inc(s["tr"], 1)

            s = ffn[0]
            route(s, 0)

            def gates0(e, slot, h, first):
                if h == 0:
                    pe.wait_ge(s["wlo"], e + 1)
                read = None if first else (s["ua"], (e - 1) * 2 + h + 1)
                gate_up(s, slot, 0, F0, F0, h, h, read)

            def down0(e, i, slot, h, final):
                if h == 0:
                    pe.wait_ge(s[f"ddma{slot}"], i * 16 + 16)
                pe.wait_ge(s["act"], e * 2 + h + 1)
                ins = mm(ps[:, 6 + h, :], exp_d[:, slot, 0:D], act_f[:, 2 * slot + h, :], False, final)
                if final:
                    ins.then_inc(s["down"], 1)
                elif h == 1:
                    ins.then_inc(s["wfree"], 1)

            def expert0(i, slot, last):
                e = i * 2 + slot
                for h in range(2):
                    if not last:
                        gates0(e + 1, 1 - slot, h, False)
                        pe.wait_ge(s["wbc"], e * 2 + h + 1)
                        spread_weights(s, e + 1, h)
                    down0(e, i, slot, h, last)

            for h in range(2):
                gates0(0, 0, h, True)
            turn_weights(s, 6)
            pe.wait_ge(s["wtc"], 1)
            for h in range(2):
                spread_weights(s, 0, h)
            first_products(s, 0)
            with pe.Fori(0, E0 // 2 - 1) as i:
                for slot in range(2):
                    expert0(i, slot, False)
            for slot in range(2):
                expert0(E0 // 2 - 1, slot, slot == 1)
            ffn_end(s)
            s = a1

            def project1(n):
                what, half, g = PIECES1[n]
                tokens = slice(half * HT, (half + 1) * HT)
                if n >= 4:
                    pe.wait_ge(s["stk"], n - 3 if n < 3 * G else n - 1)
                if what == "k":
                    which, hi, lo = 3, c_hi[:, tokens], c_lo[:, tokens]
                else:
                    which, hi, lo = 2, x_hi[:, tokens], x_lo[:, tokens]
                    if g == 0:
                        pe.wait_ge(s["xlo"], half + 1)
                cols = slice(g * P, (g + 1) * P)
                three_pass(ps[:, bank1(n), :], qk_hi[:, which, cols], qk_lo[:, which, cols],
                           hi, lo).then_inc(s["proj"], 1)

            def head_scores(u):
                b, r = divmod(u, 2)
                if u == 0:
                    pe.wait_ge(s["blkv"], 2)
                    pe.wait_ge(s["blks"], 2)
                    pe.wait_ge(s["stk"], 3 * G)
                    pe.wait_ge(s["xlo"], 2)
                for turn_of, (first, n) in enumerate(BLOCKS1):
                    if r == 0 and b == first:
                        earlier = sum(f % HB == b % HB for f, _ in BLOCKS1[:turn_of])
                        pe.wait_ge(s[f"blk{b % HB}"], 16 * GH * (earlier + 1))
                if u >= 3:
                    pe.wait_ge(s["rec"], u - 2)
                at = (b % HB) * P + r * UQ
                for g in range(G):
                    ins = mm(ps[:, 2 * (u % 3) + g // 2, (g % 2) * GH * UQ:(g % 2 + 1) * GH * UQ
                                ].rearrange("p (j q) -> p j q", j=GH),
                             k1[:, g, b * P:(b + 1) * P], q_blk[:, g, :, at:at + UQ], g % 2 == 0, False)
                ins.then_inc(s["st"], 1)

            def less_max(u):
                pe.wait_ge(s["max"], u + 1)
                for k in range(2):
                    ins = mm(ps[:, 2 * (u % 3) + k, :].rearrange("p (a q) -> p a q", q=UQ), negid[:],
                             hmax[:, u % 2, :].unsqueeze(1).to_broadcast([P, H // 2, UQ]), False, True)
                ins.then_inc(s["nm"], 1)

            def head_sum(u):
                pe.wait_ge(s["fours"], u + 1)
                for h in range(H // 4):
                    ins = mm(ps[:, 2 * (u % 3), 0:UQ], ident, hsum[:, u % 2, h, :], h == 0, h == H // 4 - 1)
                ins.then_inc(s["sum"], 1)

            def weigh_values1(u):
                b, r = divmod(u, 2)
                if u == 0:
                    pe.wait_ge(s["stk"], 4 * G)
                    pe.wait_ge(s["vcopy"], 2)
                elif r == 0:
                    pe.wait_ge(s["ot"], b)
                pe.wait_ge(s["wtd"], u + 1)
                pe.wait_ge(s["wtp"], u + 1)
                for g in range(G):
                    for j in range(GH):
                        ins = mm(ps[SLOT * j:SLOT * (j + 1), 7, g * P + r * UQ:g * P + (r + 1) * UQ],
                                 vals[:, b // HB, b % HB, GH * g + j, :], hprobs[:, u % 3, GH * g + j, :])
                ins.then_inc(s["pv"], 1)

            def project_out(b):
                pe.wait_ge(s["ot"], b + 1)
                if b:
                    pe.wait_ge(s["res"], b)
                for g in range(G):
                    ins = mm(ps[:, 6, 0:D], heads1[:, g, :], wo1[:, g, :], g == 0, g == G - 1)
                ins.then_inc(s["wo"], 1)

            for half in range(HALVES):
                for b in range(HB):
                    at = (half * HB + b) * P
                    ins = mm(ps[:, 4 + half, b * P:(b + 1) * P], ctx_sb[:, at:at + P], w["wv1"])
                ins.then_inc(s["v"], 1)
            pe.wait_ge(ffn[0]["res"], 2)
            pe.wait_ge(ready["split"], 2)
            pe.wait_ge(ready["negid"], 1)
            turn(s, "norm", xn, HB, 2, "xt")
            for n in range(3 * G):
                project1(n)
                if n == 1:
                    turn(s, "norm", xn, HB, 3, "xt", HB)
            pe.wait_ge(s["vcopy"], 2)
            head_scores(0)
            head_scores(1)
            for n in (12, 13):
                project1(n)
            less_max(0)
            for n in (14, 15):
                project1(n)
            less_max(1)
            for u in range(UNITS):
                if u + 2 < UNITS:
                    head_scores(u + 2)
                head_sum(u)
                if u >= 1:
                    weigh_values1(u - 1)
                if u + 2 < UNITS:
                    less_max(u + 2)
                if u >= 3 and u % 2 == 1:
                    project_out((u - 3) // 2)
            weigh_values1(UNITS - 1)
            project_out(B - 1)
            s = ffn[1]
            pe.wait_ge(a1["res"], B)
            route(s, 1)

            def gates1(e, slot, n, first=False):
                h, c = divmod(n, 3)
                at, m = CH1[c]
                if n == 0:
                    pe.wait_ge(s["wlo"], e + 1)
                    pe.wait_ge(s["wlou"], e + 1)
                reads = () if first else ((s["glu"], e * 6 + n - 1), (s["act"], e * 6 + n - 1))
                gate_up(s, slot, at, F1 + at, m, h, n % 2, *reads)

            def down1(e, slot, n, final):
                h, c = divmod(n, 3)
                m, at, cols = CH1[c][1], (6 * slot + n) % 4, slice(c * D, (c + 1) * D)
                if n == 0:
                    pe.wait_ge(s["dlo"], e + 1)
                pe.wait_ge(s["alo"], e * 6 + n + 1)
                dst = ps[:, 6 + h, :]
                mm(dst, down_hi[0:m, slot, cols], act_hi[0:m, at, :], False, False)
                mm(dst, down_hi[0:m, slot, cols], act_lo[0:m, at, :], False, False)
                ins = mm(dst, down_lo[0:m, slot, cols], act_hi[0:m, at, :], False, final and c == 2)
                if final and c == 2:
                    ins.then_inc(s["down"], 1)

            def expert1(e, slot, kind=""):
                for n in range(6):
                    if n < 3:
                        gates1(e, slot, n + 3)
                    elif kind != "last":
                        gates1(e + 1, 1 - slot, n - 3)
                    down1(e, slot, n, kind == "last")
                    if n == 2 and kind == "unweighted":
                        turn_weights(s, 4)
                        pe.wait_ge(s["wtc"], 1)
                    if n == 2 and kind != "last":
                        spread_weights(s, e, 0)
                    if n == 5 and kind != "last":
                        spread_weights(s, e, 1)

            for n in range(2):
                gates1(0, 0, n, True)
            first_products(s, 1)
            gates1(0, 0, 2)
            expert1(0, 0, "unweighted")
            with pe.Fori(0, E1 // 2 - 1) as i:
                for slot in (1, 0):
                    expert1((i + 1 - slot) * 2 + slot, slot)
            expert1(E1 - 1, 1, "next to last")
            expert1(E1, 0, "last")
            ffn_end(s)


def _head_slots(wt):
    a = np.zeros((D, H, GH, HD), wt.dtype)
    a[:, :, :3, :] = wt.T.reshape(D, H, 1, HD)
    return a.reshape(D, G * P)


def kernel(**inputs):
    import concourse.bacc as bacc
    from concourse.bass_utils import run_bass_kernel_spmd

    a = {n: np.asarray(v) for n, v in inputs.items()}
    f32 = np.float32
    bf16 = mybir.dt.np(BF16)
    consts = np.zeros((P, C_END), f32)
    consts[:, C_ID:C_ID + P] = np.eye(P)
    consts[:, C_NEG:C_NEG + P] = -np.eye(P)
    lane = np.arange(P) % SLOT // HD
    consts[:, C_QSEL] = np.where(lane == 1, -1.0, 0.0)
    consts[:, C_KSEL] = np.where(lane == 2, -1.0, 0.0)
    consts[0, C_ONE:C_ONE + P] = 1.0
    gather = np.zeros((P, G, OUTW), f32)
    for h in range(H):
        g, j = divmod(h, GH)
        for d in range(HD):
            gather[SLOT * j + d, g, h * HD + d] = 1.0
        gather[SLOT * j + HD, g, D + h] = 1.0
    consts[:, C_GATHER:] = gather.reshape(P, G * OUTW)
    part_sel = np.zeros((P, E0, P), bf16)
    for part in range(PARTS):
        for e in range(E0):
            part_sel[E0 * part + e, e, :] = 1.0
    qk = np.stack([_head_slots(a[n]) for n in ("L0_xattn_Wq", "L0_xattn_Wk", "L1_xattn_Wq", "L1_xattn_Wk")], 1)
    small = np.zeros((P, W_END), f32)
    for n, v in (("wv0", a["L0_xattn_Wv"].T), ("wp0", a["L0_xattn_Wp"].T), ("wv1", a["L1_xattn_Wv"].T),
                 ("rw0", a["L0_ffn_router_weight"].T), ("gw1", a["L1_ffn_gate_w"])):
        small[:, W_AT[n]:W_AT[n] + W_WIDTH[n]] = v
    small[:, W_LN], small[:, W_LN + 1] = a["L0_xattn_ln_g"], a["L0_xattn_ln_b"]
    wo = np.zeros((GH, SLOT, G, D), f32)
    wo[:, :HD] = a["L1_xattn_Wo"].T.reshape(G, GH, HD, D).transpose(1, 2, 0, 3)
    small[:, W_WO:] = wo.reshape(P, G * D)
    rows = np.concatenate([a["L0_xattn_gate"].reshape(-1)] + [a["L0_xattn_bp"]] * HB +
                          [a["L0_ffn_router_bias"]] * B)[None, :]
    down_bias = np.zeros((P, D), f32)
    for part in range(PARTS):
        down_bias[E0 * part:E0 * (part + 1)] = a["L0_ffn_down_bias"]
    gu_bias = a["L0_ffn_gate_up_bias"].reshape(E0, 2, F0).transpose(2, 1, 0)
    experts0 = np.concatenate([a["L0_ffn_gate_up_proj"], a["L0_ffn_down_proj"]], 2)
    wgu = np.concatenate([a["L1_ffn_base_wgu"][None], a["L1_ffn_exp_wgu"]], 0)
    wd = np.zeros((E1 + 1, 3 * P, D), f32)
    wd[:, :F1] = np.concatenate([a["L1_ffn_base_wd"][None], a["L1_ffn_exp_wd"]], 0)
    experts1 = np.concatenate([wgu, wd.reshape(E1 + 1, 3, P, D).transpose(0, 2, 1, 3).reshape(E1 + 1, P, 3 * D)], 2)
    arrays = {
        "x": a["x"], "ctx_t": a["ctx_1024"].transpose(2, 0, 1).reshape(D, T), "qk_w": qk, "small_w": small,
        "consts": consts, "rows": rows, "down_bias": down_bias, "gu_bias": gu_bias, "part_sel": part_sel,
        "ident_bf": np.eye(P).astype(bf16), "experts0": experts0, "experts1": experts1,
    }
    arrays = {n + "_dram": np.ascontiguousarray(v) for n, v in arrays.items()}
    nc = bacc.Bacc("TRN2", target_bir_lowering=False, num_devices=1)
    args = [nc.dram_tensor(n, v.shape, mybir.dt.from_np(v.dtype), kind="ExternalInput").ap()
            for n, v in arrays.items()]
    out = nc.dram_tensor("out_dram", (B, P, D), F32, kind="ExternalOutput").ap()
    two_layers(nc, *args, out)
    r = run_bass_kernel_spmd(nc, [arrays], core_ids=[0])
    return r.results[0]["out_dram"]
```
